# Optimizing a Trainium2 kernel written in Bass

```python
import numpy as np
import jax
import jax.numpy as jnp

def _softmax(x, axis=-1):
    return jax.nn.softmax(x, axis=axis)

def _gelu(x):
    return jax.nn.gelu(x, approximate=True)

def _silu(x):
    return jax.nn.silu(x)

def _sigmoid(x):
    return jax.nn.sigmoid(x)

def _layernorm(x, axis=-1, eps=1e-05):
    m = jnp.mean(x, axis=axis, keepdims=True)
    v = jnp.var(x, axis=axis, keepdims=True)
    return (x - m) / jnp.sqrt(v + eps)

def _scatter_add(tgt, idx, src, axis=0):
    return tgt.at[idx].add(src)

def _segment_sum(src, seg, n):
    return jax.ops.segment_sum(src, seg, n)
kernel_name = 'mk_adaln_ffn_d4_seqx_r8_746b77'

def setup_inputs(seed: int=0):
    np.random.seed(seed)
    _w = jnp.asarray

    def _rec_inputs():
        import jax
        import jax.numpy as jnp
        _rk = jax.random.key(seed)
        x = -0.0003929 + 0.9999 * jax.random.normal(jax.random.fold_in(_rk, 1), (64, 32, 512), jnp.float32)
        _lenS = 32 - jax.random.randint(jax.random.fold_in(_rk, 7), (64,), 0, max(1, 32 // 4) + 1, jnp.int32)
        _lenS2 = 32 - jax.random.randint(jax.random.fold_in(_rk, 8), (64,), 0, max(1, 32 // 4) + 1, jnp.int32)
        itok_B_8_3872 = jax.random.randint(jax.random.fold_in(_rk, 11), (64,), 8, 3873, jnp.int32)
        itok_B_1_14 = jax.random.randint(jax.random.fold_in(_rk, 12), (64,), 1, 15, jnp.int32)
        itok_B_0_7 = jax.random.randint(jax.random.fold_in(_rk, 13), (64,), 0, 8, jnp.int32)
        itok_B_9_3973 = jax.random.randint(jax.random.fold_in(_rk, 14), (64,), 9, 3974, jnp.int32)
        return (x, itok_B_8_3872, itok_B_1_14, itok_B_0_7, itok_B_9_3973)
    x, itok_B_8_3872, itok_B_1_14, itok_B_0_7, itok_B_9_3973 = _rec_inputs()

    def _L0_cond_setup():
        import math
        import jax, jax.numpy as jnp
        import numpy as np
        H, N, B, L = (32, 64, 16, 512)
        DT_MIN, DT_MAX = (0.001, 0.1)

        def _get_kernel(log_dt, C, log_A_real, A_imag, length):
            Cc = C[..., 0] + 1j * C[..., 1]
            dt = jnp.exp(log_dt)
            A = -jnp.exp(log_A_real) + 1j * A_imag
            dtA = A * dt[:, None]
            P = dtA[:, :, None] * jnp.arange(length, dtype=jnp.float32)
            Cs = Cc * (jnp.exp(dtA) - 1.0) / A
            K = 2.0 * jnp.einsum('hn,hnl->hl', Cs, jnp.exp(P)).real
            return K
        key = jax.random.key(seed)
        ks = jax.random.split(key, 6)
        u = jax.random.normal(ks[0], (B, H, L), dtype=jnp.float32)
        length = jax.random.randint(ks[1], (B,), 0, L)
        log_dt = jax.random.uniform(ks[2], (H,), dtype=jnp.float32) * (math.log(DT_MAX) - math.log(DT_MIN)) + math.log(DT_MIN)
        C = jax.random.normal(ks[3], (H, N, 2), dtype=jnp.float32)
        log_A_real = jnp.log(0.5 * jnp.ones((H, N), dtype=jnp.float32))
        A_imag = math.pi * jnp.broadcast_to(jnp.arange(N, dtype=jnp.float32), (H, N))
        D = jax.random.normal(ks[4], (H,), dtype=jnp.float32)
        return {'u': u, 'length': length, 'log_dt': log_dt, 'C': C, 'log_A_real': log_A_real, 'A_imag': A_imag, 'D': D}
    _L0_cond_all = _L0_cond_setup()
    _L0_cond_in = {k: v for k, v in _L0_cond_all.items() if k in ('log_dt', 'C', 'log_A_real', 'A_imag', 'D')}
    del _L0_cond_all

    def _L0_ffn_setup():
        import jax, jax.numpy as jnp
        import numpy as np
        OUT_FEATURES = 512
        IN_FEATURES = 512
        FP8_MAX = 448.0
        key = jax.random.key(seed)
        kx, kw = jax.random.split(key)
        x = jax.random.normal(kx, (4, 512, IN_FEATURES), dtype=jnp.float32)
        w = jax.random.normal(kw, (OUT_FEATURES, IN_FEATURES), dtype=jnp.float32) * 0.02
        abs_max = jnp.max(jnp.abs(w))
        weight_scale = (abs_max / FP8_MAX).reshape(1)
        weight_fp8 = (w / weight_scale).astype(jnp.float8_e4m3fn)
        return {'x': x, 'weight_fp8': weight_fp8, 'weight_scale': weight_scale}
    _L0_ffn_all = _L0_ffn_setup()
    _L0_ffn_in = {k: v for k, v in _L0_ffn_all.items() if k in ('weight_fp8', 'weight_scale')}
    del _L0_ffn_all

    def _L1_cond_setup():
        import jax, jax.numpy as jnp
        import numpy as np
        B, S, D_IN = (8, 256, 512)
        A, D_OUT = (16, 512)
        key = jax.random.key(seed)
        k1, k2, k3 = jax.random.split(key, 3)
        x = jax.random.normal(k1, (B, S, D_IN), dtype=jnp.float32)
        weight = jax.random.normal(k2, (A, D_OUT, D_IN), dtype=jnp.float32) * 0.02
        adapter_ids = jax.random.randint(k3, (B,), 0, A, dtype=jnp.int64)
        return {'x': x, 'weight': weight, 'adapter_ids': adapter_ids}
    _L1_cond_all = _L1_cond_setup()
    _L1_cond_in = {k: v for k, v in _L1_cond_all.items() if k in ('weight',)}
    del _L1_cond_all

    def _L1_ffn_setup():
        import jax, jax.numpy as jnp
        import numpy as np
        NF4_CODE = jnp.array([-1.0, -0.6961928009986877, -0.5250730514526367, -0.39491748809814453, -0.28444138169288635, -0.18477343022823334, -0.09105003625154495, 0.0, 0.07958029955625534, 0.16093020141124725, 0.24611230194568634, 0.33791524171829224, 0.44070982933044434, 0.5626170039176941, 0.7229568362236023, 1.0], dtype=jnp.float32)
        BLOCKSIZE = 64

        def nf4_quant_dequant(w):
            shape = w.shape
            flat = w.reshape(-1, BLOCKSIZE)
            absmax = jnp.max(jnp.abs(flat), axis=1, keepdims=True)
            normalized = flat / jnp.where(absmax == 0, 1.0, absmax)
            bounds = (NF4_CODE[:-1] + NF4_CODE[1:]) * 0.5
            idx = jnp.searchsorted(bounds, normalized)
            return (NF4_CODE[idx] * absmax).reshape(shape)
        key = jax.random.key(seed)
        k1, k2, k3, kx = jax.random.split(key, 4)
        D, H = (512, 1376)
        scale = 0.02
        w1 = jax.random.normal(k1, (H, D), jnp.float32) * scale
        w2 = jax.random.normal(k2, (H, D), jnp.float32) * scale
        w3 = jax.random.normal(k3, (D, H), jnp.float32) * scale
        x = jax.random.normal(kx, (2, 256, D), jnp.float32)
        return {'x': x, 'w1': w1, 'w2': w2, 'w3': w3}
    _L1_ffn_all = _L1_ffn_setup()
    _L1_ffn_in = {k: v for k, v in _L1_ffn_all.items() if k in ('w1', 'w2', 'w3')}
    del _L1_ffn_all

    def _L2_cond_setup():
        import jax, jax.numpy as jnp
        import numpy as np
        TOP_K = 2
        LANG_BIAS = 5.0
        SCALING = 32.0 / 16.0
        LANGUAGE_PAD_ID = -1
        key = jax.random.key(seed)
        ks = jax.random.split(key, 6)
        B, T, D, O, E, R = (4, 256, 512, 512, 8, 16)
        x = jax.random.normal(ks[0], (B, T, D), dtype=jnp.float32)
        language_ids = jax.random.randint(ks[1], (B,), 0, E).astype(jnp.int64)
        W = jax.random.normal(ks[2], (O, D), dtype=jnp.float32) * (1.0 / np.sqrt(D))
        Wr = jax.random.normal(ks[3], (E, D), dtype=jnp.float32) * (1.0 / np.sqrt(D))
        A = jax.random.normal(ks[4], (E, R, D), dtype=jnp.float32) * (1.0 / np.sqrt(D))
        Bm = jax.random.normal(ks[5], (O, R), dtype=jnp.float32) * 0.0
        Bm = jnp.broadcast_to(Bm, (E, O, R)) + jax.random.normal(ks[5], (E, O, R), dtype=jnp.float32) * 0.02
        return {'x': x, 'language_ids': language_ids, 'W': W, 'Wr': Wr, 'A': A, 'B': Bm}
    _L2_cond_all = _L2_cond_setup()
    _L2_cond_in = {k: v for k, v in _L2_cond_all.items() if k in ('W', 'Wr', 'A', 'B')}
    del _L2_cond_all

    def _L2_ffn_setup():
        import jax, jax.numpy as jnp
        import numpy as np
        HID, BOT, RDIM, NSLOT, K, VB = (512, 64, 48, 128, 8, 32)
        TAU_LOW, TAU_HIGH, EARLY_EXIT = (0.5, 2.0, 0.05)

        def _uncertainty(h, Wu1, bu1, Wu2, bu2):
            var = jnp.var(h, axis=-1)
            log_var = jnp.log1p(var)
            norm_var = log_var / (jnp.mean(log_var) + 1e-06)
            learned = (jax.nn.gelu(h @ Wu1.T + bu1) @ Wu2.T + bu2)[..., 0]
            return jnp.clip(norm_var * 0.5 + jax.nn.sigmoid(learned) * 2.5, 0.0, 5.0)
        key = jax.random.key(seed)
        ks = jax.random.split(key, 12)
        B, S = (2, 256)
        return {'hidden_states': jax.random.normal(ks[0], (B, S, HID), dtype=jnp.float32), 'Wq': jax.random.normal(ks[1], (BOT, HID), dtype=jnp.float32) / np.sqrt(HID), 'Wr': jax.random.normal(ks[2], (RDIM, BOT), dtype=jnp.float32) / np.sqrt(BOT), 'aux_keys': jax.random.normal(ks[3], (NSLOT, BOT), dtype=jnp.float32) * 0.01, 'aux_values': jax.random.normal(ks[4], (NSLOT, HID), dtype=jnp.float32) * 0.02, 'Wvd': jax.random.normal(ks[5], (VB, HID), dtype=jnp.float32) * 0.1 / np.sqrt(HID), 'Wvu': jax.random.normal(ks[6], (HID, VB), dtype=jnp.float32) * 0.1 / np.sqrt(VB), 'Wu1': jax.random.normal(ks[7], (HID // 4, HID), dtype=jnp.float32) / np.sqrt(HID), 'bu1': jnp.zeros((HID // 4,), dtype=jnp.float32), 'Wu2': jax.random.normal(ks[8], (1, HID // 4), dtype=jnp.float32) * 0.01, 'bu2': jnp.zeros((1,), dtype=jnp.float32), 'gate_w1': jnp.float32(0.5), 'gate_bias': jnp.float32(-1.0), 'log_rel': jnp.zeros((NSLOT,), dtype=jnp.float32)}
    _L2_ffn_all = _L2_ffn_setup()
    _L2_ffn_in = {k: v for k, v in _L2_ffn_all.items() if k in ('Wq', 'Wr', 'aux_keys', 'aux_values', 'Wvd', 'Wvu', 'Wu1', 'bu1', 'Wu2', 'bu2', 'gate_w1', 'gate_bias', 'log_rel')}
    del _L2_ffn_all

    def _L3_cond_setup():
        import jax, jax.numpy as jnp
        import numpy as np
        from jax import lax
        B, E, T = (32, 64, 512)
        K = 5
        PAD = (K - 1) // 2
        key = jax.random.key(seed)
        k1, k2, k3 = jax.random.split(key, 3)
        x = jax.random.normal(k1, (B, E, T), dtype=jnp.float32)
        length = jax.random.randint(k2, (B,), 1, T + 1, dtype=jnp.int64)
        conv_w = jax.random.normal(k3, (1, 1, K), dtype=jnp.float32) * (1.0 / np.sqrt(K))
        return {'x': x, 'length': length, 'conv_w': conv_w}
    _L3_cond_all = _L3_cond_setup()
    _L3_cond_in = {k: v for k, v in _L3_cond_all.items() if k in ('conv_w',)}
    del _L3_cond_all

    def _L3_ffn_setup():
        import jax, jax.numpy as jnp
        import numpy as np
        NUM_EXPERTS = 8
        RANK = 32
        ALPHA = 16.0
        TOP_K = 2
        TEMPERATURE = 1.0
        GAMMA = 0.5
        SOFT_TOPK_TEMP = 0.5
        N_GRAM = 2
        EPS = 1e-06
        key = jax.random.key(seed)
        ks = jax.random.split(key, 6)
        d_in, d_out = (512, 512)
        Bsz, T = (4, 256)
        x = jax.random.normal(ks[0], (Bsz, T, d_in), dtype=jnp.float32)
        W = jax.random.normal(ks[1], (d_out, d_in), dtype=jnp.float32) / np.sqrt(d_in)
        b = jax.random.normal(ks[2], (d_out,), dtype=jnp.float32) * 0.01
        A = jax.random.normal(ks[3], (d_in, RANK), dtype=jnp.float32) / np.sqrt(d_in)
        Bmat = jax.random.normal(ks[4], (RANK, d_out), dtype=jnp.float32) * 0.01
        LiMEs = jax.random.normal(ks[5], (NUM_EXPERTS, RANK), dtype=jnp.float32) * 0.1
        return {'x': x, 'W': W, 'b': b, 'A': A, 'Bmat': Bmat, 'LiMEs': LiMEs}
    _L3_ffn_all = _L3_ffn_setup()
    _L3_ffn_in = {k: v for k, v in _L3_ffn_all.items() if k in ('W', 'b', 'A', 'Bmat', 'LiMEs')}
    del _L3_ffn_all
    return {'x': x, 'itok_B_8_3872': itok_B_8_3872, 'itok_B_1_14': itok_B_1_14, 'itok_B_0_7': itok_B_0_7, 'itok_B_9_3973': itok_B_9_3973, 'L0_cond_log_dt': _L0_cond_in['log_dt'], 'L0_cond_C': _L0_cond_in['C'], 'L0_cond_log_A_real': _L0_cond_in['log_A_real'], 'L0_cond_A_imag': _L0_cond_in['A_imag'], 'L0_cond_D': _L0_cond_in['D'], 'L0_ffn_weight_fp8': _L0_ffn_in['weight_fp8'], 'L0_ffn_weight_scale': _L0_ffn_in['weight_scale'], 'L1_cond_weight': _L1_cond_in['weight'], 'L1_ffn_w1': _L1_ffn_in['w1'], 'L1_ffn_w2': _L1_ffn_in['w2'], 'L1_ffn_w3': _L1_ffn_in['w3'], 'L2_cond_W': _L2_cond_in['W'], 'L2_cond_Wr': _L2_cond_in['Wr'], 'L2_cond_A': _L2_cond_in['A'], 'L2_cond_B': _L2_cond_in['B'], 'L2_ffn_Wq': _L2_ffn_in['Wq'], 'L2_ffn_Wr': _L2_ffn_in['Wr'], 'L2_ffn_aux_keys': _L2_ffn_in['aux_keys'], 'L2_ffn_aux_values': _L2_ffn_in['aux_values'], 'L2_ffn_Wvd': _L2_ffn_in['Wvd'], 'L2_ffn_Wvu': _L2_ffn_in['Wvu'], 'L2_ffn_Wu1': _L2_ffn_in['Wu1'], 'L2_ffn_bu1': _L2_ffn_in['bu1'], 'L2_ffn_Wu2': _L2_ffn_in['Wu2'], 'L2_ffn_bu2': _L2_ffn_in['bu2'], 'L2_ffn_gate_w1': _L2_ffn_in['gate_w1'], 'L2_ffn_gate_bias': _L2_ffn_in['gate_bias'], 'L2_ffn_log_rel': _L2_ffn_in['log_rel'], 'L3_cond_conv_w': _L3_cond_in['conv_w'], 'L3_ffn_W': _L3_ffn_in['W'], 'L3_ffn_b': _L3_ffn_in['b'], 'L3_ffn_A': _L3_ffn_in['A'], 'L3_ffn_Bmat': _L3_ffn_in['Bmat'], 'L3_ffn_LiMEs': _L3_ffn_in['LiMEs']}

def reference(x, itok_B_8_3872, itok_B_1_14, itok_B_0_7, itok_B_9_3973, L0_cond_log_dt, L0_cond_C, L0_cond_log_A_real, L0_cond_A_imag, L0_cond_D, L0_ffn_weight_fp8, L0_ffn_weight_scale, L1_cond_weight, L1_ffn_w1, L1_ffn_w2, L1_ffn_w3, L2_cond_W, L2_cond_Wr, L2_cond_A, L2_cond_B, L2_ffn_Wq, L2_ffn_Wr, L2_ffn_aux_keys, L2_ffn_aux_values, L2_ffn_Wvd, L2_ffn_Wvu, L2_ffn_Wu1, L2_ffn_bu1, L2_ffn_Wu2, L2_ffn_bu2, L2_ffn_gate_w1, L2_ffn_gate_bias, L2_ffn_log_rel, L3_cond_conv_w, L3_ffn_W, L3_ffn_b, L3_ffn_A, L3_ffn_Bmat, L3_ffn_LiMEs):
    import jax
    import jax.numpy as jnp

    def _L0_cond_ref(u, length, log_dt, C, log_A_real, A_imag, D):
        import math
        import jax, jax.numpy as jnp
        import numpy as np
        H, N, B, L = (32, 64, 16, 512)
        DT_MIN, DT_MAX = (0.001, 0.1)

        def _get_kernel(log_dt, C, log_A_real, A_imag, length):
            Cc = C[..., 0] + 1j * C[..., 1]
            dt = jnp.exp(log_dt)
            A = -jnp.exp(log_A_real) + 1j * A_imag
            dtA = A * dt[:, None]
            P = dtA[:, :, None] * jnp.arange(length, dtype=jnp.float32)
            Cs = Cc * (jnp.exp(dtA) - 1.0) / A
            K = 2.0 * jnp.einsum('hn,hnl->hl', Cs, jnp.exp(P)).real
            return K
        Bq, Hq, Lq = u.shape
        mask = (jnp.arange(Lq) < length[:, None]).astype(u.dtype)
        u_m = u * mask[:, None, :]
        kernel = _get_kernel(log_dt, C, log_A_real, A_imag, Lq)
        n = 2 * Lq
        k_f = jnp.fft.rfft(kernel, n=n)
        u_f = jnp.fft.rfft(u_m, n=n)
        y = jnp.fft.irfft(u_f * k_f, n=n)[..., :Lq]
        y = y + u_m * D[:, None]
        return y * mask[:, None, :]

    def _L0_ffn_ref(x, weight_fp8, weight_scale):
        import jax, jax.numpy as jnp
        import numpy as np
        OUT_FEATURES = 512
        IN_FEATURES = 512
        FP8_MAX = 448.0
        w = weight_fp8.astype(x.dtype) * weight_scale
        return jnp.einsum('bsd,od->bso', x, w)

    def _L1_cond_ref(x, weight, adapter_ids):
        import jax, jax.numpy as jnp
        import numpy as np
        B, S, D_IN = (8, 256, 512)
        A, D_OUT = (16, 512)
        w = weight[adapter_ids]
        return jnp.einsum('bij,bkj->bik', x, w)

    def _L1_ffn_ref(x, w1, w2, w3):
        import jax, jax.numpy as jnp
        import numpy as np
        NF4_CODE = jnp.array([-1.0, -0.6961928009986877, -0.5250730514526367, -0.39491748809814453, -0.28444138169288635, -0.18477343022823334, -0.09105003625154495, 0.0, 0.07958029955625534, 0.16093020141124725, 0.24611230194568634, 0.33791524171829224, 0.44070982933044434, 0.5626170039176941, 0.7229568362236023, 1.0], dtype=jnp.float32)
        BLOCKSIZE = 64

        def nf4_quant_dequant(w):
            shape = w.shape
            flat = w.reshape(-1, BLOCKSIZE)
            absmax = jnp.max(jnp.abs(flat), axis=1, keepdims=True)
            normalized = flat / jnp.where(absmax == 0, 1.0, absmax)
            bounds = (NF4_CODE[:-1] + NF4_CODE[1:]) * 0.5
            idx = jnp.searchsorted(bounds, normalized)
            return (NF4_CODE[idx] * absmax).reshape(shape)
        dq1 = nf4_quant_dequant(w1)
        dq2 = nf4_quant_dequant(w2)
        dq3 = nf4_quant_dequant(w3)
        gate = jnp.einsum('bsd,hd->bsh', x, dq1)
        up = jnp.einsum('bsd,hd->bsh', x, dq2)
        h = jax.nn.silu(gate) * up
        return jnp.einsum('bsh,dh->bsd', h, dq3)

    def _L2_cond_ref(x, language_ids, W, Wr, A, B):
        import jax, jax.numpy as jnp
        import numpy as np
        TOP_K = 2
        LANG_BIAS = 5.0
        SCALING = 32.0 / 16.0
        LANGUAGE_PAD_ID = -1
        base = jnp.einsum('btd,od->bto', x, W)
        E = Wr.shape[0]
        logits = jnp.einsum('btd,ed->bte', x.astype(jnp.float32), Wr.astype(jnp.float32))
        expert_targets = language_ids
        valid = expert_targets >= 0
        tgt = jnp.where(valid, expert_targets, 0)
        bias = jax.nn.one_hot(tgt, E, dtype=logits.dtype) * LANG_BIAS
        bias = jnp.where(valid[:, None], bias, 0.0)
        logits = logits + bias[:, None, :]
        topw, topi = jax.lax.top_k(logits, TOP_K)
        weights = jax.nn.softmax(topw, axis=-1)
        gates = jnp.sum(jax.nn.one_hot(topi, E, dtype=weights.dtype) * weights[..., None], axis=-2)
        gates = gates.astype(x.dtype)
        h = jnp.einsum('btd,erd->bter', x, A)
        lora_out = jnp.einsum('bter,bte,eor->bto', h, gates, B)
        return base + SCALING * lora_out

    def _L2_ffn_ref(hidden_states, Wq, Wr, aux_keys, aux_values, Wvd, Wvu, Wu1, bu1, Wu2, bu2, gate_w1, gate_bias, log_rel):
        import jax, jax.numpy as jnp
        import numpy as np
        HID, BOT, RDIM, NSLOT, K, VB = (512, 64, 48, 128, 8, 32)
        TAU_LOW, TAU_HIGH, EARLY_EXIT = (0.5, 2.0, 0.05)

        def _uncertainty(h, Wu1, bu1, Wu2, bu2):
            var = jnp.var(h, axis=-1)
            log_var = jnp.log1p(var)
            norm_var = log_var / (jnp.mean(log_var) + 1e-06)
            learned = (jax.nn.gelu(h @ Wu1.T + bu1) @ Wu2.T + bu2)[..., 0]
            return jnp.clip(norm_var * 0.5 + jax.nn.sigmoid(learned) * 2.5, 0.0, 5.0)
        query = hidden_states @ Wq.T
        rq = query @ Wr.T
        rk = aux_keys @ Wr.T
        router_scores = jnp.einsum('bsr,nr->bsn', rq, rk) / np.sqrt(RDIM) + log_rel
        top_scores, top_idx = jax.lax.top_k(router_scores, K)
        sel_keys = aux_keys[top_idx]
        attn = jnp.einsum('bsd,bskd->bsk', query, sel_keys) / np.sqrt(BOT) + log_rel[top_idx]
        w = jax.nn.softmax(attn, axis=-1)
        sel_vals = aux_values[top_idx]
        aux_out = jnp.einsum('bsk,bskh->bsh', w, sel_vals)
        aux_out = aux_out @ Wvd.T @ Wvu.T
        u = _uncertainty(hidden_states, Wu1, bu1, Wu2, bu2)
        u_norm = jnp.clip((u - TAU_LOW) / (TAU_HIGH - TAU_LOW), 0.0, 1.0)
        gate = jax.nn.sigmoid(gate_w1 * u_norm + gate_bias)
        gate = jnp.where(gate < EARLY_EXIT, 0.0, gate)
        return hidden_states + gate[..., None] * aux_out

    def _L3_cond_ref(x, length, conv_w):
        import jax, jax.numpy as jnp
        import numpy as np
        from jax import lax
        B, E, T = (32, 64, 512)
        K = 5
        PAD = (K - 1) // 2
        mask = (jnp.arange(T)[None, :] < length[:, None]).astype(x.dtype)
        denom = length.astype(x.dtype)[:, None]
        y = jnp.einsum('bet,bt->be', x, mask) / denom
        yc = lax.conv_general_dilated(y[:, None, :], conv_w, window_strides=(1,), padding=[(PAD, PAD)], dimension_numbers=('NCH', 'OIH', 'NCH'))[:, 0, :]
        gate = jax.nn.sigmoid(yc)
        return x * gate[:, :, None]

    def _L3_ffn_ref(x, W, b, A, Bmat, LiMEs):
        import jax, jax.numpy as jnp
        import numpy as np
        NUM_EXPERTS = 8
        RANK = 32
        ALPHA = 16.0
        TOP_K = 2
        TEMPERATURE = 1.0
        GAMMA = 0.5
        SOFT_TOPK_TEMP = 0.5
        N_GRAM = 2
        EPS = 1e-06
        Bsz, T, d_in = x.shape
        E = LiMEs.shape[0]
        scaling = ALPHA / RANK
        H = jnp.einsum('btd,od->bto', x, W) + b
        z = jnp.einsum('btd,dr->btr', x, A)
        anchors = jnp.arange(N_GRAM - 1, T, N_GRAM)
        H_slice = H[:, anchors, :E]
        delta_slice = jnp.einsum('bar,er->bae', z[:, anchors], LiMEs)
        H_scale = jnp.maximum(jnp.max(jnp.abs(H_slice)), EPS)
        d_scale = jnp.maximum(jnp.max(jnp.abs(delta_slice)), EPS)
        logits = ((1.0 - GAMMA) * (H_slice / H_scale) + GAMMA * (delta_slice / d_scale)) / TEMPERATURE
        probs = jax.nn.softmax(logits, axis=-1)
        topk_vals, _ = jax.lax.top_k(probs, TOP_K)
        thresh = topk_vals[..., -1:]
        mask = jax.nn.sigmoid((probs - thresh) / SOFT_TOPK_TEMP)
        weights = probs * mask
        weights = weights / (jnp.sum(weights, axis=-1, keepdims=True) + 1e-09)
        weights_full = jnp.repeat(weights, N_GRAM, axis=1)
        p_mix = jnp.einsum('bte,er->btr', weights_full, LiMEs)
        delta = jnp.einsum('btr,ro->bto', z * p_mix, Bmat) * scaling
        return H + delta
    x = x + _L0_ffn_ref(_L0_cond_ref(x, itok_B_8_3872, L0_cond_log_dt, L0_cond_C, L0_cond_log_A_real, L0_cond_A_imag, L0_cond_D), L0_ffn_weight_fp8, L0_ffn_weight_scale)
    x = x + _L1_ffn_ref(_L1_cond_ref(x, L1_cond_weight, itok_B_1_14), L1_ffn_w1, L1_ffn_w2, L1_ffn_w3)
    x = x + _L2_ffn_ref(_L2_cond_ref(x, itok_B_0_7, L2_cond_W, L2_cond_Wr, L2_cond_A, L2_cond_B), L2_ffn_Wq, L2_ffn_Wr, L2_ffn_aux_keys, L2_ffn_aux_values, L2_ffn_Wvd, L2_ffn_Wvu, L2_ffn_Wu1, L2_ffn_bu1, L2_ffn_Wu2, L2_ffn_bu2, L2_ffn_gate_w1, L2_ffn_gate_bias, L2_ffn_log_rel)
    x = x + _L3_ffn_ref(_L3_cond_ref(x, itok_B_9_3973, L3_cond_conv_w), L3_ffn_W, L3_ffn_b, L3_ffn_A, L3_ffn_Bmat, L3_ffn_LiMEs)
    return x

_drawn_inputs = setup_inputs


def setup_inputs(seed=0):
    import zlib

    import numpy as np

    out = dict(_drawn_inputs(seed))
    spreads = {'L0_cond_log_A_real': (-0.6931471824645996, 0.2),
     'L2_ffn_bu1': (0.0, 2.0),
     'L2_ffn_log_rel': (0.0, 2.0)}
    factors = {'L1_cond_weight': 2.734,
     'L1_ffn_w1': 2.736,
     'L1_ffn_w2': 2.713,
     'L1_ffn_w3': 2.72,
     'L2_ffn_Wq': 64.0,
     'L2_ffn_Wr': 64.0,
     'L2_ffn_aux_keys': 64.0,
     'L2_ffn_aux_values': 64.0,
     'L2_ffn_Wvd': 64.0,
     'L2_ffn_Wvu': 64.0,
     'L2_ffn_Wu1': 64.0,
     'L2_ffn_Wu2': 64.0,
     'L3_cond_conv_w': 3.376,
     'L3_ffn_b': 48.671,
     'L3_ffn_A': 8.0,
     'L3_ffn_Bmat': 8.0,
     'L3_ffn_LiMEs': 8.0}
    for name, (base, spread) in spreads.items():
        noise = np.random.default_rng([zlib.crc32(name.encode()), seed]).standard_normal(out[name].shape)
        drawn = base * np.exp(spread * noise) if base else spread * noise
        out[name] = jnp.asarray(drawn.astype(out[name].dtype))
    for name, factor in factors.items():
        out[name] = (out[name] * factor).astype(out[name].dtype)
    return out
```

```python
import numpy as np

import concourse.bass as bass
from concourse import mybir
from contextlib import ExitStack

f32 = mybir.dt.float32
f16 = mybir.dt.float16
i32 = mybir.dt.int32
u8 = mybir.dt.uint8
u16 = mybir.dt.uint16
ALU = mybir.AluOpType
ACT = mybir.ActivationFunctionType
AX = mybir.AxisListType

P = 128
NB, S, D = 64, 32, 512
TOK = NB * S
DC = D // P
TB = 4
TW = TOK // TB
NT = TW // P
TT = TOK // P
MODES = 64
LA, LC = 16, 32
PAD = P
KROW = PAD + D
GH = 2
HG = S // GH
ADAPT = 16
HID = 1376
HCH = [min(P, HID - P * c) for c in range((HID + P - 1) // P)]
NH = len(HCH)
E, R = 8, 16
BOT, RDIM, NSLOT, VB = 64, 48, 128, 32
RANK = 32
BLK = 64
HALF = 1408
SENT = 6
CMULT = 67
ANCH = TOK // 2

NF4 = np.array([-1.0, -0.6961928009986877, -0.5250730514526367, -0.39491748809814453, -0.28444138169288635,
                -0.18477343022823334, -0.09105003625154495, 0.0, 0.07958029955625534, 0.16093020141124725,
                0.24611230194568634, 0.33791524171829224, 0.44070982933044434, 0.5626170039176941,
                0.7229568362236023, 1.0], np.float32)
BOUNDS = ((NF4[:-1] + NF4[1:]) * np.float32(0.5)).astype(np.float32)
STEPS = (NF4[1:] - NF4[:-1]).astype(np.float32)

ROUND = float(1.5 * 2 ** 23)
LOG2E = float(np.log2(np.e))
LN2_HI = float(np.float32(0.693359375))
LN2_LO = float(np.log(2.0) - 0.693359375)
TWO_PI = 2 * np.pi
PI_A = float(np.float32(6.28125))
PI_B = float(np.float32(np.round((TWO_PI - 6.28125) * 2 ** 21) / 2 ** 21))
PI_C = float(np.float32(TWO_PI - 6.28125 - PI_B))

C_ID = 0
C_MUL = C_ID + P
C_PH = C_MUL + CMULT
C_IOTA = C_PH + CMULT
C_L = C_IOTA + P
C_LREV = C_L + DC
C_PCOL = C_LREV + DC
C_COLS = C_PCOL + 1


def constants():
    c = np.zeros((P, C_COLS), np.float32)
    c[:, C_ID:C_ID + P] = np.eye(P)
    mul = np.concatenate([np.arange(LC), LC * np.arange(LA), LC * np.arange(LA), [1, 1, 0.5]])
    c[:, C_MUL:C_MUL + CMULT] = mul
    ph = np.zeros((P, CMULT))
    ph[:MODES, :LC] = np.pi / 2
    ph[:, LC:LC + LA] = np.pi / 2
    ph[:, LC + 2 * LA] = np.pi / 2
    c[:, C_PH:C_PH + CMULT] = ph
    c[:, C_IOTA:C_IOTA + P] = np.arange(P)
    p = np.arange(P)[:, None]
    c[:, C_L:C_L + DC] = np.arange(DC) * P + p
    c[:, C_LREV:C_LREV + DC] = np.arange(DC) * P + (P - 1 - p)
    c[:, C_PCOL] = np.arange(P)
    diag = (np.arange(NB)[:, None] == (np.arange(TOK) // S)[None, :]).astype(np.float32)
    return c, diag


def build(nc, A, out):
    ctx = ExitStack()
    with ctx:
        def sb(name, shape, dt=f32):
            return ctx.enter_context(nc.sbuf_tensor(name, shape, dt))

        ps = ctx.enter_context(nc.psum_tensor("ps", [P, 8, 512], f32))
        kpad = nc.dram_tensor("kpad", [S, KROW], f32, kind="Internal")

        X = sb("X", [P, DC, TOK])
        Y = sb("Y", [P, DC, TOK])
        U = sb("U", [P, DC, S, NB])
        T = sb("T", [P, 2, GH, D])
        W1T = sb("W1T", [P, DC, HID])
        W2T = sb("W2T", [P, DC, HID])
        W3T = sb("W3T", [P, NH, D])
        w1f = W1T[:, :, :].rearrange("p a b -> p (a b)")
        w2f = W2T[:, :, :].rearrange("p a b -> p (a b)")
        w3f = W3T[:, :, :].rearrange("p a b -> p (a b)")
        uf = U[:, :, :, :].rearrange("p a b c -> p (a b c)")
        tf = T[:, :, :, :].rearrange("p a b c -> p (a b c)")
        cst = sb("cst", [P, C_COLS])
        ident = cst[:, C_ID:C_ID + P]
        ones = sb("ones", [P, P])

        raw = sb("raw", [P, 2, HALF])
        acc = sb("acc", [P, HALF])
        step = sb("step", [P, HALF])
        amax = sb("amax", [P, HALF // BLK])
        rmax = sb("rmax", [P, HALF // BLK])

        ang = w1f[:, 0:S * CMULT].rearrange("p (h m) -> p h m", h=S)
        dec = w1f[:, S * CMULT:2 * S * CMULT].rearrange("p (h m) -> p h m", h=S)
        turn = w2f[:, 0:S * CMULT].rearrange("p (h m) -> p h m", h=S)
        n0 = S * CMULT
        pc = w2f[:, n0:n0 + S * LA].rearrange("p (h m) -> p h m", h=S)
        pq = w2f[:, n0 + S * LA:n0 + 2 * S * LA].rearrange("p (h m) -> p h m", h=S)
        n0 += 2 * S * LA
        ksb = w2f[0:LA, n0:n0 + S * LC].rearrange("p (h m) -> p h m", h=S)
        zpad = w2f[0:S, n0 + S * LC:n0 + S * LC + PAD]
        w0u = w3f[:, 0:512].bitcast(u8).rearrange("p (c o) -> p c o", c=DC)
        w0 = w3f[:, 512:512 + DC * D].rearrange("p (c o) -> p c o", c=DC)
        sm = w3f[:, 2560:2560 + 40 * S].rearrange("p (k h) -> p k h", h=S)
        h16a = step[:, 0:1024].bitcast(u16).rearrange("p (c o) -> p c o", c=DC)
        h16b = acc[:, 0:1024].bitcast(u16).rearrange("p (c o) -> p c o", c=DC)
        wsc = sb("wsc", [P, 1])
        leni = sb("leni", [P, 2, NB], i32)
        lenf = sb("lenf", [P, 2, NB])
        mnat = sb("mnat", [P, DC, NB])
        mrev = sb("mrev", [P, DC, NB])

        idc_i = sb("idc_i", [NB, 1], i32)
        idr_i = sb("idr_i", [NB, NB], i32)
        idc = sb("idc", [NB, 1])
        keyc = sb("keyc", [NB, 1])
        keyr = sb("keyr", [NB, NB])
        below = sb("below", [NB, NB])
        rank = sb("rank", [NB, 1])
        oneh = sb("oneh", [NB, NB + ADAPT + 1])
        order = sb("order", [1, NB + ADAPT + 1], i32)
        WA = uf[:, 0:3 * DC * D].rearrange("p (s c o) -> p s c o", s=3, c=DC)

        l2w = tf[:, 0:2048].rearrange("p (c o) -> p c o", c=DC)
        tail = uf[:, 3 * DC * D:4 * DC * D]
        l2a = tail[:, 0:512].rearrange("p (c o) -> p c o", c=DC)
        l2u = tail[:, 512:1024].rearrange("p (c o) -> p c o", c=DC)
        l2b = tail[:, 1024:1536]
        l2q = tail[:, 1536:1792].rearrange("p (c o) -> p c o", c=DC)
        l3a = tail[:, 1792:1920].rearrange("p (c o) -> p c o", c=DC)
        wvd = tail[:, 1920:2048].rearrange("p (c o) -> p c o", c=DC)
        avT = acc[:, 0:512].rearrange("p (c o) -> p c o", c=DC)
        wvu = step[0:VB, 0:512]
        v1 = step[0:VB, 512:512 + NSLOT]
        l2r = sb("l2r", [P, DC, E])
        rq48 = sb("rq48", [BOT, RDIM])
        akT = sb("akT", [BOT + 1, NSLOT])
        rk = sb("rk", [RDIM + 1, NSLOT])
        bu1 = sb("bu1", [P, 1])
        wu2 = sb("wu2", [P, 1])
        gsc = sb("gsc", [P, 3])
        lan_i = sb("lan_i", [P, TT], i32)
        lan = sb("lan", [P, TT])
        lbias = sb("lbias", [P, TT, E])
        b3 = sb("b3", [P, DC])
        b8 = sb("b8", [P, E])
        lim = sb("lim", [E, RANK])
        limT = sb("limT", [RANK, E])
        w16 = sb("w16", [P, DC, 2 * E])
        cw = sb("cw", [NB, 5])
        lc_i = sb("lc_i", [NB, 1], i32)
        ilen = sb("ilen", [NB, 2])

        rawf = raw[:, :, :].rearrange("p a b -> p (a b)")
        sg = [rawf[:, 0:512], rawf[:, 512:1024]]
        hh = [rawf[:, 1024:1536], rawf[:, 1536:2048]]

        free = [0]

        def cut(n, parts=P):
            a = free[0]
            free[0] += n
            assert free[0] <= 3 * DC * D
            return uf[0:parts, a:a + n]

        def tiles(n, k, parts=P):
            return cut(n * k, parts).rearrange("p (t k) -> p t k", t=n)

        ha, hgx, qT, rqT, gu = cut(512), cut(512), cut(512, BOT + 1), cut(512, RDIM + 1), cut(512)
        vals, vrep = tiles(NT, 16), tiles(NT, 16)
        top, repl, ge, gs = (tiles(NT, 8) for _ in range(4))
        gt = tiles(NT, E * R)
        z4 = tiles(3, NT)
        sc, am = tiles(NT, NSLOT), tiles(NT, NSLOT)
        top8 = tiles(NT, 8)
        nmx = cut(NT)
        bst = tiles(NT, 8)
        v2, bm, aT = cut(D), cut(D, RANK), cut(D, RANK)
        PR = w1f[:, 0:TT * NSLOT].rearrange("p (t k) -> p t k", t=TT)
        oT = [w1f[:, 512 * i:512 * (i + 1)] for i in range(4)]
        PT = w1f[:, 2048:4096]
        zt = w2f[0:RANK, 0:TOK]
        diag = w2f[0:NB, 2048:4096]
        sl, lg3, pr3, mk3, tp3, tm3 = (w2f[:, 4096 + 128 * i:4096 + 128 * i + k * 8].rearrange("p (t k) -> p t k", t=8)
                                       for i, k in enumerate([16, 8, 8, 8, 8, 8]))
        ss3 = w2f[:, 4864:4864 + 8 * 6].rearrange("p (a t) -> p a t", t=8)
        mx4, gm4, gm2 = w2f[:, 4928:4932], w2f[:, 4932:4936], w2f[:, 4936:4940]
        yd, gex = w3f[0:NB, 0:512], w3f[0:NB, 512:1024]
        ysm = w3f[0:NB, 1024:1024 + 4 * 40].rearrange("p (a b) -> p a b", a=4)
        zp = w3f[0:RANK, 1536:2048]
        wT = w3f[0:E, 2048:3072]
        l3w = w3f[:, 3584:5632].rearrange("p (c o) -> p c o", c=DC)
        var = sb("var", [P, TT, 2])
        lv = sb("lv", [P, TT])
        lvs = sb("lvs", [P, 2])
        lrn = sb("lrn", [P, TT])
        den = sb("den", [P, TT])
        gq = sb("gq", [P, 6, TT])

        s = {}
        for n in """l_cst l_s4 l_w0 l_u l_x l_len l_ids l_kpad l_strip0 l_strip1 l_raw0 l_raw1 l_wa0 l_wa1 l_wa2 l_late l_prep l_l3w
                l_sml l_diag l_out0 l_out1 l_out2 l_out3
                v_step a_step d_ones d_mask g_mask d_ang a_ang d_pp p_k d_k d_w0 p_conv d_conv p_ffn0 d_x1
                d_oneh p_ord d_ord p_ad ad_out d_dq p_qt a_qt p_gu a_silu d_h p_down d_x2
                p_prep a_v1 p_v2 prep_done p_lg d_gl a_ge d_gate p_ha a_ha p_gx d_hg p_c2 a_c2 g_xc
                p_tr d_st p_q a_q p_rq a_rq p_gup a_gu p_lr a_lr p_sc d_am a_pr a_lv p_lv a_sg d_un a_gt
                d_pn p_pt a_pt p_aux d_x3 p_y d_ys a_yg d_gex p_gb d_c3 p_z a_z p_sl d_mx g_mx d_lg3 a_e3 d_th a_mk
                d_w3 p_wt a_wt p_pm d_zp p_o d_o""".split():
            s[n] = ctx.enter_context(nc.semaphore(n))
        block = ctx.enter_context(nc.Block())

        UNITS = [(1, c) for c in range(NH)] + [(3, q) for q in range(4)]
        NU = len(UNITS)
        EARLY = 4
        QB = np.cumsum([0] + [2 if k == 1 else (NH + 3) // 4 for k, _ in UNITS]).tolist()

        def unit_shape(u):
            return (HCH[UNITS[u][1]], 2 * D) if UNITS[u][0] == 1 else (P, HALF)

        def tok(tb):
            return slice(tb * TW, (tb + 1) * TW)

        def tile(tb, t):
            return slice(tb * TW + t * P, tb * TW + (t + 1) * P)

        @block.sync
        def _(sp):
            sp.dma_start(cst[:, :], A["const"]).then_inc(s["l_cst"], 16)
            for half in range(2):
                r = slice(half * MODES, (half + 1) * MODES)
                sp.dma_start(sm[r, 1, :], A["log_A_real"]).then_inc(s["l_s4"], 16)
                sp.dma_start(sm[r, 2, :], A["A_imag"]).then_inc(s["l_s4"], 16)
                sp.dma_start(sm[r, 3, :], A["C_re"]).then_inc(s["l_s4"], 16)
                sp.dma_start(sm[r, 4, :], A["C_im"]).then_inc(s["l_s4"], 16)
            sp.dma_start(sm[:, 0, :], A["log_dt"].partition_broadcast(P)).then_inc(s["l_s4"], 16)
            sp.dma_start(sm[0:1, 5, :], A["Dskip"].partition_broadcast(1)).then_inc(s["l_s4"], 16)
            sp.dma_start(leni[:, 0, :], A["len0"].partition_broadcast(P)).then_inc(s["l_len"], 16)
            sp.dma_start(leni[:, 1, :], A["len3"].partition_broadcast(P)).then_inc(s["l_len"], 16)
            sp.dma_start(w0u, A["w0"].bitcast(u8).rearrange("(c p) o -> p c o", p=P)).then_inc(s["l_w0"], 16)
            sp.dma_start(wsc[:, :], A["w0scale"].partition_broadcast(P)).then_inc(s["l_w0"], 16)
            sp.dma_start(U[:, :, :, :].rearrange("p a b c -> p a (b c)"),
                         A["xconv"].rearrange("a p n -> p a n")).then_inc(s["l_u"], 16)
            sp.dma_start(X[:, :, :], A["xT"].rearrange("(c p) n -> p c n", p=P)).then_inc(s["l_x"], 16)
            sp.wait_ge(s["d_k"], 1)
            kv = kpad.ap()
            sp.dma_start(kv[:, 0:PAD], zpad).then_inc(s["l_kpad"], 16)
            sp.dma_start(kv[:, PAD:KROW].rearrange("h (a c) -> a h c", a=LA), ksb).then_inc(s["l_kpad"], 16)
            sp.wait_ge(s["l_kpad"], 32)
            for g in range(HG):
                if g >= 2:
                    sp.wait_ge(s["p_conv"], g - 1)
                    sp.wait_ge(s[f"l_strip{g % 2}"], 16 * (g // 2))
                sp.dma_start(T[:, g % 2, :, :], bass.AP(kpad, g * GH * KROW + 1, [[1, P], [KROW, GH], [1, D]])
                             ).then_inc(s[f"l_strip{g % 2}"], 16)
            sp.wait_ge(s["p_conv"], HG)
            sp.wait_ge(s["d_ord"], 1)
            for a in range(ADAPT):
                if a >= 3:
                    last = sp.value_load(order[0:1, NB + a - 2:NB + a - 1], min_val=0, max_val=NB)
                    sp.wait_ge(s["ad_out"], last + 2)
                    sp.wait_ge(s[f"l_wa{a % 3}"], 16 * (a // 3))
                sp.dma_start(WA[:, a % 3, :, :], A["wa"][a].rearrange("(c p) o -> p c o", p=P)
                             ).then_inc(s[f"l_wa{a % 3}"], 16)
                if a == 2:
                    for dst, name in ((l2a, "l2a"), (l2u, "wu1"), (l2q, "wq"), (l3a, "l3a"), (wvd, "wvd"),
                                      (l2w, "l2w")):
                        sp.dma_start(dst, A[name].rearrange("(c p) o -> p c o", p=P)).then_inc(s["l_late"], 16)
                    sp.dma_start(l2b, A["l2b"]).then_inc(s["l_late"], 16)
            sp.wait_ge(s["ad_out"], NB + 2)
            sp.wait_ge(s["p_qt"], QB[NU])
            sp.dma_start(avT, A["avT"].rearrange("(c p) o -> p c o", p=P)).then_inc(s["l_prep"], 16)
            sp.dma_start(wvu, A["wvu"]).then_inc(s["l_prep"], 16)
            sp.dma_start(bm, A["bmat"]).then_inc(s["l_prep"], 16)
            sp.dma_start(aT, A["l3aT"]).then_inc(s["l_prep"], 16)
            sp.wait_ge(s["p_down"], TB * NH)
            sp.dma_start(l3w, A["l3w"].rearrange("(c p) o -> p c o", p=P)).then_inc(s["l_l3w"], 16)
            sp.dma_start(diag, A["diag"]).then_inc(s["l_diag"], 16)
            for n in range(TB * DC):
                tb, oc = n // DC, n % DC
                sp.wait_ge(s["d_o"], n + 1)
                sp.dma_start(out[oc * P:(oc + 1) * P, tok(tb)], oT[n % 4]).then_inc(s[f"l_out{n % 4}"], 16)
            for i in range(4):
                sp.wait_ge(s[f"l_out{i}"], 16 * TB * DC // 4)

        @block.gpsimd
        def _(pool):
            pool.dma_start(idc_i[:, :], A["ids"].rearrange("(n a) -> n a", a=1)).then_inc(s["l_ids"], 16)
            pool.dma_start(idr_i[:, :], A["ids"].partition_broadcast(NB)).then_inc(s["l_ids"], 16)
            pool.wait_ge(s["l_u"], 16)
            pool.wait_ge(s["d_mask"], 1)
            for c in range(DC):
                nc.gpsimd.tensor_tensor(U[:, c, :, :], U[:, c, :, :],
                                        mrev[:, c:c + 1, :].to_broadcast([P, S, NB]), ALU.mult).then_inc(s["g_mask"], 1)
            for u, (kind, c) in enumerate(UNITS):
                if u >= 2:
                    pool.wait_ge(s["d_dq"], u - 1)
                slot = raw[:, u % 2, :]
                got = s[f"l_raw{u % 2}"]
                if kind == 1:
                    h = HCH[c]
                    pool.dma_start(slot[0:h, 0:D], A["w1"][c * P:c * P + h, :]).then_inc(got, 16)
                    pool.dma_start(slot[0:h, D:2 * D], A["w2"][c * P:c * P + h, :]).then_inc(got, 16)
                else:
                    g, q = c // 2, c % 2
                    o = q * (2 * HID - HALF)
                    pool.dma_start(slot[:, 0:HALF // 2], A["w3"][g * P:(g + 1) * P, o:o + HALF // 2]).then_inc(got, 16)
                    pool.dma_start(slot[:, HALF // 2:HALF],
                                   A["w3"][g * P:(g + 1) * P, o + HALF // 2:o + HALF]).then_inc(got, 16)
                if u == 1:
                    for dst, src in ((l2r[:, :, :], A["wr"].rearrange("(c p) o -> p c o", p=P)), (rq48[:, :], A["wrq"]),
                                     (akT[0:BOT, :], A["akT"]),
                                     (akT[BOT:BOT + 1, :], A["log_rel"].partition_broadcast(1)),
                                     (rk[RDIM:RDIM + 1, :], A["log_rel"].partition_broadcast(1)),
                                     (bu1[:, :], A["bu1"].rearrange("(n a) -> n a", a=1)), (wu2[:, :], A["wu2"]),
                                     (gsc[:, 0:1], A["gate_w1"].partition_broadcast(P)),
                                     (gsc[:, 1:2], A["gate_bias"].partition_broadcast(P)),
                                     (gsc[:, 2:3], A["bu2"].partition_broadcast(P)),
                                     (b3[:, :], A["b3"]), (b8[:, :], A["b3row"][0:E].partition_broadcast(P)),
                                     (lim[:, :], A["lim"]), (limT[:, :], A["limT"]),
                                     (cw[:, :], A["conv_w"].partition_broadcast(NB)),
                                     (lc_i[:, :], A["len3"].rearrange("(n a) -> n a", a=1))):
                        pool.dma_start(dst, src).then_inc(s["l_sml"], 16)
                    for q in range(4):
                        src = A["lang"][q]
                        pool.dma_start(lan_i[q * S:(q + 1) * S, :], src.partition_broadcast(S)).then_inc(s["l_sml"], 16)
            for tb in range(TB):
                pool.wait_ge(s["a_c2"], tb + 1)
                pool.wait_ge(s["p_c2"], tb + 1)
                nc.gpsimd.tensor_tensor(X[:, :, tok(tb)], X[:, :, tok(tb)], Y[:, :, tok(tb)], ALU.add
                                        ).then_inc(s["g_xc"], 1)
            pool.wait_ge(s["d_mx"], 1)
            nc.gpsimd.partition_all_reduce(gm4, mx4, P, bass.bass_isa.ReduceOp.absmax).then_inc(s["g_mx"], 1)

        NSML = 16 * 20

        @block.scalar
        def _(act):
            act.wait_ge(s["d_ang"], 1)
            nc.scalar.activation(dec, dec, ACT.Exp).then_inc(s["a_ang"], 1)
            act.wait_ge(s["d_ang"], 2)
            nc.scalar.activation(ang, ang, ACT.Sin).then_inc(s["a_ang"], 1)

            def evac_quant(u):
                kind, c = UNITS[u]
                n = QB[u]
                if kind == 1:
                    h = HCH[c]
                    for dst in (W1T, W2T):
                        act.wait_ge(s["p_qt"], n + 1)
                        nc.scalar.activation(dst[:, :, c * P:c * P + h],
                                             ps[:, 6 + n % 2, :].rearrange("p (c h) -> p c h", c=DC)[:, :, 0:h],
                                             ACT.Copy).then_inc(s["a_qt"], 1)
                        n += 1
                    return
                g, q = c // 2, c % 2
                rows = slice(g * 2 * P + q, (g + 1) * 2 * P, 2)
                for c0 in range(0, NH, 4):
                    k = min(4, NH - c0)
                    whole = sum(HCH[c0 + i] == P for i in range(k))
                    act.wait_ge(s["p_qt"], n + 1)
                    src = ps[:, 6 + n % 2, :].rearrange("p (c r) -> p c r", c=4)
                    if whole < k:
                        r = HCH[c0 + k - 1]
                        nc.scalar.activation(W3T[0:r, c0 + k - 1, rows], src[0:r, k - 1, :], ACT.Copy)
                    nc.scalar.activation(W3T[:, c0:c0 + whole, rows], src[:, 0:whole, :], ACT.Copy
                                         ).then_inc(s["a_qt"], 1)
                    n += 1

            for u in range(EARLY):
                evac_quant(u)
            act.wait_ge(s["d_ord"], 1)
            act.sem_inc(s["ad_out"], 2)
            for a in range(ADAPT):
                lo = act.value_load(order[0:1, NB + a:NB + a + 1], min_val=0, max_val=NB)
                hi = act.value_load(order[0:1, NB + a + 1:NB + a + 2], min_val=0, max_val=NB)
                with act.If(lo < hi), act.Fori(lo, hi) as t:
                    b = act.value_load(order[0:1, bass.ds(t, 1)], min_val=0, max_val=NB - 1)
                    act.wait_ge(s["p_ad"], t + 1)
                    act.activation(Y[:, :, bass.ds(b * S, S)],
                                   ps[:, bass.ds(t % 2, 1), 0:DC * S].rearrange("p a (c n) -> p (a c) n", c=DC),
                                   ACT.Copy).then_inc(s["ad_out"], 1)
                if EARLY + a < NU:
                    evac_quant(EARLY + a)
            for n in range(TB * NH):
                h = HCH[n % NH]
                act.wait_ge(s["p_gu"], n + 1)
                if n >= 2:
                    act.wait_ge(s["d_h"], n - 1)
                nc.scalar.activation(sg[n % 2][0:h, :], ps[0:h, n % 2, :], ACT.Silu).then_inc(s["a_silu"], 1)
            act.wait_ge(s["p_prep"], 1)
            nc.scalar.activation(v1, ps[0:VB, 1, 0:NSLOT], ACT.Copy).then_inc(s["a_v1"], 1)
            nc.scalar.activation(rk[0:RDIM, :], ps[0:RDIM, 0, 0:NSLOT], ACT.Copy,
                                 scale=float(RDIM ** -0.5)).then_inc(s["prep_done"], 1)
            nc.scalar.activation(w16[:, :, E:2 * E], ps[:, 2, 0:DC * E].rearrange("p (c e) -> p c e", c=DC),
                                 ACT.Copy).then_inc(s["prep_done"], 1)
            act.wait_ge(s["p_v2"], 1)
            nc.scalar.activation(v2, ps[:, 3, :], ACT.Copy).then_inc(s["prep_done"], 1)
            for tb in range(TB):
                act.wait_ge(s["p_ha"], tb + 1)
                if tb:
                    act.wait_ge(s["d_hg"], tb)
                nc.scalar.activation(ha, ps[:, 0, :], ACT.Copy).then_inc(s["a_ha"], 1)
                act.wait_ge(s["d_gl"], tb + 1)
                nc.scalar.activation(ge, ge, ACT.Exp).then_inc(s["a_ge"], 1)
                act.wait_ge(s["p_c2"], tb + 1)
                nc.scalar.activation(Y[:, :, tok(tb)], ps[:, 4:8, :], ACT.Copy).then_inc(s["a_c2"], 1)
                act.wait_ge(s["p_q"], tb + 1)
                if tb:
                    act.wait_ge(s["p_sc"], tb)
                nc.scalar.activation(qT[0:BOT, :], ps[0:BOT, 0, :], ACT.Copy).then_inc(s["a_q"], 1)
                act.wait_ge(s["p_rq"], tb + 1)
                nc.scalar.activation(rqT[0:RDIM, :], ps[0:RDIM, 1, :], ACT.Copy).then_inc(s["a_rq"], 1)
                act.wait_ge(s["p_gup"], tb + 1)
                nc.scalar.activation(gu, ps[:, 4, :], ACT.Gelu_apprx_tanh, bias=bu1[:, 0:1]).then_inc(s["a_gu"], 1)
                act.wait_ge(s["p_lr"], tb + 1)
                nc.scalar.activation(lrn[:, tb * NT:(tb + 1) * NT], ps[:, 5, 0:NT], ACT.Copy).then_inc(s["a_lr"], 1)
                act.wait_ge(s["d_am"], tb + 1)
                for t in range(NT):
                    k = tb * NT + t
                    nc.scalar.activation(PR[:, k, :], am[:, t, :], ACT.Exp, bias=nmx[:, t:t + 1],
                                         accum_out=den[:, k:k + 1]).then_inc(s["a_pr"], 1)
            act.wait_ge(s["d_st"], TT + 1)
            nc.scalar.activation(lv[:, :], var[:, :, 1], ACT.Ln, bias=1.0, accum_out=lvs[:, 0:1]).then_inc(s["a_lv"], 1)
            act.wait_ge(s["a_lr"], TB)
            nc.scalar.activation(gq[:, 0, :], lrn[:, :], ACT.Sigmoid, bias=gsc[:, 2:3]).then_inc(s["a_sg"], 1)
            act.wait_ge(s["d_un"], 1)
            nc.scalar.activation(gq[:, 2, :], gq[:, 1, :], ACT.Sigmoid, scale=gsc[:, 0:1], bias=gsc[:, 1:2]
                                 ).then_inc(s["a_gt"], 1)
            for tb in range(TB):
                act.wait_ge(s["p_pt"], tb + 1)
                nc.scalar.activation(PT[:, tok(tb)], ps[:, tb % 2, :], ACT.Copy).then_inc(s["a_pt"], 1)
            for tb in range(TB):
                act.wait_ge(s["d_ys"], tb + 1)
                nc.scalar.activation(ysm[:, 2, 0:S], ysm[:, 1, 0:S], ACT.Sigmoid).then_inc(s["a_yg"], 1)
                act.wait_ge(s["p_z"], tb + 1)
                nc.scalar.activation(zt[:, tok(tb)], ps[0:RANK, 0, :], ACT.Copy).then_inc(s["a_z"], 1)
            act.wait_ge(s["d_lg3"], 1)
            nc.scalar.activation(pr3, lg3, ACT.Exp).then_inc(s["a_e3"], 1)
            act.wait_ge(s["d_th"], 1)
            nc.scalar.activation(mk3, mk3, ACT.Sigmoid, scale=2.0).then_inc(s["a_mk"], 1)
            for k in range(2):
                act.wait_ge(s["p_wt"], k + 1)
                nc.scalar.activation(wT[:, k * 512:(k + 1) * 512], ps[0:E, 2 + k, :], ACT.Copy).then_inc(s["a_wt"], 1)

        @block.tensor
        def _(pe):
            def mm(o, l, r, start, stop, **kw):
                return nc.tensor.matmul(o, l, r, start=start, stop=stop, **kw)

            pe.wait_ge(s["l_cst"], 16)
            pe.wait_ge(s["d_ones"], 1)
            pe.wait_ge(s["d_oneh"], 1)
            mm(ps[0:1, 5, 0:NB], cst[0:NB, C_PCOL:C_PCOL + 1], oneh[:, 0:NB], True, True)
            mm(ps[0:1, 5, NB:NB + ADAPT + 1], ones[0:NB, 0:1], oneh[:, NB:], True, True).then_inc(s["p_ord"], 1)
            pe.wait_ge(s["d_pp"], 1)
            for h in range(S):
                last = mm(ps[0:LA, 6 + h // 16, (h % 16) * LC:(h % 16 + 1) * LC], pc[:, h, :], turn[:, h, 0:LC],
                          True, True)
            last.then_inc(s["p_k"], 1)

            def turn_unit(u):
                kind, c = UNITS[u]
                pe.wait_ge(s["d_dq"], u + 1)
                n = QB[u]
                groups = []
                if kind == 1:
                    h = HCH[c]
                    for m in range(2):
                        groups.append([(ps[:, 6 + (n + m) % 2, k * P:k * P + h],
                                        acc[0:h, m * D + k * P:m * D + (k + 1) * P], h) for k in range(DC)])
                else:
                    o = (c % 2) * (HALF - HID)
                    for m, c0 in enumerate(range(0, NH, 4)):
                        groups.append([(ps[0:HCH[i], 6 + (n + m) % 2, (i - c0) * P:(i - c0 + 1) * P],
                                        acc[:, o + i * P:o + i * P + HCH[i]], P) for i in range(c0, min(c0 + 4, NH))])
                for m, group in enumerate(groups):
                    if n + m >= 2:
                        pe.wait_ge(s["a_qt"], n + m - 1)
                    else:
                        pe.wait_ge(s["d_k"], 1)
                    for dst, src, h in group:
                        last = nc.tensor.transpose(dst, src, ident[0:h, 0:h])
                    last.then_inc(s["p_qt"], 1)

            for c in range(1, DC + 1):
                pe.wait_ge(s["g_mask"], c)
            for g in range(HG):
                pe.wait_ge(s[f"l_strip{g % 2}"], 16 * (g // 2 + 1))
                if g >= 4:
                    pe.wait_ge(s["d_conv"], g - 3)
                for k in range(GH):
                    for lb in range(DC):
                        for jb in range(lb + 1):
                            o = lb * GH * NB + k * NB
                            last = mm(ps[:, g % 4, o:o + NB], T[:, g % 2, k, (lb - jb) * P:(lb - jb + 1) * P],
                                      U[:, jb, g * GH + k, :], jb == 0, jb == lb)
                last.then_inc(s["p_conv"], 1)
                if g % 4 == 3:
                    turn_unit(g // 4)
            pe.wait_ge(s["d_conv"], HG)
            pe.wait_ge(s["d_w0"], 1)
            pe.wait_ge(s["d_ord"], 1)
            for n in range(TB * DC):
                tb, oc = n // DC, n % DC
                if n >= 2:
                    pe.wait_ge(s["d_x1"], n - 1)
                for c in range(DC):
                    last = mm(ps[:, 4 + n % 2, :], w0[:, c, oc * P:(oc + 1) * P], Y[:, c, tok(tb)], c == 0, c == DC - 1)
                last.then_inc(s["p_ffn0"], 1)
            pe.wait_ge(s["d_x1"], TB * DC)
            for a in range(ADAPT):
                pe.wait_ge(s[f"l_wa{a % 3}"], 16 * (a // 3 + 1))
                lo = pe.value_load(order[0:1, NB + a:NB + a + 1], min_val=0, max_val=NB)
                hi = pe.value_load(order[0:1, NB + a + 1:NB + a + 2], min_val=0, max_val=NB)
                with pe.If(lo < hi), pe.Fori(lo, hi) as t:
                    b = pe.value_load(order[0:1, bass.ds(t, 1)], min_val=0, max_val=NB - 1)
                    pe.wait_ge(s["ad_out"], t + 1)
                    for oc in range(DC):
                        for c in range(DC):
                            last = pe.matmul(ps[:, bass.ds(t % 2, 1), oc * S:(oc + 1) * S].rearrange("p a n -> p (a n)"),
                                             WA[:, a % 3, c, oc * P:(oc + 1) * P], X[:, c, bass.ds(b * S, S)],
                                             start=(c == 0), stop=(c == DC - 1))
                    last.then_inc(s["p_ad"], 1)
                if EARLY + a < NU:
                    turn_unit(EARLY + a)
            pe.wait_ge(s["ad_out"], NB + 2)
            pe.wait_ge(s["a_qt"], QB[NU])

            def up(n):
                tb, c, h = n // NH, n % NH, HCH[n % NH]
                if n >= 2:
                    pe.wait_ge(s["d_h"], n - 1)
                for w, bk in ((W1T, n % 2), (W2T, 2 + n % 2)):
                    for k in range(DC):
                        last = mm(ps[0:h, bk, :], w[:, k, c * P:c * P + h], Y[:, k, tok(tb)], k == 0, k == DC - 1)
                last.then_inc(s["p_gu"], 1)

            def down(n):
                tb, c, h = n // NH, n % NH, HCH[n % NH]
                pe.wait_ge(s["d_h"], n + 1)
                if c == 0 and tb:
                    pe.wait_ge(s["d_x2"], tb)
                for oc in range(DC):
                    last = mm(ps[:, 4 + oc, :], W3T[0:h, c, oc * P:(oc + 1) * P], hh[n % 2][0:h, :], c == 0, c == NH - 1)
                last.then_inc(s["p_down"], 1)

            up(0)
            for n in range(TB * NH):
                if n + 1 < TB * NH:
                    up(n + 1)
                down(n)
            pe.wait_ge(s["l_sml"], NSML)
            pe.wait_ge(s["l_prep"], 64)
            pe.wait_ge(s["l_late"], 16 * 7)
            pe.wait_ge(s["a_silu"], TB * NH)
            pe.wait_ge(s["d_h"], TB * NH)
            mm(ps[0:RDIM, 0, 0:NSLOT], rq48[:, :], akT[0:BOT, :], True, True)
            for c in range(DC):
                mm(ps[0:VB, 1, 0:NSLOT], wvd[:, c, :], avT[:, c, :], c == 0, c == DC - 1)
            for c in range(DC):
                last = mm(ps[:, 2, c * E:(c + 1) * E], aT[:, c * P:(c + 1) * P], limT[:, :], True, True)
            last.then_inc(s["p_prep"], 1)
            pe.wait_ge(s["a_v1"], 1)
            mm(ps[:, 3, :], v1, wvu, True, True).then_inc(s["p_v2"], 1)
            pe.wait_ge(s["prep_done"], 4)
            for tb in range(TB):
                pe.wait_ge(s["d_x2"], tb + 1)
                if tb:
                    pe.wait_ge(s["a_pr"], NT * tb)
                    pe.wait_ge(s["a_rq"], tb)
                for t in range(NT):
                    for c in range(DC):
                        last = mm(ps[:, 1, t * E:(t + 1) * E], X[:, c, tile(tb, t)], l2r[:, c, :], c == 0, c == DC - 1)
                last.then_inc(s["p_lg"], 1)
                for c in range(DC):
                    last = mm(ps[:, 0, :], l2a[:, c, :], X[:, c, tok(tb)], c == 0, c == DC - 1)
                last.then_inc(s["p_ha"], 1)
                if tb:
                    pe.wait_ge(s["a_lr"], tb)
                for oc in range(DC):
                    for c in range(DC):
                        mm(ps[:, 4 + oc, :], l2w[:, c, oc * P:(oc + 1) * P], X[:, c, tok(tb)], c == 0, False)
                pe.wait_ge(s["d_gate"], tb + 1)
                if tb:
                    pe.wait_ge(s["d_st"], NT * tb)
                for t in range(NT):
                    last = nc.tensor.transpose(ps[:, 2, t * P:(t + 1) * P],
                                               gt[:, t, :], ident)
                last.then_inc(s["p_gx"], 1)
                pe.wait_ge(s["d_hg"], tb + 1)
                for oc in range(DC):
                    last = mm(ps[:, 4 + oc, :], l2b[:, oc * P:(oc + 1) * P], hgx, False, True)
                last.then_inc(s["p_c2"], 1)
                pe.wait_ge(s["a_c2"], tb + 1)
                for t in range(NT):
                    if tb or t >= 2:
                        pe.wait_ge(s["d_st"], NT * tb + t - 1)
                    for c in range(DC):
                        last = nc.tensor.transpose(ps[:, 3 - t % 2, c * P:(c + 1) * P], Y[:, c, tile(tb, t)], ident)
                    last.then_inc(s["p_tr"], 1)
                for c in range(DC):
                    last = mm(ps[0:BOT, 0, :], l2q[:, c, :], Y[:, c, tok(tb)], c == 0, c == DC - 1)
                last.then_inc(s["p_q"], 1)
                for c in range(DC):
                    last = mm(ps[:, 4, :], l2u[:, c, :], Y[:, c, tok(tb)], c == 0, c == DC - 1)
                last.then_inc(s["p_gup"], 1)
                pe.wait_ge(s["a_q"], tb + 1)
                mm(ps[0:RDIM, 1, :], rq48[:, :], qT[0:BOT, :], True, True).then_inc(s["p_rq"], 1)
                pe.wait_ge(s["a_gu"], tb + 1)
                for t in range(NT):
                    last = mm(ps[:, 5, t:t + 1], gu[:, t * P:(t + 1) * P], wu2[:, :], True, True)
                last.then_inc(s["p_lr"], 1)
                pe.wait_ge(s["a_rq"], tb + 1)
                for t in range(NT):
                    mm(ps[:, 6, t * NSLOT:(t + 1) * NSLOT], rqT[:, t * P:(t + 1) * P], rk[:, :], True, True)
                    last = mm(ps[:, 7, t * NSLOT:(t + 1) * NSLOT], qT[:, t * P:(t + 1) * P], akT[:, :], True, True)
                last.then_inc(s["p_sc"], 1)
            pe.wait_ge(s["a_lv"], 1)
            mm(ps[:, 0, 0:1], ones[:, :], lvs[:, 0:1], True, True).then_inc(s["p_lv"], 1)
            pe.wait_ge(s["d_pn"], 1)
            for tb in range(TB):
                if tb >= 2:
                    pe.wait_ge(s["a_pt"], tb - 1)
                for t in range(NT):
                    last = nc.tensor.transpose(ps[:, tb % 2, t * P:(t + 1) * P], PR[:, tb * NT + t, :], ident)
                last.then_inc(s["p_pt"], 1)
                pe.wait_ge(s["a_pt"], tb + 1)
                if tb:
                    pe.wait_ge(s["d_x3"], tb)
                for oc in range(DC):
                    last = mm(ps[:, 4 + oc, :], v2[:, oc * P:(oc + 1) * P], PT[:, tok(tb)], True, True)
                last.then_inc(s["p_aux"], 1)
            pe.wait_ge(s["l_l3w"], 16)
            for tb in range(TB):
                pe.wait_ge(s["d_x3"], tb + 1)
                for c in range(DC):
                    last = mm(ps[0:NB, 2, :], mnat[:, c, :], X[:, c, tok(tb)], c == 0, c == DC - 1)
                last.then_inc(s["p_y"], 1)
                pe.wait_ge(s["d_gex"], tb + 1)
                mm(ps[:, 3, :], ones[0:NB, :], gex, True, True).then_inc(s["p_gb"], 1)
                pe.wait_ge(s["d_c3"], tb + 1)
                if tb:
                    pe.wait_ge(s["a_z"], tb)
                for c in range(DC):
                    last = mm(ps[0:RANK, 0, :], l3a[:, c, :], Y[:, c, tok(tb)], c == 0, c == DC - 1)
                last.then_inc(s["p_z"], 1)
                for k in range(2):
                    for c in range(DC):
                        a0 = tb * TW + k * 2 * P + 1
                        last = mm(ps[:, 1, k * 2 * E:(k + 1) * 2 * E], Y[:, c, a0:a0 + 2 * P - 1:2], w16[:, c, :],
                                  c == 0, c == DC - 1)
                last.then_inc(s["p_sl"], 1)
            pe.wait_ge(s["d_w3"], 1)
            for k in range(2):
                for t in range(4):
                    last = nc.tensor.transpose(ps[0:E, 2 + k, t * P:(t + 1) * P], tm3[:, 4 * k + t, :], ident)
                last.then_inc(s["p_wt"], 1)
            pe.wait_ge(s["a_wt"], 2)
            pe.wait_ge(s["a_z"], TB)
            for tb in range(TB):
                mm(ps[0:RANK, tb % 2, :], lim[:, :],
                   wT[:, tb * 256:(tb + 1) * 256].unsqueeze(2).to_broadcast([E, 256, 2]), True, True
                   ).then_inc(s["p_pm"], 1)
                for oc in range(DC):
                    if tb:
                        pe.wait_ge(s["d_o"], (tb - 1) * DC + oc + 1)
                    for c in range(DC):
                        mm(ps[:, 4 + oc, :], l3w[:, c, oc * P:(oc + 1) * P], Y[:, c, tok(tb)], c == 0, False)
                    if oc == 0:
                        pe.wait_ge(s["d_zp"], tb + 1)
                    mm(ps[:, 4 + oc, :], bm[:, oc * P:(oc + 1) * P], zp, False, True).then_inc(s["p_o"], 1)

        @block.vector
        def _(dve):
            V = nc.vector
            count = [0]

            def link(ins):
                count[0] += 1
                ins.then_inc(s["v_step"], 1)
                dve.wait_ge(s["v_step"], count[0])

            def tt(o, a, b, op):
                link(V.tensor_tensor(o, a, b, op))

            def ts(o, a, x, y, op0, op1):
                link(V.tensor_scalar(o, a, x, y, op0, op1))

            def stt(o, a, x, b, op0, op1):
                link(V.scalar_tensor_tensor(out=o, in0=a, scalar=x, in1=b, op0=op0, op1=op1))

            V.memset(ones[:, :], 1.0).then_inc(s["d_ones"], 1)
            dve.wait_ge(s["d_ones"], 1)
            dve.wait_ge(s["l_cst"], 16)
            dve.wait_ge(s["l_len"], 32)
            link(V.tensor_copy(lenf[:, :, :], leni[:, :, :]))
            for c in range(DC):
                link(V.tensor_scalar(mnat[:, c, :], lenf[:, 0, :], cst[:, C_L + c:C_L + c + 1], None, ALU.is_gt))
            for c in range(DC):
                last = V.tensor_scalar(mrev[:, c, :], lenf[:, 0, :], cst[:, C_LREV + c:C_LREV + c + 1], None, ALU.is_gt)
            last.then_inc(s["d_mask"], 1)
            dve.wait_ge(s["l_ids"], 32)
            link(V.tensor_copy(idc[:, :], idc_i[:, :]))
            link(V.tensor_copy(keyr[:, :], idr_i[:, :]))
            ts(idc[:, :], idc[:, :], 0.0, float(ADAPT - 1), ALU.max, ALU.min)
            ts(keyr[:, :], keyr[:, :], 0.0, float(ADAPT - 1), ALU.max, ALU.min)
            stt(keyc[:, :], idc[:, :], float(NB), cst[0:NB, C_PCOL:C_PCOL + 1], ALU.mult, ALU.add)
            stt(keyr[:, :], keyr[:, :], float(NB), cst[0:NB, C_IOTA:C_IOTA + NB], ALU.mult, ALU.add)
            link(V.tensor_scalar(below[:, :], keyr[:, :], keyc[:, 0:1], None, ALU.is_lt))
            link(V.reduce_sum(rank[:, :], below[:, :], AX.X))
            link(V.tensor_scalar(oneh[:, 0:NB], cst[0:NB, C_IOTA:C_IOTA + NB], rank[:, 0:1], None, ALU.is_equal))
            V.tensor_scalar(oneh[:, NB:], cst[0:NB, C_IOTA:C_IOTA + ADAPT + 1], idc[:, 0:1], None, ALU.is_gt
                            ).then_inc(s["d_oneh"], 1)

            dve.wait_ge(s["l_s4"], 160)
            sl_ = [sm[:, i, :] for i in range(40)]
            ldt, lar, aim, cre, cim = sl_[0:5]

            def expm1(x, y, one, w):
                k, r, p, sc_ = w
                ts(k, x, LOG2E, ROUND, ALU.mult, ALU.add)
                ts(k, k, ROUND, -126.0, ALU.subtract, ALU.max)
                stt(r, k, -LN2_HI, x, ALU.mult, ALU.add)
                stt(r, k, -LN2_LO, r, ALU.mult, ALU.add)
                ts(p, r, 1.0 / 40320, None, ALU.mult, ALU.bypass)
                for c in (1.0 / 5040, 1.0 / 720, 1.0 / 120, 1.0 / 24, 1.0 / 6, 0.5, 1.0):
                    stt(p, p, c, r, ALU.add, ALU.mult)
                ts(sc_.bitcast(i32), k, 127.0, float(2 ** 23), ALU.add, ALU.mult)
                tt(p, p, sc_, ALU.mult)
                if one:
                    ts(sc_, sc_, -1.0, None, ALU.add, ALU.bypass)
                tt(y, p, sc_, ALU.add)

            two = sm[:, 0:2, :]
            expm1(two, sm[:, 6:8, :], False, [sm[:, 8 + 2 * i:10 + 2 * i, :] for i in range(4)])
            dt_, are = sl_[6], sl_[7]
            ts(are, are, -1.0, None, ALU.mult, ALU.bypass)
            a_, b_ = sl_[16], sl_[17]
            tt(a_, are, dt_, ALU.mult)
            tt(b_, aim, dt_, ALU.mult)
            mul = cst[:, C_MUL:C_MUL + CMULT].unsqueeze(1).to_broadcast([P, S, CMULT])
            ph = cst[:, C_PH:C_PH + CMULT].unsqueeze(1).to_broadcast([P, S, CMULT])
            V.tensor_tensor(dec, a_.unsqueeze(2).to_broadcast([P, S, CMULT]), mul, ALU.mult).then_inc(s["d_ang"], 1)
            tt(ang, b_.unsqueeze(2).to_broadcast([P, S, CMULT]), mul, ALU.mult)
            link(V.tensor_tensor(turn, ang, ph, ALU.add))
            ts(turn, turn, float(1 / TWO_PI), ROUND, ALU.mult, ALU.add)
            ts(turn, turn, ROUND, None, ALU.subtract, ALU.bypass)
            for c in (PI_A, PI_B, PI_C):
                stt(ang, turn, -c, ang, ALU.mult, ALU.add)
            tt(ang, ang, ph, ALU.add)
            V.tensor_scalar(ang, ang, float(np.float32(-3.1415925)), float(np.float32(3.1415925)), ALU.max, ALU.min
                            ).then_inc(s["d_ang"], 1)
            expm1(a_, sl_[18], True, [sl_[19], sl_[20], sl_[21], sl_[22]])
            em1 = sl_[18]
            dve.wait_ge(s["l_w0"], 32)
            link(V.tensor_copy(h16a, w0u))
            link(V.tensor_scalar(h16b, h16a, 0x7F, 7, ALU.bitwise_and, ALU.logical_shift_left))
            link(V.tensor_scalar(h16a, h16a, 0x80, 8, ALU.bitwise_and, ALU.logical_shift_left))
            link(V.tensor_tensor(h16a, h16a, h16b, ALU.bitwise_or))
            V.tensor_scalar(w0, h16a.bitcast(f16), 256.0, wsc[:, 0:1], ALU.mult, ALU.mult).then_inc(s["d_w0"], 1)
            dve.wait_ge(s["a_ang"], 2)
            o0 = LC + 2 * LA
            cb, sb_, hb = ang[:, :, o0], ang[:, :, o0 + 1], ang[:, :, o0 + 2]
            t1, t2, zr, zi, dn, rr, ri, yr, yi, cr, ci = sl_[19:30]
            tt(t1, em1, cb, ALU.mult)
            stt(t2, hb, -2.0, hb, ALU.mult, ALU.mult)
            tt(zr, t1, t2, ALU.add)
            stt(zi, em1, 1.0, sb_, ALU.add, ALU.mult)
            tt(t1, are, are, ALU.mult)
            tt(t2, aim, aim, ALU.mult)
            tt(dn, t1, t2, ALU.add)
            link(V.reciprocal(dn, dn))
            tt(rr, are, dn, ALU.mult)
            stt(ri, aim, -1.0, dn, ALU.mult, ALU.mult)

            def cmul(xr, xi, ar, ai, br, bi):
                tt(t1, ar, br, ALU.mult)
                tt(t2, ai, bi, ALU.mult)
                tt(xr, t1, t2, ALU.subtract)
                tt(t1, ar, bi, ALU.mult)
                tt(t2, ai, br, ALU.mult)
                tt(xi, t1, t2, ALU.add)

            cmul(yr, yi, cre, cim, zr, zi)
            cmul(cr, ci, yr, yi, rr, ri)
            al, be = sl_[30], sl_[31]
            lo, hi = slice(0, MODES), slice(MODES, P)
            ts(al[lo], cr[lo], 2.0, None, ALU.mult, ALU.bypass)
            ts(al[hi], ci[hi], -2.0, None, ALU.mult, ALU.bypass)
            ts(be[lo], ci[lo], -2.0, None, ALU.mult, ALU.bypass)
            ts(be[hi], cr[hi], -2.0, None, ALU.mult, ALU.bypass)
            tt(turn, ang, dec, ALU.mult)
            tt(pc, turn[:, :, LC:LC + LA], al.unsqueeze(2).to_broadcast([P, S, LA]), ALU.mult)
            tt(pq, turn[:, :, LC + LA:LC + 2 * LA], be.unsqueeze(2).to_broadcast([P, S, LA]), ALU.mult)
            V.tensor_tensor(pc, pc, pq, ALU.add).then_inc(s["d_pp"], 1)
            link(V.memset(zpad, 0.0))
            dve.wait_ge(s["p_ord"], 1)
            V.tensor_copy(order[:, :], ps[0:1, 5, 0:NB + ADAPT + 1]).then_inc(s["d_ord"], 1)
            dve.wait_ge(s["p_k"], 1)
            link(V.tensor_copy(ksb, ps[0:LA, 6:8, :].rearrange("p a (h c) -> p (a h) c", c=LC)))
            V.tensor_tensor(ksb[0:1, :, 0], ksb[0:1, :, 0], sm[0:1, 5, :], ALU.add).then_inc(s["d_k"], 1)

            def start_unit(u):
                h, w = unit_shape(u)
                nb = w // BLK
                dve.wait_ge(s[f"l_raw{u % 2}"], 32 * (u // 2 + 1))
                r = raw[0:h, u % 2, 0:w].rearrange("p (n k) -> p n k", k=BLK)
                link(V.tensor_reduce(amax[0:h, 0:nb], r, AX.X, ALU.max, apply_absolute_value=True))
                link(V.tensor_scalar(rmax[0:h, 0:nb], amax[0:h, 0:nb], 0.0, None, ALU.is_equal))
                tt(rmax[0:h, 0:nb], rmax[0:h, 0:nb], amax[0:h, 0:nb], ALU.add)
                link(V.reciprocal(rmax[0:h, 0:nb], rmax[0:h, 0:nb]))
                tt(r, r, rmax[0:h, 0:nb].unsqueeze(2).to_broadcast([h, nb, BLK]), ALU.mult)
                if u:
                    dve.wait_ge(s["p_qt"], QB[u])

            def levels(u, k0, k1):
                h, w = unit_shape(u)
                r, ac, st = raw[0:h, u % 2, 0:w], acc[0:h, 0:w], step[0:h, 0:w]
                for k in range(k0, k1):
                    if k == 0:
                        ts(ac, r, float(BOUNDS[0]), float(STEPS[0]), ALU.is_gt, ALU.mult)
                        ts(ac, ac, float(NF4[0]), None, ALU.add, ALU.bypass)
                        continue
                    ts(st, r, float(BOUNDS[k]), float(STEPS[k]), ALU.is_gt, ALU.mult)
                    tt(ac, ac, st, ALU.add)

            def end_unit(u):
                h, w = unit_shape(u)
                nb = w // BLK
                ac = acc[0:h, 0:w].rearrange("p (n k) -> p n k", k=BLK)
                V.tensor_tensor(ac, ac, amax[0:h, 0:nb].unsqueeze(2).to_broadcast([h, nb, BLK]), ALU.mult
                                ).then_inc(s["d_dq"], 1)
                dve.wait_ge(s["d_dq"], u + 1)

            def conv_out(g):
                dve.wait_ge(s["p_conv"], g + 1)
                for k in range(GH):
                    last = V.tensor_tensor(
                        Y[:, :, :].rearrange("p c (b s) -> p c b s", s=S)[:, :, :, g * GH + k],
                        ps[:, g % 4, :].rearrange("p (c k b) -> p c k b", c=DC, k=GH)[:, :, k, :],
                        mnat[:, :, :], ALU.mult)
                last.then_inc(s["d_conv"], 1)

            parts = [(0, 3), (3, 7), (7, 11), (11, 15)]
            for g in range(HG):
                u, q = g // 4, g % 4
                if q == 0:
                    start_unit(u)
                levels(u, *parts[q])
                if q == 3:
                    end_unit(u)
                conv_out(g)
            for n in range(TB * DC):
                tb, oc = n // DC, n % DC
                if n == 0:
                    dve.wait_ge(s["l_x"], 16)
                dve.wait_ge(s["p_ffn0"], n + 1)
                V.tensor_tensor(X[:, oc, tok(tb)], X[:, oc, tok(tb)], ps[:, 4 + n % 2, :], ALU.add
                                ).then_inc(s["d_x1"], 1)
            dve.wait_ge(s["d_conv"], HG)
            for c in range(DC):
                link(V.tensor_scalar(mnat[:, c, :], lenf[:, 1, :], cst[:, C_L + c:C_L + c + 1], None, ALU.is_gt))
            for u in range(EARLY, NU):
                start_unit(u)
                levels(u, 0, 15)
                end_unit(u)
            dve.wait_ge(s["l_sml"], NSML)
            link(V.tensor_copy(lan[:, :], lan_i[:, :]))
            tt(lbias[:, :, :], cst[:, C_IOTA:C_IOTA + E].unsqueeze(1).to_broadcast([P, TT, E]),
               lan[:, :].unsqueeze(2).to_broadcast([P, TT, E]), ALU.is_equal)
            ts(lbias[:, :, :], lbias[:, :, :], 5.0, None, ALU.mult, ALU.bypass)
            link(V.tensor_copy(ilen[:, 0:1], lc_i[:, :]))
            link(V.reciprocal(ilen[:, 1:2], ilen[:, 0:1]))
            for n in range(TB * NH):
                h = HCH[n % NH]
                dve.wait_ge(s["a_silu"], n + 1)
                if n >= 2:
                    dve.wait_ge(s["p_down"], n - 1)
                V.tensor_tensor(hh[n % 2][0:h, :], sg[n % 2][0:h, :], ps[0:h, 2 + n % 2, :], ALU.mult
                                ).then_inc(s["d_h"], 1)
                if n % NH == NH - 1:
                    tb = n // NH
                    dve.wait_ge(s["p_down"], n + 1)
                    V.tensor_tensor(X[:, :, tok(tb)], X[:, :, tok(tb)], ps[:, 4:8, :], ALU.add).then_inc(s["d_x2"], 1)
            dve.wait_ge(s["ad_out"], NB + 2)
            for i in range(SENT):
                link(V.memset(repl[:, :, 2 + i:3 + i], -1e30 * (i + 1)))
                link(V.memset(vals[:, :, E + i:E + i + 1], -1e30 * (i + 1)))
            link(V.memset(rqT[:, :], 1.0))
            link(V.memset(qT[BOT:BOT + 1, :], 1.0))
            dve.wait_ge(s["l_l3w"], 16)
            link(V.tensor_copy(w16[:, :, 0:E], l3w[:, :, 0:E]))
            dve.wait_ge(s["p_prep"], 1)
            V.tensor_scalar(akT[0:BOT, :], akT[0:BOT, :], float(BOT ** -0.5), None, ALU.mult).then_inc(s["prep_done"], 1)
            for tb in range(TB):
                dve.wait_ge(s["p_lg"], tb + 1)
                tt(vals[:, :, 0:E], ps[:, 1, 0:NT * E].rearrange("p (t e) -> p t e", e=E),
                   lbias[:, tb * NT:(tb + 1) * NT, :], ALU.add)
                for t in range(NT):
                    link(V.max(top[:, t, :], vals[:, t, 0:E]))
                link(V.tensor_copy(repl[:, :, 0:2], top[:, :, 0:2]))
                V.tensor_tensor(ge, vals[:, :, 0:E], top[:, :, 0:1].to_broadcast([P, NT, E]), ALU.subtract
                                ).then_inc(s["d_gl"], 1)
                for t in range(NT):
                    link(V.match_replace(vrep[:, t, 0:E + SENT], repl[:, t, :], vals[:, t, 0:E + SENT], -3e38))
                ts(gs, vrep[:, :, 0:E], -2e38, None, ALU.is_lt, ALU.bypass)
                dve.wait_ge(s["a_ge"], tb + 1)
                tt(gs, gs, ge, ALU.mult)
                link(V.tensor_reduce(z4[:, 0, :], gs, AX.X, ALU.add))
                link(V.reciprocal(z4[:, 1, :], z4[:, 0, :]))
                ts(z4[:, 2, :], z4[:, 1, :], 2.0, None, ALU.mult, ALU.bypass)
                tt(gs, gs, z4[:, 2, :].unsqueeze(2).to_broadcast([P, NT, E]), ALU.mult)
                V.tensor_copy(gt.rearrange("p t (e r) -> p t e r", e=E), gs.unsqueeze(3).to_broadcast([P, NT, E, R])
                              ).then_inc(s["d_gate"], 1)
                dve.wait_ge(s["a_ha"], tb + 1)
                dve.wait_ge(s["p_gx"], tb + 1)
                if tb:
                    dve.wait_ge(s["p_c2"], tb)
                V.tensor_tensor(hgx, ha, ps[:, 2, :], ALU.mult).then_inc(s["d_hg"], 1)
                for t in range(NT):
                    dve.wait_ge(s["p_tr"], tb * NT + t + 1)
                    V.bn_stats(bst[:, t, 0:6], ps[:, 3 - t % 2, :]).then_inc(s["d_st"], 1)
                dve.wait_ge(s["d_st"], tb * NT + NT)
                for t in range(NT):
                    link(V.bn_aggr(var[:, tb * NT + t, :], bst[:, t, 0:6]))
                dve.wait_ge(s["p_sc"], tb + 1)
                if tb:
                    dve.wait_ge(s["a_pr"], NT * tb)
                for t in range(NT):
                    sl8 = ps[:, 6, t * NSLOT:(t + 1) * NSLOT]
                    link(V.max(top8[:, t, :], sl8))
                    link(V.match_replace(sc[:, t, :], top8[:, t, :], sl8, -3e38))
                ts(am, sc, -2e38, -1e30, ALU.is_gt, ALU.mult)
                tt(am, am, ps[:, 7, :].rearrange("p (t k) -> p t k", t=NT), ALU.add)
                V.tensor_reduce(nmx, am, AX.X, ALU.max, negate=True).then_inc(s["d_am"], 1)
                dve.wait_ge(s["d_am"], tb + 1)
            V.tensor_copy(lvs[:, 1:2], ones[:, 0:1]).then_inc(s["d_st"], 1)
            dve.wait_ge(s["d_st"], TT + 1)
            dve.wait_ge(s["p_lv"], 1)
            dve.wait_ge(s["a_sg"], 1)
            ts(lvs[:, 1:2], ps[:, 0, 0:1], 1.0 / TOK, 1e-6, ALU.mult, ALU.add)
            link(V.reciprocal(lvs[:, 1:2], lvs[:, 1:2]))
            ts(gq[:, 1, :], lv[:, :], lvs[:, 1:2], None, ALU.mult, ALU.bypass)
            ts(gq[:, 1, :], gq[:, 1, :], 0.5, None, ALU.mult, ALU.bypass)
            stt(gq[:, 1, :], gq[:, 0, :], 2.5, gq[:, 1, :], ALU.mult, ALU.add)
            ts(gq[:, 1, :], gq[:, 1, :], 0.0, 5.0, ALU.max, ALU.min)
            ts(gq[:, 1, :], gq[:, 1, :], 0.5, 1.0 / 1.5, ALU.subtract, ALU.mult)
            V.tensor_scalar(gq[:, 1, :], gq[:, 1, :], 0.0, 1.0, ALU.max, ALU.min).then_inc(s["d_un"], 1)
            dve.wait_ge(s["a_pr"], TT)
            link(V.reciprocal(gq[:, 3, :], den[:, :]))
            dve.wait_ge(s["a_gt"], 1)
            stt(gq[:, 4, :], gq[:, 2, :], 0.05, gq[:, 2, :], ALU.is_ge, ALU.mult)
            tt(gq[:, 4, :], gq[:, 4, :], gq[:, 3, :], ALU.mult)
            V.tensor_tensor(PR, PR, gq[:, 4, :].unsqueeze(2).to_broadcast([P, TT, NSLOT]), ALU.mult).then_inc(s["d_pn"], 1)
            for tb in range(TB):
                dve.wait_ge(s["p_aux"], tb + 1)
                dve.wait_ge(s["g_xc"], tb + 1)
                V.tensor_tensor(X[:, :, tok(tb)], X[:, :, tok(tb)], ps[:, 4:8, :], ALU.add).then_inc(s["d_x3"], 1)
            dve.wait_ge(s["l_diag"], 16)
            link(V.memset(ysm[:, :, :], 0.0))
            for tb in range(TB):
                dve.wait_ge(s["p_y"], tb + 1)
                dg = diag[:, tok(tb)]
                tt(yd, ps[0:NB, 2, :], dg, ALU.mult)
                link(V.tensor_reduce(ysm[:, 0, 2:2 + S], yd.rearrange("p (b s) -> p s b", s=S), AX.X, ALU.add))
                link(V.tensor_scalar(ysm[:, 0, 2:2 + S], ysm[:, 0, 2:2 + S], ilen[:, 1:2], None, ALU.mult))
                link(V.tensor_scalar(ysm[:, 1, 0:S], ysm[:, 0, 0:S], cw[:, 0:1], None, ALU.mult))
                for k in range(1, 4):
                    stt(ysm[:, 1, 0:S], ysm[:, 0, k:k + S], cw[:, k:k + 1], ysm[:, 1, 0:S], ALU.mult, ALU.add)
                V.scalar_tensor_tensor(out=ysm[:, 1, 0:S], in0=ysm[:, 0, 4:4 + S], scalar=cw[:, 4:5], in1=ysm[:, 1, 0:S],
                                       op0=ALU.mult, op1=ALU.add).then_inc(s["d_ys"], 1)
                dve.wait_ge(s["a_yg"], tb + 1)
                V.tensor_tensor(gex.rearrange("p (b s) -> p b s", s=S), dg.rearrange("p (b s) -> p b s", s=S),
                                ysm[:, 2:3, 0:S].to_broadcast([NB, TW // S, S]), ALU.mult).then_inc(s["d_gex"], 1)
                dve.wait_ge(s["p_gb"], tb + 1)
                V.tensor_tensor(Y[:, :, tok(tb)], X[:, :, tok(tb)], ps[:, 3:4, :].to_broadcast([P, DC, TW]), ALU.mult
                                ).then_inc(s["d_c3"], 1)
                dve.wait_ge(s["p_sl"], tb + 1)
                src = ps[:, 1, 0:4 * E].rearrange("p (t k) -> p t k", t=2)
                link(V.tensor_copy(sl[:, 2 * tb:2 * tb + 2, E:2 * E], src[:, :, E:2 * E]))
                tt(sl[:, 2 * tb:2 * tb + 2, 0:E], src[:, :, 0:E], b8[:, :].unsqueeze(1).to_broadcast([P, 2, E]), ALU.add)
            for k in range(2):
                v = sl[:, :, k * E:(k + 1) * E]
                link(V.tensor_reduce(mx4[:, k:k + 1], v, AX.XY, ALU.max))
                link(V.tensor_reduce(mx4[:, 2 + k:3 + k], v, AX.XY, ALU.min))
            V.tensor_copy(gm2, mx4).then_inc(s["d_mx"], 1)
            dve.wait_ge(s["g_mx"], 1)
            tt(gm2[:, 0:2], gm4[:, 0:2], gm4[:, 2:4], ALU.max)
            ts(gm2[:, 0:2], gm2[:, 0:2], 1e-6, None, ALU.max, ALU.bypass)
            link(V.reciprocal(gm2[:, 0:2], gm2[:, 0:2]))
            ts(gm2[:, 0:2], gm2[:, 0:2], 0.5, None, ALU.mult, ALU.bypass)
            link(V.tensor_scalar(lg3, sl[:, :, 0:E], gm2[:, 0:1], None, ALU.mult))
            stt(lg3, sl[:, :, E:2 * E], gm2[:, 1:2], lg3, ALU.mult, ALU.add)
            link(V.tensor_reduce(ss3[:, 0, :], lg3, AX.X, ALU.max))
            V.tensor_tensor(lg3, lg3, ss3[:, 0, :].unsqueeze(2).to_broadcast([P, 8, E]), ALU.subtract
                            ).then_inc(s["d_lg3"], 1)
            dve.wait_ge(s["a_e3"], 1)
            link(V.tensor_reduce(ss3[:, 1, :], pr3, AX.X, ALU.add))
            link(V.reciprocal(ss3[:, 2, :], ss3[:, 1, :]))
            tt(pr3, pr3, ss3[:, 2, :].unsqueeze(2).to_broadcast([P, 8, E]), ALU.mult)
            for t in range(8):
                link(V.max(tp3[:, t, :], pr3[:, t, :]))
            V.tensor_tensor(mk3, pr3, tp3[:, :, 1:2].to_broadcast([P, 8, E]), ALU.subtract).then_inc(s["d_th"], 1)
            dve.wait_ge(s["a_mk"], 1)
            tt(tm3, pr3, mk3, ALU.mult)
            link(V.tensor_reduce(ss3[:, 3, :], tm3, AX.X, ALU.add))
            ts(ss3[:, 3, :], ss3[:, 3, :], 1e-9, None, ALU.add, ALU.bypass)
            link(V.reciprocal(ss3[:, 4, :], ss3[:, 3, :]))
            V.tensor_tensor(tm3, tm3, ss3[:, 4, :].unsqueeze(2).to_broadcast([P, 8, E]), ALU.mult).then_inc(s["d_w3"], 1)
            for tb in range(TB):
                dve.wait_ge(s["p_pm"], tb + 1)
                if tb:
                    dve.wait_ge(s["p_o"], tb * DC)
                V.scalar_tensor_tensor(out=zp, in0=ps[0:RANK, tb % 2, :], scalar=0.5, in1=zt[:, tok(tb)],
                                       op0=ALU.mult, op1=ALU.mult).then_inc(s["d_zp"], 1)
                for oc in range(DC):
                    n = tb * DC + oc
                    dve.wait_ge(s["p_o"], n + 1)
                    if n >= 4:
                        dve.wait_ge(s[f"l_out{n % 4}"], 16 * (n // 4))
                    V.scalar_tensor_tensor(out=oT[n % 4], in0=ps[:, 4 + oc, :], scalar=b3[:, oc:oc + 1],
                                           in1=X[:, oc, tok(tb)], op0=ALU.add, op1=ALU.add).then_inc(s["d_o"], 1)


def kernel(**inputs):
    import numpy as _np
    import concourse.bacc as _bacc
    from concourse import mybir as _mybir
    from concourse.bass_utils import run_bass_kernel_spmd as _run

    g = {k: _np.asarray(v) for k, v in inputs.items()}
    x = g["x"]
    const, diag = constants()
    lay = {
        "const": const, "diag": diag,
        "xconv": x.transpose(2, 1, 0).reshape(DC, P, S * NB)[:, ::-1],
        "xT": x.reshape(TOK, D).T,
        "log_A_real": g["L0_cond_log_A_real"].T, "A_imag": g["L0_cond_A_imag"].T,
        "C_re": g["L0_cond_C"][..., 0].T, "C_im": g["L0_cond_C"][..., 1].T,
        "log_dt": g["L0_cond_log_dt"], "Dskip": g["L0_cond_D"],
        "len0": g["itok_B_8_3872"], "len3": g["itok_B_9_3973"], "ids": g["itok_B_1_14"], "lang": g["itok_B_0_7"].reshape(TT, 4).T,
        "w0": g["L0_ffn_weight_fp8"].T, "w0scale": g["L0_ffn_weight_scale"],
        "wa": g["L1_cond_weight"].transpose(0, 2, 1),
        "w1": g["L1_ffn_w1"], "w2": g["L1_ffn_w2"], "w3": g["L1_ffn_w3"].reshape(D // 2, 2 * HID),
        "l2w": g["L2_cond_W"].T, "wr": g["L2_cond_Wr"].T, "l2a": g["L2_cond_A"].reshape(E * R, D).T,
        "l2b": g["L2_cond_B"].transpose(0, 2, 1).reshape(E * R, D),
        "wq": g["L2_ffn_Wq"].T, "wrq": g["L2_ffn_Wr"].T, "akT": g["L2_ffn_aux_keys"].T,
        "avT": g["L2_ffn_aux_values"].T, "wvd": g["L2_ffn_Wvd"].T, "wvu": g["L2_ffn_Wvu"].T,
        "wu1": g["L2_ffn_Wu1"].T, "bu1": g["L2_ffn_bu1"], "wu2": g["L2_ffn_Wu2"].T, "bu2": g["L2_ffn_bu2"],
        "gate_w1": g["L2_ffn_gate_w1"].reshape(1), "gate_bias": g["L2_ffn_gate_bias"].reshape(1),
        "log_rel": g["L2_ffn_log_rel"],
        "conv_w": g["L3_cond_conv_w"].reshape(5),
        "l3w": g["L3_ffn_W"].T, "b3": g["L3_ffn_b"].reshape(DC, P).T, "b3row": g["L3_ffn_b"],
        "l3a": g["L3_ffn_A"], "l3aT": g["L3_ffn_A"].T, "bmat": g["L3_ffn_Bmat"],
        "lim": g["L3_ffn_LiMEs"], "limT": g["L3_ffn_LiMEs"].T,
    }
    nc = _bacc.Bacc("TRN2", target_bir_lowering=False, num_devices=1)
    arrays, A = {}, {}
    for name, a in lay.items():
        a = _np.ascontiguousarray(a)
        arrays[f"in_{name}"] = a
        A[name] = nc.dram_tensor(f"in_{name}", a.shape, _mybir.dt.from_np(a.dtype), kind="ExternalInput").ap()
    out = nc.dram_tensor("out_T", (D, TOK), f32, kind="ExternalOutput").ap()
    build(nc, A, out)
    r = _run(nc, [arrays], core_ids=[0])
    return _np.ascontiguousarray(r.results[0]["out_T"].T).reshape(NB, S, D)
```

```python
import numpy as np

import concourse.bass as bass
from concourse import mybir
from contextlib import ExitStack

f32 = mybir.dt.float32
f16 = mybir.dt.float16
bf16 = mybir.dt.bfloat16
i32 = mybir.dt.int32
u8 = mybir.dt.uint8
u16 = mybir.dt.uint16
ALU = mybir.AluOpType
ACT = mybir.ActivationFunctionType
AX = mybir.AxisListType

P = 128
NB, S, D = 64, 32, 512
TOK = NB * S
DC = D // P
TB = 4
TW = TOK // TB
NT = TW // P
TT = TOK // P
MODES = 64
LA, LC = 16, 32
PAD = P
KROW = PAD + D
GH = 2
HG = S // GH
ADAPT = 16
GB = 8
NGR = (NB + ADAPT * (GB - 1)) // GB
HID = 1376
HCH = [min(P, HID - P * c) for c in range((HID + P - 1) // P)]
NH = len(HCH)
E, R = 8, 16
BOT, RDIM, NSLOT, VB = 64, 48, 128, 32
RANK = 32
BLK = 64
HALF = 1408
SENT = 6
CMULT = 67
ANCH = TOK // 2

NF4 = np.array([-1.0, -0.6961928009986877, -0.5250730514526367, -0.39491748809814453, -0.28444138169288635,
                -0.18477343022823334, -0.09105003625154495, 0.0, 0.07958029955625534, 0.16093020141124725,
                0.24611230194568634, 0.33791524171829224, 0.44070982933044434, 0.5626170039176941,
                0.7229568362236023, 1.0], np.float32)
BOUNDS = ((NF4[:-1] + NF4[1:]) * np.float32(0.5)).astype(np.float32)
STEPS = (NF4[1:] - NF4[:-1]).astype(np.float32)

STEEP = 2.0 ** 40
ROUND = float(1.5 * 2 ** 23)
LOG2E = float(np.log2(np.e))
LN2_HI = float(np.float32(0.693359375))
LN2_LO = float(np.log(2.0) - 0.693359375)
TWO_PI = 2 * np.pi
PI_A = float(np.float32(6.28125))
PI_B = float(np.float32(np.round((TWO_PI - 6.28125) * 2 ** 21) / 2 ** 21))
PI_C = float(np.float32(TWO_PI - 6.28125 - PI_B))

C_ID = 0
C_MUL = C_ID + P
C_PH = C_MUL + CMULT
C_IOTA = C_PH + CMULT
C_L = C_IOTA + P
C_LREV = C_L + DC
C_PCOL = C_LREV + DC
C_BND = C_PCOL + 1
C_COLS = C_BND + len(BOUNDS)


def constants():
    c = np.zeros((P, C_COLS), np.float32)
    c[:, C_ID:C_ID + P] = np.eye(P)
    mul = np.concatenate([np.arange(LC), LC * np.arange(LA), LC * np.arange(LA), [1, 1, 0.5]])
    c[:, C_MUL:C_MUL + CMULT] = mul
    ph = np.zeros((P, CMULT))
    ph[:MODES, :LC] = np.pi / 2
    ph[:, LC:LC + LA] = np.pi / 2
    ph[:, LC + 2 * LA] = np.pi / 2
    c[:, C_PH:C_PH + CMULT] = ph
    c[:, C_IOTA:C_IOTA + P] = np.arange(P)
    p = np.arange(P)[:, None]
    c[:, C_L:C_L + DC] = np.arange(DC) * P + p
    c[:, C_LREV:C_LREV + DC] = np.arange(DC) * P + (P - 1 - p)
    c[:, C_PCOL] = np.arange(P)
    c[:, C_BND:] = -BOUNDS * np.float32(STEEP)
    diag = (np.arange(NB)[:, None] == (np.arange(TOK) // S)[None, :]).astype(np.float32)
    return c, diag


def build(nc, A, out):
    ctx = ExitStack()
    with ctx:
        def sb(name, shape, dt=f32):
            return ctx.enter_context(nc.sbuf_tensor(name, shape, dt))

        ps = ctx.enter_context(nc.psum_tensor("ps", [P, 8, 512], f32))
        kpad = nc.dram_tensor("kpad", [S, KROW], f32, kind="Internal")

        X = sb("X", [P, DC, TOK])
        Yp = sb("Yp", [P, DC * TOK + GB * S])
        Up = sb("Up", [P, DC, TOK + (GB - 1) * S])
        yf = Yp[:, 0:DC * TOK]
        Y = yf.rearrange("p (c n) -> p c n", c=DC)
        uf = Up[:, :, :].rearrange("p c n -> p (c n)")
        uc = uf[:, 0:DC * TOK].rearrange("p (c n) -> p c n", c=DC)
        T = sb("T", [P, 2, GH, D])
        tf = T[:, :, :, :].rearrange("p a b c -> p (a b c)")
        W1T = sb("W1T", [P, DC, HID])
        W2T = sb("W2T", [P, DC, HID])
        W3T = sb("W3T", [P, NH, D])
        w1f = W1T[:, :, :].rearrange("p a b -> p (a b)")
        w2f = W2T[:, :, :].rearrange("p a b -> p (a b)")
        w3f = W3T[:, :, :].rearrange("p a b -> p (a b)")
        cst = sb("cst", [P, C_COLS])
        ident = cst[:, C_ID:C_ID + P]
        ones = sb("ones", [P, P])

        raw = sb("raw", [P, 2, HALF])
        acc = sb("acc", [P, HALF])
        above = sb("above", [P, 2, HALF], bf16)
        amax = sb("amax", [P, 2, HALF // BLK])
        rmax = sb("rmax", [P, HALF // BLK])

        ang = w1f[:, 0:S * CMULT].rearrange("p (h m) -> p h m", h=S)
        dec = w1f[:, S * CMULT:2 * S * CMULT].rearrange("p (h m) -> p h m", h=S)
        turn = w2f[:, 0:S * CMULT].rearrange("p (h m) -> p h m", h=S)
        n0 = S * CMULT
        pc = w2f[:, n0:n0 + S * LA].rearrange("p (h m) -> p h m", h=S)
        pq = w2f[:, n0 + S * LA:n0 + 2 * S * LA].rearrange("p (h m) -> p h m", h=S)
        n0 += 2 * S * LA
        ksb = w2f[0:LA, n0:n0 + S * LC].rearrange("p (h m) -> p h m", h=S)
        n0 += S * LC
        sm = w2f[:, n0:n0 + 32 * S].rearrange("p (k h) -> p k h", h=S)
        zpad = w3f[0:S, 5120:5120 + PAD]
        w0u = w1f[:, 4992:5504].bitcast(u8).rearrange("p (c o) -> p c o", c=DC)
        w0 = w3f[:, 0:2048].rearrange("p (c o) -> p c o", c=DC)
        h16a = acc[:, 0:1024].bitcast(u16).rearrange("p (c o) -> p c o", c=DC)
        h16b = raw[:, 1, 0:1024].bitcast(u16).rearrange("p (c o) -> p c o", c=DC)
        wsc = sb("wsc", [P, 1])
        leni = sb("leni", [P, 2, NB], i32)
        lenf = sb("lenf", [P, 2, NB])
        mnat = sb("mnat", [P, DC, NB])
        mrev = sb("mrev", [P, DC, NB])

        idc_i = sb("idc_i", [NB, 1], i32)
        idr_i = sb("idr_i", [NB, NB], i32)
        idc = sb("idc", [NB, 1])
        keyc = sb("keyc", [NB, 1])
        keyr = sb("keyr", [NB, NB])
        below = sb("below", [NB, NB])
        rank = sb("rank", [NB, 1])
        oneh = sb("oneh", [NB, NB + ADAPT + 1])
        cnt = sb("cnt", [1, 4, ADAPT])
        gmat = sb("gmat", [1, NGR, ADAPT])
        gord = sb("gord", [1, ADAPT + 1 + NGR])
        order = sb("order", [1, NB + ADAPT + 1 + NGR], i32)
        WS = w3f[:, 0:2 * DC * D].rearrange("p (s c o) -> p s c o", s=2, c=DC)
        gslot = ps[:, 0:4, :].rearrange("p b n -> p (b n)").rearrange("p (s c n) -> p s c n", s=2, c=DC)
        l2w = tf[:, 0:2048].rearrange("p (c o) -> p c o", c=DC)
        rawf = raw[:, :, :].rearrange("p a b -> p (a b)")
        tail = rawf[:, 0:2048]
        l2a = tail[:, 0:512].rearrange("p (c o) -> p c o", c=DC)
        l2u = tail[:, 512:1024].rearrange("p (c o) -> p c o", c=DC)
        l2b = tail[:, 1024:1536]
        l2q = tail[:, 1536:1792].rearrange("p (c o) -> p c o", c=DC)
        l3a = tail[:, 1792:1920].rearrange("p (c o) -> p c o", c=DC)
        wvd = tail[:, 1920:2048].rearrange("p (c o) -> p c o", c=DC)
        avT = acc[:, 0:512].rearrange("p (c o) -> p c o", c=DC)
        wvu = acc[0:VB, 512:1024]
        v1 = acc[0:VB, 1024:1024 + NSLOT]
        l2r = sb("l2r", [P, DC, E])
        rq48 = sb("rq48", [BOT, RDIM])
        akT = sb("akT", [BOT + 1, NSLOT])
        rk = sb("rk", [RDIM + 1, NSLOT])
        bu1 = sb("bu1", [P, 1])
        wu2 = sb("wu2", [P, 1])
        gsc = sb("gsc", [P, 3])
        lan_i = sb("lan_i", [P, TT], i32)
        lan = sb("lan", [P, TT])
        lbias = sb("lbias", [P, TT, E])
        b3 = sb("b3", [P, DC])
        b8 = sb("b8", [P, E])
        lim = sb("lim", [E, RANK])
        limT = sb("limT", [RANK, E])
        w16 = sb("w16", [P, DC, 2 * E])
        cw = sb("cw", [NB, 5])
        lc_i = sb("lc_i", [NB, 1], i32)
        ilen = sb("ilen", [NB, 2])

        hs = yf[:, 0:NH * TW].rearrange("p (n t) -> p n t", n=NH)
        sg = [yf[:, NH * TW + i * TW:NH * TW + (i + 1) * TW] for i in range(2)]

        free = [0]

        def cut(n, parts=P):
            a = free[0]
            free[0] += n
            assert free[0] <= DC * TOK
            return uf[0:parts, a:a + n]

        def tiles(n, k, parts=P):
            return cut(n * k, parts).rearrange("p (t k) -> p t k", t=n)

        ha, hgx, qT, rqT, gu = cut(512), cut(512), cut(512, BOT + 1), cut(512, RDIM + 1), cut(512)
        vals, vrep = tiles(NT, 16), tiles(NT, 16)
        top, repl, ge, gs = (tiles(NT, 8) for _ in range(4))
        gt = tiles(NT, E * R)
        z4 = tiles(3, NT)
        sc, am = tiles(NT, NSLOT), tiles(NT, NSLOT)
        top8 = tiles(NT, 8)
        nmx = cut(NT)
        bst = tiles(NT, 8)
        v2, bm, aT = cut(D), cut(D, RANK), cut(D, RANK)
        PR = w1f[:, 0:TT * NSLOT].rearrange("p (t k) -> p t k", t=TT)
        oT = [w1f[:, 512 * i:512 * (i + 1)] for i in range(4)]
        PT = w1f[:, 2048:4096]
        zt = w2f[0:RANK, 0:TOK]
        diag = w2f[0:NB, 2048:4096]
        sl, lg3, pr3, mk3, tp3, tm3 = (w2f[:, 4096 + 128 * i:4096 + 128 * i + k * 8].rearrange("p (t k) -> p t k", t=8)
                                       for i, k in enumerate([16, 8, 8, 8, 8, 8]))
        ss3 = w2f[:, 4864:4864 + 8 * 6].rearrange("p (a t) -> p a t", t=8)
        mx4, gm4, gm2 = w2f[:, 4928:4932], w2f[:, 4932:4936], w2f[:, 4936:4940]
        yd, gex = w3f[0:NB, 0:512], w3f[0:NB, 512:1024]
        ysm = w3f[0:NB, 1024:1024 + 4 * 40].rearrange("p (a b) -> p a b", a=4)
        zp = w3f[0:RANK, 1536:2048]
        wT = w3f[0:E, 2048:3072]
        l3w = w3f[:, 3584:5632].rearrange("p (c o) -> p c o", c=DC)
        var = sb("var", [P, TT, 2])
        lv = sb("lv", [P, TT])
        lvs = sb("lvs", [P, 2])
        lrn = sb("lrn", [P, TT])
        den = sb("den", [P, TT])
        gq = sb("gq", [P, 6, TT])

        s = {}
        for n in """g_u g_xs d_nrm m_ready m_used l_cst l_s4 l_w0 l_u l_x l_len l_ids l_kpad l_strip0 l_strip1 l_raw0 l_raw1 l_wa0 l_wa1 l_late l_prep l_l3w
                l_sml l_diag l_out0 l_out1 l_out2 l_out3
                v_step a_step d_ones d_mask g_mask d_ang a_ang d_pp p_k d_k d_w0 p_conv d_conv p_ffn0 d_x1
                d_oneh p_ord d_ord p_ad ad_out  d_dq p_qt a_qt p_gu a_silu d_h p_down d_x2
                p_prep a_v1 p_v2 prep_done p_lg d_gl a_ge d_gate p_ha a_ha p_gx d_hg p_c2 a_c2 g_xc
                p_tr d_st p_q a_q p_rq a_rq p_gup a_gu p_lr a_lr p_sc d_am a_pr a_lv p_lv a_sg d_un a_gt
                d_pn p_pt a_pt p_aux d_x3 p_y d_ys a_yg d_gex p_gb d_c3 p_z a_z p_sl d_mx g_mx d_lg3 a_e3 d_th a_mk
                d_w3 p_wt a_wt p_pm d_zp p_o d_o""".split():
            s[n] = ctx.enter_context(nc.semaphore(n))
        block = ctx.enter_context(nc.Block())

        UNITS = [(1, c) for c in range(NH)] + [(3, q) for q in range(4)]
        NU = len(UNITS)
        PARTS = 3 * NU
        LV = (len(NF4) - 1) // 3
        assert LV * 3 == len(BOUNDS)
        QB = np.cumsum([0] + [2 if k == 1 else (NH + 3) // 4 for k, _ in UNITS]).tolist()

        def unit_shape(u):
            return (HCH[UNITS[u][1]], 2 * D) if UNITS[u][0] == 1 else (P, HALF)

        def acc_of(u):
            return tf if u >= 5 and u % 2 else acc

        def banks_before(u):
            return QB[u] if u < 6 else QB[u - 1]

        def quant_dests(u):
            kind, c = UNITS[u]
            out_, n = [], QB[u]
            if kind == 1:
                h = HCH[c]
                for m, dst in enumerate((W1T, W2T)):
                    out_.append([(dst[:, :, c * P:c * P + h],
                                  ps[:, 6 + (n + m) % 2, :].rearrange("p (c h) -> p c h", c=DC)[:, :, 0:h])])
                return out_
            g, q = c // 2, c % 2
            rows = slice(g * 2 * P + q, (g + 1) * 2 * P, 2)
            for m, c0 in enumerate(range(0, NH, 4)):
                k = min(4, NH - c0)
                whole = sum(HCH[c0 + i] == P for i in range(k))
                src = ps[:, 6 + (n + m) % 2, :].rearrange("p (c r) -> p c r", c=4)
                pairs = [(W3T[:, c0:c0 + whole, rows], src[:, 0:whole, :])]
                if whole < k:
                    r = HCH[c0 + k - 1]
                    pairs.append((W3T[0:r, c0 + k - 1, rows], src[0:r, k - 1, :]))
                out_.append(pairs)
            return out_

        def tok(tb):
            return slice(tb * TW, (tb + 1) * TW)

        def tile(tb, t):
            return slice(tb * TW + t * P, tb * TW + (t + 1) * P)

        @block.sync
        def _(sp):
            sp.dma_start(cst[:, :], A["const"]).then_inc(s["l_cst"], 16)
            for half in range(2):
                r = slice(half * MODES, (half + 1) * MODES)
                sp.dma_start(sm[r, 1, :], A["log_A_real"]).then_inc(s["l_s4"], 16)
                sp.dma_start(sm[r, 2, :], A["A_imag"]).then_inc(s["l_s4"], 16)
                sp.dma_start(sm[r, 3, :], A["C_re"]).then_inc(s["l_s4"], 16)
                sp.dma_start(sm[r, 4, :], A["C_im"]).then_inc(s["l_s4"], 16)
            sp.dma_start(sm[:, 0, :], A["log_dt"].partition_broadcast(P)).then_inc(s["l_s4"], 16)
            sp.dma_start(sm[0:1, 5, :], A["Dskip"].partition_broadcast(1)).then_inc(s["l_s4"], 16)
            sp.dma_start(leni[:, 0, :], A["len0"].partition_broadcast(P)).then_inc(s["l_len"], 16)
            sp.dma_start(leni[:, 1, :], A["len3"].partition_broadcast(P)).then_inc(s["l_len"], 16)
            sp.dma_start(w0u, A["w0"].bitcast(u8).rearrange("(c p) o -> p c o", p=P)).then_inc(s["l_w0"], 16)
            sp.dma_start(wsc[:, :], A["w0scale"].partition_broadcast(P)).then_inc(s["l_w0"], 16)
            for c in range(DC):
                sp.dma_start(uc[:, c, :], A["xconv"][c]).then_inc(s["l_u"], 16)

            def load_unit(u):
                kind, c = UNITS[u]
                if u >= 2:
                    sp.wait_ge(s["m_ready"], 15 * (u - 1))
                    sp.wait_ge(s[f"l_raw{u % 2}"], 32 * (u // 2))
                slot = raw[:, u % 2, :]
                got = s[f"l_raw{u % 2}"]
                if kind == 1:
                    h = HCH[c]
                    sp.dma_start(slot[0:h, 0:D], A["w1"][c * P:c * P + h, :]).then_inc(got, 16)
                    sp.dma_start(slot[0:h, D:2 * D], A["w2"][c * P:c * P + h, :]).then_inc(got, 16)
                else:
                    g, q = c // 2, c % 2
                    o = q * (2 * HID - HALF)
                    for k in range(2):
                        cols = slice(k * HALF // 2, (k + 1) * HALF // 2)
                        sp.dma_start(slot[:, cols], A["w3"][g * P:(g + 1) * P, o + cols.start:o + cols.stop]
                                     ).then_inc(got, 16)

            load_unit(0)
            sp.wait_ge(s["d_k"], 1)
            kv = kpad.ap()
            sp.dma_start(kv[:, 0:PAD], zpad).then_inc(s["l_kpad"], 16)
            sp.dma_start(kv[:, PAD:KROW].rearrange("h (a c) -> a h c", a=LA), ksb).then_inc(s["l_kpad"], 16)
            sp.wait_ge(s["l_kpad"], 32)
            for g in range(HG):
                if g >= 2:
                    sp.wait_ge(s["p_conv"], g - 1)
                    sp.wait_ge(s[f"l_strip{g % 2}"], 16 * (g // 2))
                sp.dma_start(T[:, g % 2, :, :], bass.AP(kpad, g * GH * KROW + 1, [[1, P], [KROW, GH], [1, D]])
                             ).then_inc(s[f"l_strip{g % 2}"], 16)
                if g == 1:
                    sp.dma_start(X[:, :, :], A["xT"].rearrange("(c p) n -> p c n", p=P)).then_inc(s["l_x"], 16)
                    sp.wait_ge(s["d_w0"], 1)
                    load_unit(1)
                if g % 4 == 3:
                    load_unit(g // 4 + 2)
            for a in range(ADAPT):
                if a == 0:
                    sp.wait_ge(s["d_ord"], 1)
                    sp.wait_ge(s["p_ffn0"], TB * DC)
                if a >= 2:
                    done = sp.value_load(order[0:1, NB + a - 1:NB + a], min_val=0, max_val=NGR)
                    sp.wait_ge(s["p_ad"], done + 1)
                    sp.wait_ge(s[f"l_wa{a % 2}"], 16 * (a // 2))
                sp.dma_start(WS[:, a % 2, :, :], A["wa"][a].rearrange("(c p) o -> p c o", p=P)
                             ).then_inc(s[f"l_wa{a % 2}"], 16)
                if a % 3 == 2:
                    load_unit(6 + a // 3)
            for u in range(11, NU):
                load_unit(u)
            sp.wait_ge(s["m_ready"], 15 * NU)
            for dst, name in ((l2a, "l2a"), (l2u, "wu1"), (l2q, "wq"), (l3a, "l3a"), (wvd, "wvd")):
                sp.dma_start(dst, A[name].rearrange("(c p) o -> p c o", p=P)).then_inc(s["l_late"], 16)
            sp.dma_start(l2b, A["l2b"]).then_inc(s["l_late"], 16)
            sp.wait_ge(s["p_qt"], QB[NU])
            sp.dma_start(l2w, A["l2w"].rearrange("(c p) o -> p c o", p=P)).then_inc(s["l_late"], 16)
            sp.dma_start(avT, A["avT"].rearrange("(c p) o -> p c o", p=P)).then_inc(s["l_prep"], 16)
            sp.dma_start(wvu, A["wvu"]).then_inc(s["l_prep"], 16)
            sp.wait_ge(s["p_down"], TB * NH)
            sp.dma_start(bm, A["bmat"]).then_inc(s["l_prep"], 16)
            sp.dma_start(aT, A["l3aT"]).then_inc(s["l_prep"], 16)
            sp.dma_start(l3w, A["l3w"].rearrange("(c p) o -> p c o", p=P)).then_inc(s["l_l3w"], 16)
            sp.dma_start(diag, A["diag"]).then_inc(s["l_diag"], 16)
            for n in range(TB * DC):
                tb, oc = n // DC, n % DC
                sp.wait_ge(s["d_o"], n + 1)
                sp.dma_start(out[oc * P:(oc + 1) * P, tok(tb)], oT[n % 4]).then_inc(s[f"l_out{n % 4}"], 16)
            for i in range(4):
                sp.wait_ge(s[f"l_out{i}"], 16 * TB * DC // 4)

        @block.gpsimd
        def _(pool):
            pool.dma_start(idc_i[:, :], A["ids"].rearrange("(n a) -> n a", a=1)).then_inc(s["l_ids"], 16)
            pool.dma_start(idr_i[:, :], A["ids"].partition_broadcast(NB)).then_inc(s["l_ids"], 16)
            for dst, src in ((l2r[:, :, :], A["wr"].rearrange("(c p) o -> p c o", p=P)), (rq48[:, :], A["wrq"]),
                             (akT[0:BOT, :], A["akT"]),
                             (akT[BOT:BOT + 1, :], A["log_rel"].partition_broadcast(1)),
                             (rk[RDIM:RDIM + 1, :], A["log_rel"].partition_broadcast(1)),
                             (bu1[:, :], A["bu1"].rearrange("(n a) -> n a", a=1)), (wu2[:, :], A["wu2"]),
                             (gsc[:, 0:1], A["gate_w1"].partition_broadcast(P)),
                             (gsc[:, 1:2], A["gate_bias"].partition_broadcast(P)),
                             (gsc[:, 2:3], A["bu2"].partition_broadcast(P)),
                             (b3[:, :], A["b3"]), (b8[:, :], A["b3row"][0:E].partition_broadcast(P)),
                             (lim[:, :], A["lim"]), (limT[:, :], A["limT"]),
                             (cw[:, :], A["conv_w"].partition_broadcast(NB)),
                             (lc_i[:, :], A["len3"].rearrange("(n a) -> n a", a=1))):
                pool.dma_start(dst, src).then_inc(s["l_sml"], 16)
            for q in range(4):
                src = A["lang"][q]
                pool.dma_start(lan_i[q * S:(q + 1) * S, :], src.partition_broadcast(S)).then_inc(s["l_sml"], 16)
            pool.wait_ge(s["d_mask"], 1)
            for c in range(DC):
                pool.wait_ge(s["l_u"], 16 * DC)
                v = uc[:, c, :].rearrange("p (h b) -> p h b", b=NB)
                nc.gpsimd.tensor_tensor(v, v, mrev[:, c:c + 1, :].to_broadcast([P, S, NB]), ALU.mult
                                        ).then_inc(s["g_u"], 1)
            pool.wait_ge(s["d_ord"], 1)
            pool.wait_ge(s["d_x1"], TB * DC)
            with pool.Fori(0, NB) as t:
                b = pool.value_load(order[0:1, bass.ds(t, 1)], min_val=0, max_val=NB - 1)
                pool.tensor_copy(Y[:, :, bass.ds(t * S, S)], X[:, :, bass.ds(b * S, S)]).then_inc(s["g_xs"], 1)
            nc.gpsimd.memset(Yp[:, DC * TOK:], 0.0).then_inc(s["g_xs"], GB)
            for tb in range(TB):
                pool.wait_ge(s["a_c2"], tb + 1)
                pool.wait_ge(s["p_c2"], tb + 1)
                nc.gpsimd.tensor_tensor(X[:, :, tok(tb)], X[:, :, tok(tb)], Y[:, :, tok(tb)], ALU.add
                                        ).then_inc(s["g_xc"], 1)
            pool.wait_ge(s["d_mx"], 1)
            nc.gpsimd.partition_all_reduce(gm4, mx4, P, bass.bass_isa.ReduceOp.absmax).then_inc(s["g_mx"], 1)

        NSML = 16 * 20

        @block.scalar
        def _(act):
            act.wait_ge(s["d_ang"], 1)
            nc.scalar.activation(dec, dec, ACT.Exp).then_inc(s["a_ang"], 1)
            act.wait_ge(s["d_ang"], 2)
            nc.scalar.activation(ang, ang, ACT.Sin).then_inc(s["a_ang"], 1)

            def levels(k):
                u = k // 3
                h, w = unit_shape(u)
                act.wait_ge(s["d_nrm"], u + 1)
                for i in range(LV * (k % 3), LV * (k % 3 + 1)):
                    m = 15 * u + i
                    if m >= 2:
                        act.wait_ge(s["m_used"], m - 1)
                    nc.scalar.activation(above[0:h, m % 2, 0:w], raw[0:h, u % 2, 0:w], ACT.Relu,
                                         scale=STEEP, bias=cst[0:h, C_BND + i:C_BND + i + 1]).then_inc(s["m_ready"], 1)

            def evac_quant(u):
                for m, pairs in enumerate(quant_dests(u)):
                    act.wait_ge(s["p_qt"], QB[u] + m + 1)
                    for dst, src in pairs:
                        last = nc.scalar.activation(dst, src, ACT.Copy)
                    last.then_inc(s["a_qt"], 1)

            k = 0
            for g in range(HG):
                if g % 4 < 3:
                    levels(k)
                    if k % 3 == 0 and k:
                        evac_quant(k // 3 - 1)
                    k += 1
            for tb in range(3):
                levels(k)
                if k % 3 == 0:
                    evac_quant(k // 3 - 1)
                k += 1
            act.wait_ge(s["d_ord"], 1)
            act.sem_inc(s["ad_out"], 2)
            for a in range(ADAPT):
                if a < 15:
                    levels(k)
                    k += 1
                lo = act.value_load(order[0:1, NB + a:NB + a + 1], min_val=0, max_val=NGR)
                hi = act.value_load(order[0:1, NB + a + 1:NB + a + 2], min_val=0, max_val=NGR)
                with act.If(lo < hi), act.Fori(lo, hi) as g:
                    t = act.value_load(order[0:1, bass.ds(g + (NB + ADAPT + 1), 1)], min_val=0, max_val=NB - 1)
                    act.wait_ge(s["p_ad"], g + 2)
                    act.activation(Up[:, :, bass.ds(t * S, GB * S)],
                                   gslot[:, bass.ds(g % 2, 1), :, :].rearrange("p a c n -> p (a c) n"),
                                   ACT.Copy).then_inc(s["ad_out"], 1)
                if a % 3 == 0:
                    evac_quant(4 + a // 3)
            for n in range(TB * NH):
                h = HCH[n % NH]
                if n < NH:
                    levels(k)
                    if n % 3 == 0 and n:
                        evac_quant(k // 3 - 1)
                    k += 1
                act.wait_ge(s["p_gu"], n + 1)
                if n >= 2:
                    act.wait_ge(s["d_h"], n - 1)
                nc.scalar.activation(sg[n % 2][0:h, :], ps[0:h, n % 2, :], ACT.Silu).then_inc(s["a_silu"], 1)
                if n == NH - 1:
                    while k < PARTS:
                        levels(k)
                        if k % 3 == 0:
                            evac_quant(k // 3 - 1)
                        k += 1
                    evac_quant(NU - 1)
            act.wait_ge(s["p_prep"], 1)
            nc.scalar.activation(v1, ps[0:VB, 1, 0:NSLOT], ACT.Copy).then_inc(s["a_v1"], 1)
            nc.scalar.activation(rk[0:RDIM, :], ps[0:RDIM, 0, 0:NSLOT], ACT.Copy,
                                 scale=float(RDIM ** -0.5)).then_inc(s["prep_done"], 1)
            nc.scalar.activation(w16[:, :, E:2 * E], ps[:, 2, 0:DC * E].rearrange("p (c e) -> p c e", c=DC),
                                 ACT.Copy).then_inc(s["prep_done"], 1)
            act.wait_ge(s["p_v2"], 1)
            nc.scalar.activation(v2, ps[:, 3, :], ACT.Copy).then_inc(s["prep_done"], 1)
            for tb in range(TB):
                act.wait_ge(s["p_ha"], tb + 1)
                if tb:
                    act.wait_ge(s["d_hg"], tb)
                nc.scalar.activation(ha, ps[:, 0, :], ACT.Copy).then_inc(s["a_ha"], 1)
                act.wait_ge(s["d_gl"], tb + 1)
                nc.scalar.activation(ge, ge, ACT.Exp).then_inc(s["a_ge"], 1)
                act.wait_ge(s["p_c2"], tb + 1)
                nc.scalar.activation(Y[:, :, tok(tb)], ps[:, 4:8, :], ACT.Copy).then_inc(s["a_c2"], 1)
                act.wait_ge(s["p_q"], tb + 1)
                if tb:
                    act.wait_ge(s["p_sc"], tb)
                nc.scalar.activation(qT[0:BOT, :], ps[0:BOT, 0, :], ACT.Copy).then_inc(s["a_q"], 1)
                act.wait_ge(s["p_rq"], tb + 1)
                nc.scalar.activation(rqT[0:RDIM, :], ps[0:RDIM, 1, :], ACT.Copy).then_inc(s["a_rq"], 1)
                act.wait_ge(s["p_gup"], tb + 1)
                nc.scalar.activation(gu, ps[:, 4, :], ACT.Gelu_apprx_tanh, bias=bu1[:, 0:1]).then_inc(s["a_gu"], 1)
                act.wait_ge(s["p_lr"], tb + 1)
                nc.scalar.activation(lrn[:, tb * NT:(tb + 1) * NT], ps[:, 5, 0:NT], ACT.Copy).then_inc(s["a_lr"], 1)
                act.wait_ge(s["d_am"], tb + 1)
                for t in range(NT):
                    k = tb * NT + t
                    nc.scalar.activation(PR[:, k, :], am[:, t, :], ACT.Exp, bias=nmx[:, t:t + 1],
                                         accum_out=den[:, k:k + 1]).then_inc(s["a_pr"], 1)
            act.wait_ge(s["d_st"], TT + 1)
            nc.scalar.activation(lv[:, :], var[:, :, 1], ACT.Ln, bias=1.0, accum_out=lvs[:, 0:1]).then_inc(s["a_lv"], 1)
            act.wait_ge(s["a_lr"], TB)
            nc.scalar.activation(gq[:, 0, :], lrn[:, :], ACT.Sigmoid, bias=gsc[:, 2:3]).then_inc(s["a_sg"], 1)
            act.wait_ge(s["d_un"], 1)
            nc.scalar.activation(gq[:, 2, :], gq[:, 1, :], ACT.Sigmoid, scale=gsc[:, 0:1], bias=gsc[:, 1:2]
                                 ).then_inc(s["a_gt"], 1)
            for tb in range(TB):
                act.wait_ge(s["p_pt"], tb + 1)
                nc.scalar.activation(PT[:, tok(tb)], ps[:, tb % 2, :], ACT.Copy).then_inc(s["a_pt"], 1)
            for tb in range(TB):
                act.wait_ge(s["d_ys"], tb + 1)
                nc.scalar.activation(ysm[:, 2, 0:S], ysm[:, 1, 0:S], ACT.Sigmoid).then_inc(s["a_yg"], 1)
                act.wait_ge(s["p_z"], tb + 1)
                nc.scalar.activation(zt[:, tok(tb)], ps[0:RANK, 0, :], ACT.Copy).then_inc(s["a_z"], 1)
            act.wait_ge(s["d_lg3"], 1)
            nc.scalar.activation(pr3, lg3, ACT.Exp).then_inc(s["a_e3"], 1)
            act.wait_ge(s["d_th"], 1)
            nc.scalar.activation(mk3, mk3, ACT.Sigmoid, scale=2.0).then_inc(s["a_mk"], 1)
            for k in range(2):
                act.wait_ge(s["p_wt"], k + 1)
                nc.scalar.activation(wT[:, k * 512:(k + 1) * 512], ps[0:E, 2 + k, :], ACT.Copy).then_inc(s["a_wt"], 1)

        @block.tensor
        def _(pe):
            def mm(o, l, r, start, stop, **kw):
                return nc.tensor.matmul(o, l, r, start=start, stop=stop, **kw)

            pe.wait_ge(s["l_cst"], 16)
            pe.wait_ge(s["d_ones"], 1)
            pe.wait_ge(s["d_oneh"], 1)
            mm(ps[0:1, 5, 0:NB], cst[0:NB, C_PCOL:C_PCOL + 1], oneh[:, 0:NB], True, True)
            mm(ps[0:1, 5, NB:NB + ADAPT + 1], ones[0:NB, 0:1], oneh[:, NB:], True, True).then_inc(s["p_ord"], 1)
            pe.wait_ge(s["d_pp"], 1)
            for h in range(S):
                last = mm(ps[0:LA, 6 + h // 16, (h % 16) * LC:(h % 16 + 1) * LC], pc[:, h, :], turn[:, h, 0:LC],
                          True, True)
            last.then_inc(s["p_k"], 1)

            def turn_unit(u):
                kind, c = UNITS[u]
                pe.wait_ge(s["d_dq"], u + 1)
                n = QB[u]
                acc = acc_of(u)
                groups = []
                if kind == 1:
                    h = HCH[c]
                    for m in range(2):
                        groups.append([(ps[:, 6 + (n + m) % 2, k * P:k * P + h],
                                        acc[0:h, m * D + k * P:m * D + (k + 1) * P], h) for k in range(DC)])
                else:
                    o = (c % 2) * (HALF - HID)
                    for m, c0 in enumerate(range(0, NH, 4)):
                        groups.append([(ps[0:HCH[i], 6 + (n + m) % 2, (i - c0) * P:(i - c0 + 1) * P],
                                        acc[:, o + i * P:o + i * P + HCH[i]], P) for i in range(c0, min(c0 + 4, NH))])
                for m, group in enumerate(groups):
                    if n + m >= 2:
                        pe.wait_ge(s["a_qt"], n + m - 1)
                    else:
                        pe.wait_ge(s["d_k"], 1)
                    for dst, src, h in group:
                        last = nc.tensor.transpose(dst, src, ident[0:h, 0:h])
                    last.then_inc(s["p_qt"], 1)

            pe.wait_ge(s["g_u"], DC)
            for g in range(HG):
                pe.wait_ge(s[f"l_strip{g % 2}"], 16 * (g // 2 + 1))
                if g >= 4:
                    pe.wait_ge(s["d_conv"], g - 3)
                for k in range(GH):
                    h = g * GH + k
                    for lb in range(DC):
                        o = lb * GH * NB + k * NB
                        for jb in range(lb + 1):
                            last = mm(ps[:, g % 4, o:o + NB], T[:, g % 2, k, (lb - jb) * P:(lb - jb + 1) * P],
                                      uc[:, jb, h * NB:(h + 1) * NB], jb == 0, jb == lb)
                last.then_inc(s["p_conv"], 1)
                if g % 4 == 3:
                    turn_unit(g // 4)
            pe.wait_ge(s["d_conv"], HG)
            pe.wait_ge(s["d_w0"], 1)
            pe.wait_ge(s["d_ord"], 1)
            for n in range(TB * DC):
                tb, oc = n // DC, n % DC
                if n >= 2:
                    pe.wait_ge(s["d_x1"], n - 1)
                for c in range(DC):
                    last = mm(ps[:, 4 + n % 2, :], w0[:, c, oc * P:(oc + 1) * P], Y[:, c, tok(tb)], c == 0, c == DC - 1)
                last.then_inc(s["p_ffn0"], 1)
            turn_unit(4)
            pe.wait_ge(s["ad_out"], 2)
            pe.sem_inc(s["p_ad"], 1)
            for a in range(ADAPT):
                pe.wait_ge(s[f"l_wa{a % 2}"], 16 * (a // 2 + 1))
                lo = pe.value_load(order[0:1, NB + a:NB + a + 1], min_val=0, max_val=NGR)
                hi = pe.value_load(order[0:1, NB + a + 1:NB + a + 2], min_val=0, max_val=NGR)
                with pe.If(lo < hi), pe.Fori(lo, hi) as g:
                    t = pe.value_load(order[0:1, bass.ds(g + (NB + ADAPT + 1), 1)], min_val=0, max_val=NB - 1)
                    pe.wait_ge(s["ad_out"], g + 1)
                    pe.wait_ge(s["g_xs"], t + GB)
                    for oc in range(DC):
                        for c in range(DC):
                            last = mm(gslot[:, bass.ds(g % 2, 1), oc, :].rearrange("p a n -> p (a n)"),
                                      WS[:, a % 2, c, oc * P:(oc + 1) * P],
                                      Yp[:, bass.ds(t * S + c * TOK, GB * S)], c == 0, c == DC - 1)
                    last.then_inc(s["p_ad"], 1)
                if a % 3 == 0 and a:
                    turn_unit(4 + a // 3)
            pe.wait_ge(s["ad_out"], hi + 2)

            def up(n):
                tb, c, h = n // NH, n % NH, HCH[n % NH]
                if n < NH:
                    pe.wait_ge(s["a_qt"], QB[n + 1])
                if n >= 2:
                    pe.wait_ge(s["d_h"], n - 1)
                for w, bk in ((W1T, n % 2), (W2T, 2 + n % 2)):
                    for k in range(DC):
                        last = mm(ps[0:h, bk, :], w[:, k, c * P:c * P + h], Up[:, k, tok(tb)], k == 0, k == DC - 1)
                last.then_inc(s["p_gu"], 1)

            def down(n):
                tb, c, h = n // NH, n % NH, HCH[n % NH]
                pe.wait_ge(s["d_h"], n + 1)
                if c == 0 and tb:
                    pe.wait_ge(s["d_x2"], tb * (TW // S))
                for oc in range(DC):
                    last = mm(ps[:, 4 + oc, :], W3T[0:h, c, oc * P:(oc + 1) * P], hs[0:h, c, :], c == 0, c == NH - 1)
                last.then_inc(s["p_down"], 1)

            for n in range(NH):
                up(n)
                if n % 3 == 0 and n:
                    turn_unit(9 + n // 3)
            turn_unit(13)
            turn_unit(14)
            pe.wait_ge(s["a_qt"], QB[NU])
            for n in range(TB * NH):
                down(n)
                if n + NH < TB * NH:
                    up(n + NH)
            pe.wait_ge(s["l_sml"], NSML)
            pe.wait_ge(s["l_prep"], 64)
            pe.wait_ge(s["l_late"], 16 * 7)
            pe.wait_ge(s["a_silu"], TB * NH)
            pe.wait_ge(s["d_h"], TB * NH)
            mm(ps[0:RDIM, 0, 0:NSLOT], rq48[:, :], akT[0:BOT, :], True, True)
            for c in range(DC):
                mm(ps[0:VB, 1, 0:NSLOT], wvd[:, c, :], avT[:, c, :], c == 0, c == DC - 1)
            for c in range(DC):
                last = mm(ps[:, 2, c * E:(c + 1) * E], aT[:, c * P:(c + 1) * P], limT[:, :], True, True)
            last.then_inc(s["p_prep"], 1)
            pe.wait_ge(s["a_v1"], 1)
            mm(ps[:, 3, :], v1, wvu, True, True).then_inc(s["p_v2"], 1)
            pe.wait_ge(s["prep_done"], 4)
            for tb in range(TB):
                pe.wait_ge(s["d_x2"], NB)
                if tb:
                    pe.wait_ge(s["a_pr"], NT * tb)
                    pe.wait_ge(s["a_rq"], tb)
                for t in range(NT):
                    for c in range(DC):
                        last = mm(ps[:, 1, t * E:(t + 1) * E], X[:, c, tile(tb, t)], l2r[:, c, :], c == 0, c == DC - 1)
                last.then_inc(s["p_lg"], 1)
                for c in range(DC):
                    last = mm(ps[:, 0, :], l2a[:, c, :], X[:, c, tok(tb)], c == 0, c == DC - 1)
                last.then_inc(s["p_ha"], 1)
                if tb:
                    pe.wait_ge(s["a_lr"], tb)
                for oc in range(DC):
                    for c in range(DC):
                        mm(ps[:, 4 + oc, :], l2w[:, c, oc * P:(oc + 1) * P], X[:, c, tok(tb)], c == 0, False)
                pe.wait_ge(s["d_gate"], tb + 1)
                if tb:
                    pe.wait_ge(s["d_st"], NT * tb)
                for t in range(NT):
                    last = nc.tensor.transpose(ps[:, 2, t * P:(t + 1) * P],
                                               gt[:, t, :], ident)
                last.then_inc(s["p_gx"], 1)
                pe.wait_ge(s["d_hg"], tb + 1)
                for oc in range(DC):
                    last = mm(ps[:, 4 + oc, :], l2b[:, oc * P:(oc + 1) * P], hgx, False, True)
                last.then_inc(s["p_c2"], 1)
                pe.wait_ge(s["a_c2"], tb + 1)
                for t in range(NT):
                    if tb or t >= 2:
                        pe.wait_ge(s["d_st"], NT * tb + t - 1)
                    for c in range(DC):
                        last = nc.tensor.transpose(ps[:, 3 - t % 2, c * P:(c + 1) * P], Y[:, c, tile(tb, t)], ident)
                    last.then_inc(s["p_tr"], 1)
                for c in range(DC):
                    last = mm(ps[0:BOT, 0, :], l2q[:, c, :], Y[:, c, tok(tb)], c == 0, c == DC - 1)
                last.then_inc(s["p_q"], 1)
                for c in range(DC):
                    last = mm(ps[:, 4, :], l2u[:, c, :], Y[:, c, tok(tb)], c == 0, c == DC - 1)
                last.then_inc(s["p_gup"], 1)
                pe.wait_ge(s["a_q"], tb + 1)
                mm(ps[0:RDIM, 1, :], rq48[:, :], qT[0:BOT, :], True, True).then_inc(s["p_rq"], 1)
                pe.wait_ge(s["a_gu"], tb + 1)
                for t in range(NT):
                    last = mm(ps[:, 5, t:t + 1], gu[:, t * P:(t + 1) * P], wu2[:, :], True, True)
                last.then_inc(s["p_lr"], 1)
                pe.wait_ge(s["a_rq"], tb + 1)
                for t in range(NT):
                    mm(ps[:, 6, t * NSLOT:(t + 1) * NSLOT], rqT[:, t * P:(t + 1) * P], rk[:, :], True, True)
                    last = mm(ps[:, 7, t * NSLOT:(t + 1) * NSLOT], qT[:, t * P:(t + 1) * P], akT[:, :], True, True)
                last.then_inc(s["p_sc"], 1)
            pe.wait_ge(s["a_lv"], 1)
            mm(ps[:, 0, 0:1], ones[:, :], lvs[:, 0:1], True, True).then_inc(s["p_lv"], 1)
            pe.wait_ge(s["d_pn"], 1)
            for tb in range(TB):
                if tb >= 2:
                    pe.wait_ge(s["a_pt"], tb - 1)
                for t in range(NT):
                    last = nc.tensor.transpose(ps[:, tb % 2, t * P:(t + 1) * P], PR[:, tb * NT + t, :], ident)
                last.then_inc(s["p_pt"], 1)
                pe.wait_ge(s["a_pt"], tb + 1)
                if tb:
                    pe.wait_ge(s["d_x3"], tb)
                for oc in range(DC):
                    last = mm(ps[:, 4 + oc, :], v2[:, oc * P:(oc + 1) * P], PT[:, tok(tb)], True, True)
                last.then_inc(s["p_aux"], 1)
            pe.wait_ge(s["l_l3w"], 16)
            for tb in range(TB):
                pe.wait_ge(s["d_x3"], tb + 1)
                for c in range(DC):
                    last = mm(ps[0:NB, 2, :], mnat[:, c, :], X[:, c, tok(tb)], c == 0, c == DC - 1)
                last.then_inc(s["p_y"], 1)
                pe.wait_ge(s["d_gex"], tb + 1)
                mm(ps[:, 3, :], ones[0:NB, :], gex, True, True).then_inc(s["p_gb"], 1)
                pe.wait_ge(s["d_c3"], tb + 1)
                if tb:
                    pe.wait_ge(s["a_z"], tb)
                for c in range(DC):
                    last = mm(ps[0:RANK, 0, :], l3a[:, c, :], Y[:, c, tok(tb)], c == 0, c == DC - 1)
                last.then_inc(s["p_z"], 1)
                for k in range(2):
                    for c in range(DC):
                        a0 = tb * TW + k * 2 * P + 1
                        last = mm(ps[:, 1, k * 2 * E:(k + 1) * 2 * E], Y[:, c, a0:a0 + 2 * P - 1:2], w16[:, c, :],
                                  c == 0, c == DC - 1)
                last.then_inc(s["p_sl"], 1)
            pe.wait_ge(s["d_w3"], 1)
            for k in range(2):
                for t in range(4):
                    last = nc.tensor.transpose(ps[0:E, 2 + k, t * P:(t + 1) * P], tm3[:, 4 * k + t, :], ident)
                last.then_inc(s["p_wt"], 1)
            pe.wait_ge(s["a_wt"], 2)
            pe.wait_ge(s["a_z"], TB)
            for tb in range(TB):
                mm(ps[0:RANK, tb % 2, :], lim[:, :],
                   wT[:, tb * 256:(tb + 1) * 256].unsqueeze(2).to_broadcast([E, 256, 2]), True, True
                   ).then_inc(s["p_pm"], 1)
                for oc in range(DC):
                    if tb:
                        pe.wait_ge(s["d_o"], (tb - 1) * DC + oc + 1)
                    for c in range(DC):
                        mm(ps[:, 4 + oc, :], l3w[:, c, oc * P:(oc + 1) * P], Y[:, c, tok(tb)], c == 0, False)
                    if oc == 0:
                        pe.wait_ge(s["d_zp"], tb + 1)
                    mm(ps[:, 4 + oc, :], bm[:, oc * P:(oc + 1) * P], zp, False, True).then_inc(s["p_o"], 1)

        @block.vector
        def _(dve):
            V = nc.vector
            count = [0]

            def link(ins):
                count[0] += 1
                ins.then_inc(s["v_step"], 1)
                dve.wait_ge(s["v_step"], count[0])

            def tt(o, a, b, op):
                link(V.tensor_tensor(o, a, b, op))

            def ts(o, a, x, y, op0, op1):
                link(V.tensor_scalar(o, a, x, y, op0, op1))

            def stt(o, a, x, b, op0, op1):
                link(V.scalar_tensor_tensor(out=o, in0=a, scalar=x, in1=b, op0=op0, op1=op1))

            V.memset(ones[:, :], 1.0).then_inc(s["d_ones"], 1)
            dve.wait_ge(s["d_ones"], 1)
            dve.wait_ge(s["l_cst"], 16)
            dve.wait_ge(s["l_len"], 32)
            link(V.tensor_copy(lenf[:, :, :], leni[:, :, :]))
            for c in range(DC):
                link(V.tensor_scalar(mnat[:, c, :], lenf[:, 0, :], cst[:, C_L + c:C_L + c + 1], None, ALU.is_gt))
            for c in range(DC):
                last = V.tensor_scalar(mrev[:, c, :], lenf[:, 0, :], cst[:, C_LREV + c:C_LREV + c + 1], None, ALU.is_gt)
            last.then_inc(s["d_mask"], 1)
            dve.wait_ge(s["l_ids"], 32)
            link(V.tensor_copy(idc[:, :], idc_i[:, :]))
            link(V.tensor_copy(keyr[:, :], idr_i[:, :]))
            ts(idc[:, :], idc[:, :], 0.0, float(ADAPT - 1), ALU.max, ALU.min)
            ts(keyr[:, :], keyr[:, :], 0.0, float(ADAPT - 1), ALU.max, ALU.min)
            stt(keyc[:, :], idc[:, :], float(NB), cst[0:NB, C_PCOL:C_PCOL + 1], ALU.mult, ALU.add)
            stt(keyr[:, :], keyr[:, :], float(NB), cst[0:NB, C_IOTA:C_IOTA + NB], ALU.mult, ALU.add)
            link(V.tensor_scalar(below[:, :], keyr[:, :], keyc[:, 0:1], None, ALU.is_lt))
            link(V.reduce_sum(rank[:, :], below[:, :], AX.X))
            link(V.tensor_scalar(oneh[:, 0:NB], cst[0:NB, C_IOTA:C_IOTA + NB], rank[:, 0:1], None, ALU.is_equal))
            V.tensor_scalar(oneh[:, NB:], cst[0:NB, C_IOTA:C_IOTA + ADAPT + 1], idc[:, 0:1], None, ALU.is_gt
                            ).then_inc(s["d_oneh"], 1)

            dve.wait_ge(s["l_s4"], 160)
            sl_ = [sm[:, i, :] for i in range(32)]
            ldt, lar, aim, cre, cim = sl_[0:5]

            def expm1(x, y, one, w):
                k, r, p, sc_ = w
                ts(k, x, LOG2E, ROUND, ALU.mult, ALU.add)
                ts(k, k, ROUND, -126.0, ALU.subtract, ALU.max)
                stt(r, k, -LN2_HI, x, ALU.mult, ALU.add)
                stt(r, k, -LN2_LO, r, ALU.mult, ALU.add)
                ts(p, r, 1.0 / 40320, None, ALU.mult, ALU.bypass)
                for c in (1.0 / 5040, 1.0 / 720, 1.0 / 120, 1.0 / 24, 1.0 / 6, 0.5, 1.0):
                    stt(p, p, c, r, ALU.add, ALU.mult)
                ts(sc_.bitcast(i32), k, 127.0, float(2 ** 23), ALU.add, ALU.mult)
                tt(p, p, sc_, ALU.mult)
                if one:
                    ts(sc_, sc_, -1.0, None, ALU.add, ALU.bypass)
                tt(y, p, sc_, ALU.add)

            two = sm[:, 0:2, :]
            expm1(two, sm[:, 6:8, :], False, [sm[:, 8 + 2 * i:10 + 2 * i, :] for i in range(4)])
            dt_, are = sl_[6], sl_[7]
            ts(are, are, -1.0, None, ALU.mult, ALU.bypass)
            a_, b_ = sl_[16], sl_[17]
            tt(a_, are, dt_, ALU.mult)
            tt(b_, aim, dt_, ALU.mult)
            mul = cst[:, C_MUL:C_MUL + CMULT].unsqueeze(1).to_broadcast([P, S, CMULT])
            ph = cst[:, C_PH:C_PH + CMULT].unsqueeze(1).to_broadcast([P, S, CMULT])
            V.tensor_tensor(dec, a_.unsqueeze(2).to_broadcast([P, S, CMULT]), mul, ALU.mult).then_inc(s["d_ang"], 1)
            tt(ang, b_.unsqueeze(2).to_broadcast([P, S, CMULT]), mul, ALU.mult)
            link(V.tensor_tensor(turn, ang, ph, ALU.add))
            ts(turn, turn, float(1 / TWO_PI), ROUND, ALU.mult, ALU.add)
            ts(turn, turn, ROUND, None, ALU.subtract, ALU.bypass)
            for c in (PI_A, PI_B, PI_C):
                stt(ang, turn, -c, ang, ALU.mult, ALU.add)
            tt(ang, ang, ph, ALU.add)
            V.tensor_scalar(ang, ang, float(np.float32(-3.1415925)), float(np.float32(3.1415925)), ALU.max, ALU.min
                            ).then_inc(s["d_ang"], 1)
            expm1(a_, sl_[18], True, [sl_[19], sl_[20], sl_[21], sl_[22]])
            em1 = sl_[18]
            dve.wait_ge(s["l_w0"], 32)
            link(V.tensor_copy(h16a, w0u))
            link(V.tensor_scalar(h16b, h16a, 0x7F, 7, ALU.bitwise_and, ALU.logical_shift_left))
            link(V.tensor_scalar(h16a, h16a, 0x80, 8, ALU.bitwise_and, ALU.logical_shift_left))
            link(V.tensor_tensor(h16a, h16a, h16b, ALU.bitwise_or))
            V.tensor_scalar(w0, h16a.bitcast(f16), 256.0, None, ALU.mult).then_inc(s["d_w0"], 1)
            dve.wait_ge(s["a_ang"], 2)
            o0 = LC + 2 * LA
            cb, sb_, hb = ang[:, :, o0], ang[:, :, o0 + 1], ang[:, :, o0 + 2]
            t1, t2, zr, zi, dn, rr, ri, yr, yi, cr, ci = sl_[19:30]
            tt(t1, em1, cb, ALU.mult)
            stt(t2, hb, -2.0, hb, ALU.mult, ALU.mult)
            tt(zr, t1, t2, ALU.add)
            stt(zi, em1, 1.0, sb_, ALU.add, ALU.mult)
            tt(t1, are, are, ALU.mult)
            tt(t2, aim, aim, ALU.mult)
            tt(dn, t1, t2, ALU.add)
            link(V.reciprocal(dn, dn))
            tt(rr, are, dn, ALU.mult)
            stt(ri, aim, -1.0, dn, ALU.mult, ALU.mult)

            def cmul(xr, xi, ar, ai, br, bi):
                tt(t1, ar, br, ALU.mult)
                tt(t2, ai, bi, ALU.mult)
                tt(xr, t1, t2, ALU.subtract)
                tt(t1, ar, bi, ALU.mult)
                tt(t2, ai, br, ALU.mult)
                tt(xi, t1, t2, ALU.add)

            cmul(yr, yi, cre, cim, zr, zi)
            cmul(cr, ci, yr, yi, rr, ri)
            al, be = sl_[30], sl_[31]
            lo, hi = slice(0, MODES), slice(MODES, P)
            ts(al[lo], cr[lo], 2.0, None, ALU.mult, ALU.bypass)
            ts(al[hi], ci[hi], -2.0, None, ALU.mult, ALU.bypass)
            ts(be[lo], ci[lo], -2.0, None, ALU.mult, ALU.bypass)
            ts(be[hi], cr[hi], -2.0, None, ALU.mult, ALU.bypass)
            tt(turn, ang, dec, ALU.mult)
            tt(pc, turn[:, :, LC:LC + LA], al.unsqueeze(2).to_broadcast([P, S, LA]), ALU.mult)
            tt(pq, turn[:, :, LC + LA:LC + 2 * LA], be.unsqueeze(2).to_broadcast([P, S, LA]), ALU.mult)
            V.tensor_tensor(pc, pc, pq, ALU.add).then_inc(s["d_pp"], 1)
            link(V.memset(zpad, 0.0))
            dve.wait_ge(s["p_ord"], 1)
            link(V.tensor_copy(order[:, 0:NB], ps[0:1, 5, 0:NB]))
            n_, m_, w_, e_ = (cnt[:, i, :] for i in range(4))
            link(V.tensor_copy(gord[:, 0:ADAPT + 1], ps[0:1, 5, NB:NB + ADAPT + 1]))
            tt(n_, gord[:, 1:ADAPT + 1], gord[:, 0:ADAPT], ALU.subtract)
            link(V.tensor_scalar(m_, n_, 0.0, None, ALU.is_gt))
            for k in range(GB, NB, GB):
                stt(m_, n_, float(k), m_, ALU.is_gt, ALU.add)
            link(V.memset(gord[:, 0:1], 0.0))
            link(V.tensor_copy(gord[:, 1:ADAPT + 1], m_))
            step = 1
            while step < ADAPT:
                link(V.tensor_copy(w_, gord[:, 1:ADAPT + 1]))
                tt(gord[:, 1 + step:ADAPT + 1], w_[:, step:], w_[:, 0:ADAPT - step], ALU.add)
                step *= 2
            giota = cst[0:1, C_IOTA:C_IOTA + NGR]
            tt(gmat[:, :, :], giota.unsqueeze(2).to_broadcast([1, NGR, ADAPT]),
               gord[:, 1:ADAPT + 1].unsqueeze(1).to_broadcast([1, NGR, ADAPT]), ALU.is_ge)
            stt(e_, m_, -float(GB), n_, ALU.mult, ALU.add)
            tt(gmat[:, :, :], gmat[:, :, :], cnt[:, 3:4, :].to_broadcast([1, NGR, ADAPT]), ALU.mult)
            link(V.tensor_reduce(gord[:, ADAPT + 1:], gmat[:, :, :], AX.X, ALU.add))
            stt(gord[:, ADAPT + 1:], giota, float(GB), gord[:, ADAPT + 1:], ALU.mult, ALU.add)
            V.tensor_copy(order[:, NB:], gord[:, :]).then_inc(s["d_ord"], 1)
            dve.wait_ge(s["p_k"], 1)
            link(V.tensor_copy(ksb, ps[0:LA, 6:8, :].rearrange("p a (h c) -> p (a h) c", c=LC)))
            V.tensor_tensor(ksb[0:1, :, 0], ksb[0:1, :, 0], sm[0:1, 5, :], ALU.add).then_inc(s["d_k"], 1)

            def start_unit(u):
                h, w = unit_shape(u)
                nb = w // BLK
                dve.wait_ge(s[f"l_raw{u % 2}"], 32 * (u // 2 + 1))
                r = raw[0:h, u % 2, 0:w].rearrange("p (n k) -> p n k", k=BLK)
                am_ = amax[0:h, u % 2, 0:nb]
                link(V.tensor_reduce(am_, r, AX.X, ALU.max, apply_absolute_value=True))
                link(V.tensor_scalar(rmax[0:h, 0:nb], am_, 0.0, None, ALU.is_equal))
                tt(rmax[0:h, 0:nb], rmax[0:h, 0:nb], am_, ALU.add)
                link(V.reciprocal(rmax[0:h, 0:nb], rmax[0:h, 0:nb]))
                V.tensor_tensor(r, r, rmax[0:h, 0:nb].unsqueeze(2).to_broadcast([h, nb, BLK]), ALU.mult
                                ).then_inc(s["d_nrm"], 1)
                dve.wait_ge(s["d_nrm"], u + 1)

            def levels(k):
                u = k // 3
                h, w = unit_shape(u)
                ac = acc_of(u)[0:h, 0:w]
                if k % 3 == 0 and u:
                    dve.wait_ge(s["p_qt"], banks_before(u))
                if k % 3 == 1 and u + 1 < NU:
                    start_unit(u + 1)
                for i in range(LV * (k % 3), LV * (k % 3 + 1)):
                    m = 15 * u + i
                    dve.wait_ge(s["m_ready"], m + 1)
                    src = above[0:h, m % 2, 0:w]
                    if i == 0:
                        V.tensor_scalar(ac, src, float(STEPS[0]), float(NF4[0]), ALU.min, ALU.add
                                        ).then_inc(s["m_used"], 1)
                    else:
                        V.scalar_tensor_tensor(out=ac, in0=src, scalar=float(STEPS[i]), in1=ac,
                                               op0=ALU.min, op1=ALU.add).then_inc(s["m_used"], 1)
                    dve.wait_ge(s["m_used"], m + 1)
                if k % 3 == 2:
                    nb = w // BLK
                    acb = ac.rearrange("p (n k) -> p n k", k=BLK)
                    V.tensor_tensor(acb, acb, amax[0:h, u % 2, 0:nb].unsqueeze(2).to_broadcast([h, nb, BLK]), ALU.mult
                                    ).then_inc(s["d_dq"], 1)
                    dve.wait_ge(s["d_dq"], u + 1)

            def conv_out(g):
                dve.wait_ge(s["p_conv"], g + 1)
                V.tensor_tensor(Y.rearrange("p c (b s) -> p c s b", s=S)[:, :, g * GH:(g + 1) * GH, :],
                                ps[:, g % 4, :].rearrange("p (c k b) -> p c k b", c=DC, k=GH),
                                mnat[:, :, :].unsqueeze(2).to_broadcast([P, DC, GH, NB]), ALU.mult
                                ).then_inc(s["d_conv"], 1)

            k = 0
            start_unit(0)
            for g in range(HG):
                if g % 4 < 3:
                    levels(k)
                    k += 1
                conv_out(g)
            dve.wait_ge(s["l_x"], 16)
            for n in range(TB * DC):
                tb, oc = n // DC, n % DC
                if oc == 0 and tb < 3:
                    levels(k)
                    k += 1
                dve.wait_ge(s["p_ffn0"], n + 1)
                V.scalar_tensor_tensor(out=X[:, oc, tok(tb)], in0=ps[:, 4 + n % 2, :], scalar=wsc[:, 0:1],
                                       in1=X[:, oc, tok(tb)], op0=ALU.mult, op1=ALU.add).then_inc(s["d_x1"], 1)
            dve.wait_ge(s["d_conv"], HG)
            for c in range(DC):
                link(V.tensor_scalar(mnat[:, c, :], lenf[:, 1, :], cst[:, C_L + c:C_L + c + 1], None, ALU.is_gt))
            for a in range(ADAPT):
                if a < 15:
                    levels(k)
                    k += 1
            dve.wait_ge(s["l_sml"], NSML)
            link(V.tensor_copy(lan[:, :], lan_i[:, :]))
            tt(lbias[:, :, :], cst[:, C_IOTA:C_IOTA + E].unsqueeze(1).to_broadcast([P, TT, E]),
               lan[:, :].unsqueeze(2).to_broadcast([P, TT, E]), ALU.is_equal)
            ts(lbias[:, :, :], lbias[:, :, :], 5.0, None, ALU.mult, ALU.bypass)
            link(V.tensor_copy(ilen[:, 0:1], lc_i[:, :]))
            link(V.reciprocal(ilen[:, 1:2], ilen[:, 0:1]))
            def hidden(n):
                h = HCH[n % NH]
                dve.wait_ge(s["a_silu"], n + 1)
                if n >= NH:
                    dve.wait_ge(s["p_down"], n - NH + 1)
                V.tensor_tensor(hs[0:h, n % NH, :], sg[n % 2][0:h, :], ps[0:h, 2 + n % 2, :], ALU.mult
                                ).then_inc(s["d_h"], 1)

            for n in range(NH):
                levels(k)
                k += 1
                hidden(n)
            while k < PARTS:
                levels(k)
                k += 1
            for n in range(TB * NH):
                if n + NH < TB * NH:
                    hidden(n + NH)
                if n % NH == NH - 1:
                    tb = n // NH
                    dve.wait_ge(s["p_down"], n + 1)
                    with dve.Fori(0, TW // S) as t:
                        b = dve.value_load(order[0:1, bass.ds(t + tb * (TW // S), 1)], min_val=0, max_val=NB - 1)
                        dve.tensor_tensor(X[:, :, bass.ds(b * S, S)], X[:, :, bass.ds(b * S, S)],
                                          ps[:, 4:8, bass.ds(t * S, S)], ALU.add).then_inc(s["d_x2"], 1)
            dve.wait_ge(s["p_down"], TB * NH)
            for i in range(SENT):
                link(V.memset(repl[:, :, 2 + i:3 + i], -1e30 * (i + 1)))
                link(V.memset(vals[:, :, E + i:E + i + 1], -1e30 * (i + 1)))
            link(V.memset(rqT[:, :], 1.0))
            link(V.memset(qT[BOT:BOT + 1, :], 1.0))
            dve.wait_ge(s["l_l3w"], 16)
            link(V.tensor_copy(w16[:, :, 0:E], l3w[:, :, 0:E]))
            dve.wait_ge(s["p_prep"], 1)
            V.tensor_scalar(akT[0:BOT, :], akT[0:BOT, :], float(BOT ** -0.5), None, ALU.mult).then_inc(s["prep_done"], 1)
            for tb in range(TB):
                dve.wait_ge(s["p_lg"], tb + 1)
                tt(vals[:, :, 0:E], ps[:, 1, 0:NT * E].rearrange("p (t e) -> p t e", e=E),
                   lbias[:, tb * NT:(tb + 1) * NT, :], ALU.add)
                for t in range(NT):
                    link(V.max(top[:, t, :], vals[:, t, 0:E]))
                link(V.tensor_copy(repl[:, :, 0:2], top[:, :, 0:2]))
                V.tensor_tensor(ge, vals[:, :, 0:E], top[:, :, 0:1].to_broadcast([P, NT, E]), ALU.subtract
                                ).then_inc(s["d_gl"], 1)
                for t in range(NT):
                    link(V.match_replace(vrep[:, t, 0:E + SENT], repl[:, t, :], vals[:, t, 0:E + SENT], -3e38))
                ts(gs, vrep[:, :, 0:E], -2e38, None, ALU.is_lt, ALU.bypass)
                dve.wait_ge(s["a_ge"], tb + 1)
                tt(gs, gs, ge, ALU.mult)
                link(V.tensor_reduce(z4[:, 0, :], gs, AX.X, ALU.add))
                link(V.reciprocal(z4[:, 1, :], z4[:, 0, :]))
                ts(z4[:, 2, :], z4[:, 1, :], 2.0, None, ALU.mult, ALU.bypass)
                tt(gs, gs, z4[:, 2, :].unsqueeze(2).to_broadcast([P, NT, E]), ALU.mult)
                V.tensor_copy(gt.rearrange("p t (e r) -> p t e r", e=E), gs.unsqueeze(3).to_broadcast([P, NT, E, R])
                              ).then_inc(s["d_gate"], 1)
                dve.wait_ge(s["a_ha"], tb + 1)
                dve.wait_ge(s["p_gx"], tb + 1)
                if tb:
                    dve.wait_ge(s["p_c2"], tb)
                V.tensor_tensor(hgx, ha, ps[:, 2, :], ALU.mult).then_inc(s["d_hg"], 1)
                for t in range(NT):
                    dve.wait_ge(s["p_tr"], tb * NT + t + 1)
                    V.bn_stats(bst[:, t, 0:6], ps[:, 3 - t % 2, :]).then_inc(s["d_st"], 1)
                dve.wait_ge(s["d_st"], tb * NT + NT)
                for t in range(NT):
                    link(V.bn_aggr(var[:, tb * NT + t, :], bst[:, t, 0:6]))
                dve.wait_ge(s["p_sc"], tb + 1)
                if tb:
                    dve.wait_ge(s["a_pr"], NT * tb)
                for t in range(NT):
                    sl8 = ps[:, 6, t * NSLOT:(t + 1) * NSLOT]
                    link(V.max(top8[:, t, :], sl8))
                    link(V.match_replace(sc[:, t, :], top8[:, t, :], sl8, -3e38))
                ts(am, sc, -2e38, -1e30, ALU.is_gt, ALU.mult)
                tt(am, am, ps[:, 7, :].rearrange("p (t k) -> p t k", t=NT), ALU.add)
                V.tensor_reduce(nmx, am, AX.X, ALU.max, negate=True).then_inc(s["d_am"], 1)
                dve.wait_ge(s["d_am"], tb + 1)
            V.tensor_copy(lvs[:, 1:2], ones[:, 0:1]).then_inc(s["d_st"], 1)
            dve.wait_ge(s["d_st"], TT + 1)
            dve.wait_ge(s["p_lv"], 1)
            dve.wait_ge(s["a_sg"], 1)
            ts(lvs[:, 1:2], ps[:, 0, 0:1], 1.0 / TOK, 1e-6, ALU.mult, ALU.add)
            link(V.reciprocal(lvs[:, 1:2], lvs[:, 1:2]))
            ts(gq[:, 1, :], lv[:, :], lvs[:, 1:2], None, ALU.mult, ALU.bypass)
            ts(gq[:, 1, :], gq[:, 1, :], 0.5, None, ALU.mult, ALU.bypass)
            stt(gq[:, 1, :], gq[:, 0, :], 2.5, gq[:, 1, :], ALU.mult, ALU.add)
            ts(gq[:, 1, :], gq[:, 1, :], 0.0, 5.0, ALU.max, ALU.min)
            ts(gq[:, 1, :], gq[:, 1, :], 0.5, 1.0 / 1.5, ALU.subtract, ALU.mult)
            V.tensor_scalar(gq[:, 1, :], gq[:, 1, :], 0.0, 1.0, ALU.max, ALU.min).then_inc(s["d_un"], 1)
            dve.wait_ge(s["a_pr"], TT)
            link(V.reciprocal(gq[:, 3, :], den[:, :]))
            dve.wait_ge(s["a_gt"], 1)
            stt(gq[:, 4, :], gq[:, 2, :], 0.05, gq[:, 2, :], ALU.is_ge, ALU.mult)
            tt(gq[:, 4, :], gq[:, 4, :], gq[:, 3, :], ALU.mult)
            V.tensor_tensor(PR, PR, gq[:, 4, :].unsqueeze(2).to_broadcast([P, TT, NSLOT]), ALU.mult).then_inc(s["d_pn"], 1)
            for tb in range(TB):
                dve.wait_ge(s["p_aux"], tb + 1)
                dve.wait_ge(s["g_xc"], tb + 1)
                V.tensor_tensor(X[:, :, tok(tb)], X[:, :, tok(tb)], ps[:, 4:8, :], ALU.add).then_inc(s["d_x3"], 1)
            dve.wait_ge(s["l_diag"], 16)
            link(V.memset(ysm[:, :, :], 0.0))
            for tb in range(TB):
                dve.wait_ge(s["p_y"], tb + 1)
                dg = diag[:, tok(tb)]
                tt(yd, ps[0:NB, 2, :], dg, ALU.mult)
                link(V.tensor_reduce(ysm[:, 0, 2:2 + S], yd.rearrange("p (b s) -> p s b", s=S), AX.X, ALU.add))
                link(V.tensor_scalar(ysm[:, 0, 2:2 + S], ysm[:, 0, 2:2 + S], ilen[:, 1:2], None, ALU.mult))
                link(V.tensor_scalar(ysm[:, 1, 0:S], ysm[:, 0, 0:S], cw[:, 0:1], None, ALU.mult))
                for k in range(1, 4):
                    stt(ysm[:, 1, 0:S], ysm[:, 0, k:k + S], cw[:, k:k + 1], ysm[:, 1, 0:S], ALU.mult, ALU.add)
                V.scalar_tensor_tensor(out=ysm[:, 1, 0:S], in0=ysm[:, 0, 4:4 + S], scalar=cw[:, 4:5], in1=ysm[:, 1, 0:S],
                                       op0=ALU.mult, op1=ALU.add).then_inc(s["d_ys"], 1)
                dve.wait_ge(s["a_yg"], tb + 1)
                V.tensor_tensor(gex.rearrange("p (b s) -> p b s", s=S), dg.rearrange("p (b s) -> p b s", s=S),
                                ysm[:, 2:3, 0:S].to_broadcast([NB, TW // S, S]), ALU.mult).then_inc(s["d_gex"], 1)
                dve.wait_ge(s["p_gb"], tb + 1)
                V.tensor_tensor(Y[:, :, tok(tb)], X[:, :, tok(tb)], ps[:, 3:4, :].to_broadcast([P, DC, TW]), ALU.mult
                                ).then_inc(s["d_c3"], 1)
                dve.wait_ge(s["p_sl"], tb + 1)
                src = ps[:, 1, 0:4 * E].rearrange("p (t k) -> p t k", t=2)
                link(V.tensor_copy(sl[:, 2 * tb:2 * tb + 2, E:2 * E], src[:, :, E:2 * E]))
                tt(sl[:, 2 * tb:2 * tb + 2, 0:E], src[:, :, 0:E], b8[:, :].unsqueeze(1).to_broadcast([P, 2, E]), ALU.add)
            for k in range(2):
                v = sl[:, :, k * E:(k + 1) * E]
                link(V.tensor_reduce(mx4[:, k:k + 1], v, AX.XY, ALU.max))
                link(V.tensor_reduce(mx4[:, 2 + k:3 + k], v, AX.XY, ALU.min))
            V.tensor_copy(gm2, mx4).then_inc(s["d_mx"], 1)
            dve.wait_ge(s["g_mx"], 1)
            tt(gm2[:, 0:2], gm4[:, 0:2], gm4[:, 2:4], ALU.max)
            ts(gm2[:, 0:2], gm2[:, 0:2], 1e-6, None, ALU.max, ALU.bypass)
            link(V.reciprocal(gm2[:, 0:2], gm2[:, 0:2]))
            ts(gm2[:, 0:2], gm2[:, 0:2], 0.5, None, ALU.mult, ALU.bypass)
            link(V.tensor_scalar(lg3, sl[:, :, 0:E], gm2[:, 0:1], None, ALU.mult))
            stt(lg3, sl[:, :, E:2 * E], gm2[:, 1:2], lg3, ALU.mult, ALU.add)
            link(V.tensor_reduce(ss3[:, 0, :], lg3, AX.X, ALU.max))
            V.tensor_tensor(lg3, lg3, ss3[:, 0, :].unsqueeze(2).to_broadcast([P, 8, E]), ALU.subtract
                            ).then_inc(s["d_lg3"], 1)
            dve.wait_ge(s["a_e3"], 1)
            link(V.tensor_reduce(ss3[:, 1, :], pr3, AX.X, ALU.add))
            link(V.reciprocal(ss3[:, 2, :], ss3[:, 1, :]))
            tt(pr3, pr3, ss3[:, 2, :].unsqueeze(2).to_broadcast([P, 8, E]), ALU.mult)
            for t in range(8):
                link(V.max(tp3[:, t, :], pr3[:, t, :]))
            V.tensor_tensor(mk3, pr3, tp3[:, :, 1:2].to_broadcast([P, 8, E]), ALU.subtract).then_inc(s["d_th"], 1)
            dve.wait_ge(s["a_mk"], 1)
            tt(tm3, pr3, mk3, ALU.mult)
            link(V.tensor_reduce(ss3[:, 3, :], tm3, AX.X, ALU.add))
            ts(ss3[:, 3, :], ss3[:, 3, :], 1e-9, None, ALU.add, ALU.bypass)
            link(V.reciprocal(ss3[:, 4, :], ss3[:, 3, :]))
            V.tensor_tensor(tm3, tm3, ss3[:, 4, :].unsqueeze(2).to_broadcast([P, 8, E]), ALU.mult).then_inc(s["d_w3"], 1)
            for tb in range(TB):
                dve.wait_ge(s["p_pm"], tb + 1)
                if tb:
                    dve.wait_ge(s["p_o"], tb * DC)
                V.scalar_tensor_tensor(out=zp, in0=ps[0:RANK, tb % 2, :], scalar=0.5, in1=zt[:, tok(tb)],
                                       op0=ALU.mult, op1=ALU.mult).then_inc(s["d_zp"], 1)
                for oc in range(DC):
                    n = tb * DC + oc
                    dve.wait_ge(s["p_o"], n + 1)
                    if n >= 4:
                        dve.wait_ge(s[f"l_out{n % 4}"], 16 * (n // 4))
                    V.scalar_tensor_tensor(out=oT[n % 4], in0=ps[:, 4 + oc, :], scalar=b3[:, oc:oc + 1],
                                           in1=X[:, oc, tok(tb)], op0=ALU.add, op1=ALU.add).then_inc(s["d_o"], 1)


def kernel(**inputs):
    import numpy as _np
    import concourse.bacc as _bacc
    from concourse import mybir as _mybir
    from concourse.bass_utils import run_bass_kernel_spmd as _run

    g = {k: _np.asarray(v) for k, v in inputs.items()}
    x = g["x"]
    const, diag = constants()
    lay = {
        "const": const, "diag": diag,
        "xconv": x.transpose(2, 1, 0).reshape(DC, P, S * NB)[:, ::-1],
        "xT": x.reshape(TOK, D).T,
        "log_A_real": g["L0_cond_log_A_real"].T, "A_imag": g["L0_cond_A_imag"].T,
        "C_re": g["L0_cond_C"][..., 0].T, "C_im": g["L0_cond_C"][..., 1].T,
        "log_dt": g["L0_cond_log_dt"], "Dskip": g["L0_cond_D"],
        "len0": g["itok_B_8_3872"], "len3": g["itok_B_9_3973"], "ids": g["itok_B_1_14"], "lang": g["itok_B_0_7"].reshape(TT, 4).T,
        "w0": g["L0_ffn_weight_fp8"].T, "w0scale": g["L0_ffn_weight_scale"],
        "wa": g["L1_cond_weight"].transpose(0, 2, 1),
        "w1": g["L1_ffn_w1"], "w2": g["L1_ffn_w2"], "w3": g["L1_ffn_w3"].reshape(D // 2, 2 * HID),
        "l2w": g["L2_cond_W"].T, "wr": g["L2_cond_Wr"].T, "l2a": g["L2_cond_A"].reshape(E * R, D).T,
        "l2b": g["L2_cond_B"].transpose(0, 2, 1).reshape(E * R, D),
        "wq": g["L2_ffn_Wq"].T, "wrq": g["L2_ffn_Wr"].T, "akT": g["L2_ffn_aux_keys"].T,
        "avT": g["L2_ffn_aux_values"].T, "wvd": g["L2_ffn_Wvd"].T, "wvu": g["L2_ffn_Wvu"].T,
        "wu1": g["L2_ffn_Wu1"].T, "bu1": g["L2_ffn_bu1"], "wu2": g["L2_ffn_Wu2"].T, "bu2": g["L2_ffn_bu2"],
        "gate_w1": g["L2_ffn_gate_w1"].reshape(1), "gate_bias": g["L2_ffn_gate_bias"].reshape(1),
        "log_rel": g["L2_ffn_log_rel"],
        "conv_w": g["L3_cond_conv_w"].reshape(5),
        "l3w": g["L3_ffn_W"].T, "b3": g["L3_ffn_b"].reshape(DC, P).T, "b3row": g["L3_ffn_b"],
        "l3a": g["L3_ffn_A"], "l3aT": g["L3_ffn_A"].T, "bmat": g["L3_ffn_Bmat"],
        "lim": g["L3_ffn_LiMEs"], "limT": g["L3_ffn_LiMEs"].T,
    }
    nc = _bacc.Bacc("TRN2", target_bir_lowering=False, num_devices=1)
    arrays, A = {}, {}
    for name, a in lay.items():
        a = _np.ascontiguousarray(a)
        arrays[f"in_{name}"] = a
        A[name] = nc.dram_tensor(f"in_{name}", a.shape, _mybir.dt.from_np(a.dtype), kind="ExternalInput").ap()
    out = nc.dram_tensor("out_T", (D, TOK), f32, kind="ExternalOutput").ap()
    build(nc, A, out)
    r = _run(nc, [arrays], core_ids=[0])
    return _np.ascontiguousarray(r.results[0]["out_T"].T).reshape(NB, S, D)
```

```python
import numpy as np

import concourse.bass as bass
from concourse import mybir
from contextlib import ExitStack

f32 = mybir.dt.float32
f16 = mybir.dt.float16
bf16 = mybir.dt.bfloat16
i32 = mybir.dt.int32
u8 = mybir.dt.uint8
u16 = mybir.dt.uint16
ALU = mybir.AluOpType
ACT = mybir.ActivationFunctionType
AX = mybir.AxisListType

P = 128
NB, S, D = 64, 32, 512
TOK = NB * S
DC = D // P
TB = 4
TW = TOK // TB
NT = TW // P
TT = TOK // P
MODES = 64
LA, LC = 16, 32
PAD = P
KROW = PAD + D
GH = 2
HG = S // GH
ADAPT = 16
GB = 8
NGR = (NB + ADAPT * (GB - 1)) // GB
HID = 1376
HCH = [min(P, HID - P * c) for c in range((HID + P - 1) // P)]
NH = len(HCH)
E, R = 8, 16
BOT, RDIM, NSLOT, VB = 64, 48, 128, 32
RANK = 32
BLK = 64
HALF = 1408
SENT = 6
CMULT = 67
ANCH = TOK // 2

NF4 = np.array([-1.0, -0.6961928009986877, -0.5250730514526367, -0.39491748809814453, -0.28444138169288635,
                -0.18477343022823334, -0.09105003625154495, 0.0, 0.07958029955625534, 0.16093020141124725,
                0.24611230194568634, 0.33791524171829224, 0.44070982933044434, 0.5626170039176941,
                0.7229568362236023, 1.0], np.float32)
BOUNDS = ((NF4[:-1] + NF4[1:]) * np.float32(0.5)).astype(np.float32)
STEPS = (NF4[1:] - NF4[:-1]).astype(np.float32)

STEEP = 2.0 ** 40
ROUND = float(1.5 * 2 ** 23)
LOG2E = float(np.log2(np.e))
LN2_HI = float(np.float32(0.693359375))
LN2_LO = float(np.log(2.0) - 0.693359375)
TWO_PI = 2 * np.pi
PI_A = float(np.float32(6.28125))
PI_B = float(np.float32(np.round((TWO_PI - 6.28125) * 2 ** 21) / 2 ** 21))
PI_C = float(np.float32(TWO_PI - 6.28125 - PI_B))

C_ID = 0
C_MUL = C_ID + P
C_PH = C_MUL + CMULT
C_IOTA = C_PH + CMULT
C_L = C_IOTA + P
C_LREV = C_L + DC
C_PCOL = C_LREV + DC
C_BND = C_PCOL + 1
C_COLS = C_BND + len(BOUNDS)


def constants():
    c = np.zeros((P, C_COLS), np.float32)
    c[:, C_ID:C_ID + P] = np.eye(P)
    mul = np.concatenate([np.arange(LC), LC * np.arange(LA), LC * np.arange(LA), [1, 1, 0.5]])
    c[:, C_MUL:C_MUL + CMULT] = mul
    ph = np.zeros((P, CMULT))
    ph[:MODES, :LC] = np.pi / 2
    ph[:, LC:LC + LA] = np.pi / 2
    ph[:, LC + 2 * LA] = np.pi / 2
    c[:, C_PH:C_PH + CMULT] = ph
    c[:, C_IOTA:C_IOTA + P] = np.arange(P)
    p = np.arange(P)[:, None]
    c[:, C_L:C_L + DC] = np.arange(DC) * P + p
    c[:, C_LREV:C_LREV + DC] = np.arange(DC) * P + (P - 1 - p)
    c[:, C_PCOL] = np.arange(P)
    c[:, C_BND:] = -BOUNDS * np.float32(STEEP)
    diag = (np.arange(NB)[:, None] == (np.arange(TOK) // S)[None, :]).astype(np.float32)
    return c, diag


def build(nc, A, out):
    ctx = ExitStack()
    with ctx:
        def sb(name, shape, dt=f32):
            return ctx.enter_context(nc.sbuf_tensor(name, shape, dt))

        ps = ctx.enter_context(nc.psum_tensor("ps", [P, 8, 512], f32))
        kpad = nc.dram_tensor("kpad", [S, KROW], f32, kind="Internal")

        X = sb("X", [P, DC, TOK])
        Yp = sb("Yp", [P, DC * TOK + GB * S])
        Up = sb("Up", [P, DC, TOK + (GB - 1) * S])
        yf = Yp[:, 0:DC * TOK]
        Y = yf.rearrange("p (c n) -> p c n", c=DC)
        uf = Up[:, :, :].rearrange("p c n -> p (c n)")
        uc = uf[:, 0:DC * TOK].rearrange("p (c n) -> p c n", c=DC)
        T = sb("T", [P, 2, GH, D])
        tf = T[:, :, :, :].rearrange("p a b c -> p (a b c)")
        W1T = sb("W1T", [P, DC, HID])
        W2T = sb("W2T", [P, DC, HID])
        W3T = sb("W3T", [P, NH, D])
        w1f = W1T[:, :, :].rearrange("p a b -> p (a b)")
        w2f = W2T[:, :, :].rearrange("p a b -> p (a b)")
        w3f = W3T[:, :, :].rearrange("p a b -> p (a b)")
        cst = sb("cst", [P, C_COLS])
        ident = cst[:, C_ID:C_ID + P]
        ones = sb("ones", [P, P])

        raw = sb("raw", [P, 2, HALF])
        acc = sb("acc", [P, HALF])
        xtail = X[:, DC - 1, TOK - HALF:]
        above = sb("above", [P, 2, HALF], bf16)
        amax = sb("amax", [P, 2, HALF // BLK])
        rmax = sb("rmax", [P, HALF // BLK])
        mrev = sb("mrev", [P, DC, NB])
        lstep = mrev[:, :, :].rearrange("p c b -> p (c b)")

        ang = w1f[:, 0:S * CMULT].rearrange("p (h m) -> p h m", h=S)
        dec = w1f[:, S * CMULT:2 * S * CMULT].rearrange("p (h m) -> p h m", h=S)
        turn = w2f[:, 0:S * CMULT].rearrange("p (h m) -> p h m", h=S)
        n0 = S * CMULT
        pc = w2f[:, n0:n0 + S * LA].rearrange("p (h m) -> p h m", h=S)
        pq = w2f[:, n0 + S * LA:n0 + 2 * S * LA].rearrange("p (h m) -> p h m", h=S)
        n0 += 2 * S * LA
        ksb = w2f[0:LA, n0:n0 + S * LC].rearrange("p (h m) -> p h m", h=S)
        n0 += S * LC
        sm = w2f[:, n0:n0 + 32 * S].rearrange("p (k h) -> p k h", h=S)
        zpad = w3f[0:S, 5120:5120 + PAD]
        w0u = w1f[:, 4992:5504].bitcast(u8).rearrange("p (c o) -> p c o", c=DC)
        w0 = w3f[:, 0:2048].rearrange("p (c o) -> p c o", c=DC)
        h16a = acc[:, 0:1024].bitcast(u16).rearrange("p (c o) -> p c o", c=DC)
        h16b = raw[:, 1, 0:1024].bitcast(u16).rearrange("p (c o) -> p c o", c=DC)
        wsc = sb("wsc", [P, 1])
        leni = sb("leni", [P, 2, NB], i32)
        lenf = sb("lenf", [P, 2, NB])
        mnat = sb("mnat", [P, DC, NB])

        idc_i = sb("idc_i", [NB, 1], i32)
        idr_i = sb("idr_i", [NB, NB], i32)
        idc = sb("idc", [NB, 1])
        keyc = sb("keyc", [NB, 1])
        keyr = sb("keyr", [NB, NB])
        below = sb("below", [NB, NB])
        rank = sb("rank", [NB, 1])
        oneh = sb("oneh", [NB, NB + ADAPT + 1])
        cnt = sb("cnt", [1, 4, ADAPT])
        gmat = sb("gmat", [1, NGR, ADAPT])
        gord = sb("gord", [1, ADAPT + 1 + NGR])
        order = sb("order", [1, NB + ADAPT + 1 + NGR], i32)
        WS = [w3f[:, o:o + DC * D].rearrange("p (c o) -> p c o", c=DC) for o in (DC * D, 0)]
        gslot = ps[:, 0:4, :].rearrange("p b n -> p (b n)").rearrange("p (s c n) -> p s c n", s=2, c=DC)
        l2w = tf[:, 0:2048].rearrange("p (c o) -> p c o", c=DC)
        rawf = raw[:, :, :].rearrange("p a b -> p (a b)")
        tail = rawf[:, 0:2048]
        l2a = tail[:, 0:512].rearrange("p (c o) -> p c o", c=DC)
        l2u = tail[:, 512:1024].rearrange("p (c o) -> p c o", c=DC)
        l2b = tail[:, 1024:1536]
        l2q = tail[:, 1536:1792].rearrange("p (c o) -> p c o", c=DC)
        wvd = tail[:, 1920:2048].rearrange("p (c o) -> p c o", c=DC)
        avT = acc[:, 0:512].rearrange("p (c o) -> p c o", c=DC)
        wvu = acc[0:VB, 512:1024]
        v1 = acc[0:VB, 1024:1024 + NSLOT]
        l2r = sb("l2r", [P, DC, E])
        rq48 = sb("rq48", [BOT, RDIM])
        akT = sb("akT", [BOT + 1, NSLOT])
        rk = sb("rk", [RDIM + 1, NSLOT])
        bu1 = sb("bu1", [P, 1])
        wu2 = sb("wu2", [P, 1])
        gsc = sb("gsc", [P, 3])
        lan_i = sb("lan_i", [P, TT], i32)
        lan = sb("lan", [P, TT])
        lbias = sb("lbias", [P, TT, E])
        b3 = sb("b3", [P, DC])
        b8 = sb("b8", [P, E])
        lim = sb("lim", [E, RANK])
        limT = sb("limT", [RANK, E])
        cw = sb("cw", [NB, 5])
        lc_i = sb("lc_i", [NB, 1], i32)
        ilen = sb("ilen", [NB, 2])

        hs = yf[:, 0:NH * TW].rearrange("p (n t) -> p n t", n=NH)
        sg = [yf[:, NH * TW + i * TW:NH * TW + (i + 1) * TW] for i in range(2)]

        free = [0]

        def cut(n, parts=P):
            a = free[0]
            free[0] += n
            assert free[0] <= DC * TOK
            return uf[0:parts, a:a + n]

        def tiles(n, k, parts=P):
            return cut(n * k, parts).rearrange("p (t k) -> p t k", t=n)

        ha, hgx, qT, rqT, gu = cut(512), cut(512), cut(512, BOT + 1), cut(512, RDIM + 1), cut(512)
        vals, vrep = tiles(NT, 16), tiles(NT, 16)
        top, repl, ge, gs = (tiles(NT, 8) for _ in range(4))
        gt = tiles(NT, E * R)
        z4 = tiles(3, NT)
        sc, am = tiles(NT, NSLOT), tiles(NT, NSLOT)
        top8 = tiles(NT, 8)
        nmx = cut(NT)
        bst = tiles(NT, 8)
        lgT = cut(TW, E)
        v2, bm, aT = cut(D), cut(D, RANK), cut(D, RANK)
        PR = w1f[:, 0:TT * NSLOT].rearrange("p (t k) -> p t k", t=TT)
        PT = w1f[:, 2048:4096]
        w48 = w1f[:, 5120:5120 + DC * (RANK + 2 * E)].rearrange("p (c k) -> p c k", c=DC)
        w16 = w48[:, :, RANK:]
        ZW = RANK + 2 * E
        zt = w2f[0:RANK + 2 * E, 0:TOK]
        diag = w2f[0:NB, 2048:4096]
        sl, lg3, pr3, mk3, tp3, tm3 = (w2f[:, 4096 + 128 * i:4096 + 128 * i + k * 8].rearrange("p (t k) -> p t k", t=8)
                                       for i, k in enumerate([16, 8, 8, 8, 8, 8]))
        ss3 = w2f[:, 4864:4864 + 8 * 6].rearrange("p (a t) -> p a t", t=8)
        mx4, gm4, gm2 = w2f[:, 4928:4932], w2f[:, 4932:4936], w2f[:, 4936:4940]
        yd = w3f[0:NB, 0:512]
        gex = [w3f[0:NB, 512:1024], w3f[0:NB, 3072:3584], w1f[0:NB, 4096:4608], w1f[0:NB, 4608:5120]]
        ysm = w3f[0:NB, 1024:1024 + 4 * 40].rearrange("p (a b) -> p a b", a=4)
        zp = [w3f[0:RANK, 1536:2048], w3f[0:RANK, 512:1024]]
        wT = w3f[0:E, 2048:3072]
        l3w = w3f[:, 3584:5632].rearrange("p (c o) -> p c o", c=DC)
        var = sb("var", [P, TT, 2])
        lv = sb("lv", [P, TT])
        lvs = sb("lvs", [P, 2])
        lrn = sb("lrn", [P, TT])
        den = sb("den", [P, TT])
        gq = sb("gq", [P, 6, TT])

        s = {}
        for n in """g_u g_xs d_nrm m_ready m_used l_xt g_used g_nrm d_xs p_w16 a_rk a_v2 p_lgt a_lgt l_l3 a_w16 d_w16 d_ak d_rmx g_dq g_step a_fo g_x2 l_cst l_s4 l_w0 l_u l_x l_len l_ids l_kpad l_strip0 l_strip1 l_raw0 l_raw1 l_wa0 l_wa1 l_late l_prep l_l3w
                l_sml l_diag l_out d_b p_b d_sl
                v_step d_ones d_mask d_ang a_ang d_pp p_k d_k d_w0 p_conv d_conv p_ffn0 d_x1
                d_oneh p_ord d_ord p_ad ad_out  d_dq p_qt a_qt p_gu a_silu d_h p_down d_x2
                p_prep a_v1 p_v2 p_lg d_gl a_ge d_gate p_ha a_ha p_gx d_hg p_c2 a_c2 g_xc
                p_tr d_st p_q a_q p_rq a_rq p_gup a_gu p_lr a_lr p_sc d_am a_pr a_lv p_lv a_sg d_un a_gt
                d_pn p_pt a_pt p_aux d_x3 p_y d_ys a_yg d_gex p_gb d_c3 p_z a_z p_sl d_mx g_mx d_lg3 a_e3 d_th a_mk
                d_w3 p_wt a_wt p_pm d_zp p_o d_o""".split():
            s[n] = ctx.enter_context(nc.semaphore(n))
        block = ctx.enter_context(nc.Block())

        UNITS = [(1, c) for c in range(NH)] + [(3, q) for q in range(4)]
        NU = len(UNITS)
        PARTS = 3 * NU
        LV = (len(NF4) - 1) // 3
        assert LV * 3 == len(BOUNDS)
        DP = 4
        BANKS0 = [4, 5, 0, 1, 2, 3]
        QB = np.cumsum([0] + [2 if k == 1 else (NH + 3) // 4 for k, _ in UNITS]).tolist()

        K_CONV = np.cumsum([2 if g in (7, 15) else 1 for g in range(HG)]).tolist()
        K_FFN0 = (K_CONV[-1] + np.cumsum([2, 1, 2, 1])).tolist()
        K_AD = [min(K_FFN0[-1] + a + 1, 39) for a in range(ADAPT)]
        K_UP = [max(39, min(39 + n, PARTS)) for n in range(NH)]
        assert K_UP[-1] == PARTS and K_AD[-1] == 39
        W3_FIRST = NH

        def shared(k):
            return k < K_FFN0[-1] or k >= K_AD[8]

        def split_cols(k):
            w = unit_shape(k // 3)[1]
            return w - w // 8 // 32 * 32 if shared(k) else w

        def pool_norm(u):
            return u > 0 and shared(3 * u - 2)

        def pool_scale(u):
            return shared(3 * u + 2)

        def normed(eng, u):
            if pool_norm(u):
                eng.wait_ge(s["g_nrm"], sum(pool_norm(i) for i in range(u + 1)))
            else:
                eng.wait_ge(s["d_nrm"], sum(not pool_norm(i) for i in range(u + 1)))

        def parts_of(K, i, first=0):
            return range(K[i - 1] if i else first, K[i])

        def units_between(a, b):
            return [u for u in range(NU) if a < 3 * u + 3 <= b]

        def turns_conv(g):
            if g == 0:
                return []
            return units_between(K_CONV[g - 2] if g >= 2 else 0, K_CONV[g - 1]) + (
                units_between(K_CONV[g - 1], K_CONV[g]) if g == HG - 1 else [])

        def turns_ffn0(tb):
            return units_between(K_FFN0[tb - 1] if tb else K_CONV[-1], K_FFN0[tb])

        def turns_ad(a):
            if a == 0:
                return []
            return [u for u in units_between(K_AD[a - 2] if a >= 2 else K_FFN0[-1], K_AD[a - 1]) if u < W3_FIRST]

        TURN_UP = {0: [W3_FIRST + 1], 5: [W3_FIRST + 2], 8: [W3_FIRST + 3]}

        def unit_shape(u):
            return (HCH[UNITS[u][1]], 2 * D) if UNITS[u][0] == 1 else (P, HALF)

        def acc_of(u):
            return acc if u % 2 == 0 else tf if u >= 7 else xtail

        def banks_before(u):
            return QB[u - 1] if u >= 2 else 0

        def quant_dests(u):
            kind, c = UNITS[u]
            out_, n = [], QB[u]
            if kind == 1:
                h = HCH[c]
                for m, dst in enumerate((W1T, W2T)):
                    out_.append([(dst[:, :, c * P:c * P + h],
                                  ps[:, 6 + (n + m) % 2, :].rearrange("p (c h) -> p c h", c=DC)[:, :, 0:h])])
                return out_
            g, q = c // 2, c % 2
            rows = slice(g * 2 * P + q, (g + 1) * 2 * P, 2)
            for m, c0 in enumerate(range(0, NH, 4)):
                k = min(4, NH - c0)
                whole = sum(HCH[c0 + i] == P for i in range(k))
                src = ps[:, 6 + (n + m) % 2, :].rearrange("p (c r) -> p c r", c=4)
                pairs = [(W3T[:, c0:c0 + whole, rows], src[:, 0:whole, :])]
                if whole < k:
                    r = HCH[c0 + k - 1]
                    pairs.append((W3T[0:r, c0 + k - 1, rows], src[0:r, k - 1, :]))
                out_.append(pairs)
            return out_

        def g_levels(m):
            return sum(shared(i // LV) for i in range(m + 1))

        def tok(tb):
            return slice(tb * TW, (tb + 1) * TW)

        def tile(tb, t):
            return slice(tb * TW + t * P, tb * TW + (t + 1) * P)

        @block.sync
        def _(sp):
            sp.dma_start(cst[:, :], A["const"]).then_inc(s["l_cst"], 16)
            for half in range(2):
                r = slice(half * MODES, (half + 1) * MODES)
                sp.dma_start(sm[r, 1, :], A["log_A_real"]).then_inc(s["l_s4"], 16)
                sp.dma_start(sm[r, 2, :], A["A_imag"]).then_inc(s["l_s4"], 16)
                sp.dma_start(sm[r, 3, :], A["C_re"]).then_inc(s["l_s4"], 16)
                sp.dma_start(sm[r, 4, :], A["C_im"]).then_inc(s["l_s4"], 16)
            sp.dma_start(sm[:, 0, :], A["log_dt"].partition_broadcast(P)).then_inc(s["l_s4"], 16)
            sp.dma_start(sm[0:1, 5, :], A["Dskip"].partition_broadcast(1)).then_inc(s["l_s4"], 16)
            sp.dma_start(leni[:, 0, :], A["len0"].partition_broadcast(P)).then_inc(s["l_len"], 16)
            sp.dma_start(leni[:, 1, :], A["len3"].partition_broadcast(P)).then_inc(s["l_len"], 16)
            sp.dma_start(w0u, A["w0"].bitcast(u8).rearrange("(c p) o -> p c o", p=P)).then_inc(s["l_w0"], 16)
            sp.dma_start(wsc[:, :], A["w0scale"].partition_broadcast(P)).then_inc(s["l_w0"], 16)
            for c in range(DC):
                sp.dma_start(uc[:, c, :], A["xconv"][c]).then_inc(s["l_u"], 16)

            def load_unit(u):
                kind, c = UNITS[u]
                if u >= 2:
                    sp.wait_ge(s["m_ready"], 15 * (u - 1))
                    if g_levels(15 * (u - 1) - 1):
                        sp.wait_ge(s["g_used"], g_levels(15 * (u - 1) - 1))
                    sp.wait_ge(s[f"l_raw{u % 2}"], 32 * (u // 2))
                slot = raw[:, u % 2, :]
                got = s[f"l_raw{u % 2}"]
                if kind == 1:
                    h = HCH[c]
                    sp.dma_start(slot[0:h, 0:D], A["w1"][c * P:c * P + h, :]).then_inc(got, 16)
                    sp.dma_start(slot[0:h, D:2 * D], A["w2"][c * P:c * P + h, :]).then_inc(got, 16)
                else:
                    g, q = c // 2, c % 2
                    o = q * (2 * HID - HALF)
                    for k in range(2):
                        cols = slice(k * HALF // 2, (k + 1) * HALF // 2)
                        sp.dma_start(slot[:, cols], A["w3"][g * P:(g + 1) * P, o + cols.start:o + cols.stop]
                                     ).then_inc(got, 16)

            load_unit(0)
            sp.wait_ge(s["d_k"], 1)
            kv = kpad.ap()
            sp.dma_start(kv[:, 0:PAD], zpad).then_inc(s["l_kpad"], 16)
            sp.dma_start(kv[:, PAD:KROW].rearrange("h (a c) -> a h c", a=LA), ksb).then_inc(s["l_kpad"], 16)
            sp.wait_ge(s["l_kpad"], 32)
            for g in range(HG):
                if g >= 2:
                    sp.wait_ge(s["p_conv"], g - 1)
                    sp.wait_ge(s[f"l_strip{g % 2}"], 16 * (g // 2))
                sp.dma_start(T[:, g % 2, :, :], bass.AP(kpad, g * GH * KROW + 1, [[1, P], [KROW, GH], [1, D]])
                             ).then_inc(s[f"l_strip{g % 2}"], 16)
                if g == 1:
                    xT = A["xT"].rearrange("(c p) n -> p c n", p=P)
                    sp.dma_start(X[:, 0:DC - 1, :], xT[:, 0:DC - 1, :]).then_inc(s["l_x"], 16)
                    sp.dma_start(X[:, DC - 1, 0:TOK - HALF], xT[:, DC - 1, 0:TOK - HALF]).then_inc(s["l_x"], 16)
                    sp.wait_ge(s["d_w0"], 1)
                    load_unit(1)
                for u in units_between(K_CONV[g - 2] if g >= 2 else 0, K_CONV[g - 1]) if g else []:
                    load_unit(u + 2)
            for u in units_between(K_CONV[-2], K_CONV[-1]):
                load_unit(u + 2)
            sp.wait_ge(s["p_qt"], QB[6])
            sp.dma_start(xtail, xT[:, DC - 1, TOK - HALF:]).then_inc(s["l_xt"], 16)
            for u in units_between(K_CONV[-1], K_FFN0[-2]):
                load_unit(u + 2)
            for a in range(ADAPT):
                if a == 1:
                    sp.wait_ge(s["d_ord"], 1)
                    sp.wait_ge(s["p_ffn0"], TB * DC)
                if a >= 2:
                    done = sp.value_load(order[0:1, NB + a - 1:NB + a], min_val=0, max_val=NGR)
                    sp.wait_ge(s["p_ad"], done + 1)
                    sp.wait_ge(s[f"l_wa{a % 2}"], 16 * (a // 2))
                sp.dma_start(WS[a % 2][:, :, :], A["wa"][a].rearrange("(c p) o -> p c o", p=P)
                             ).then_inc(s[f"l_wa{a % 2}"], 16)
                if a == 1:
                    for u in units_between(K_FFN0[-2], K_FFN0[-1]):
                        load_unit(u + 2)
                if a >= 2:
                    for u in units_between(K_AD[a - 3] if a >= 3 else K_FFN0[-1], K_AD[a - 2]):
                        load_unit(u + 2)
            for u in units_between(K_AD[-3], K_AD[-1]):
                load_unit(u + 2)
            sp.wait_ge(s["m_ready"], 15 * NU)
            sp.wait_ge(s["g_used"], g_levels(15 * NU - 1))
            for dst, name in ((l2a, "l2a"), (l2u, "wu1"), (l2q, "wq"), (wvd, "wvd")):
                sp.dma_start(dst, A[name].rearrange("(c p) o -> p c o", p=P)).then_inc(s["l_late"], 16)
            sp.dma_start(l2b, A["l2b"]).then_inc(s["l_late"], 16)
            sp.wait_ge(s["p_qt"], QB[NU])
            sp.dma_start(l2w, A["l2w"].rearrange("(c p) o -> p c o", p=P)).then_inc(s["l_late"], 16)
            sp.dma_start(avT, A["avT"].rearrange("(c p) o -> p c o", p=P)).then_inc(s["l_prep"], 16)
            sp.dma_start(wvu, A["wvu"]).then_inc(s["l_prep"], 16)
            sp.wait_ge(s["p_down"], TB * NH)
            sp.wait_ge(s["d_x2"], NB // 8)
            sp.wait_ge(s["g_x2"], NB - NB // 8)
            sp.dma_start(bm, A["bmat"]).then_inc(s["l_l3"], 16)
            sp.dma_start(aT, A["l3aT"]).then_inc(s["l_l3"], 16)
            sp.dma_start(w48[:, :, 0:RANK], A["l3a"].rearrange("(c p) o -> p c o", p=P)).then_inc(s["l_l3w"], 16)
            sp.dma_start(l3w, A["l3w"].rearrange("(c p) o -> p c o", p=P)).then_inc(s["l_l3w"], 16)
            sp.dma_start(diag, A["diag"]).then_inc(s["l_diag"], 16)
            for n in range(TB * DC):
                tb, oc = n // DC, n % DC
                sp.wait_ge(s["d_o"], n + 1)
                sp.dma_start(out[oc * P:(oc + 1) * P, tok(tb)], X[:, oc, tok(tb)]).then_inc(s["l_out"], 16)
            sp.wait_ge(s["l_out"], 16 * TB * DC)

        @block.gpsimd
        def _(pool):
            pool.dma_start(idc_i[:, :], A["ids"].rearrange("(n a) -> n a", a=1)).then_inc(s["l_ids"], 16)
            pool.dma_start(idr_i[:, :], A["ids"].partition_broadcast(NB)).then_inc(s["l_ids"], 16)
            for dst, src in ((l2r[:, :, :], A["wr"].rearrange("(c p) o -> p c o", p=P)), (rq48[:, :], A["wrq"]),
                             (akT[0:BOT, :], A["akT"]),
                             (akT[BOT:BOT + 1, :], A["log_rel"].partition_broadcast(1)),
                             (rk[RDIM:RDIM + 1, :], A["log_rel"].partition_broadcast(1)),
                             (bu1[:, :], A["bu1"].rearrange("(n a) -> n a", a=1)), (wu2[:, :], A["wu2"]),
                             (gsc[:, 0:1], A["gate_w1"].partition_broadcast(P)),
                             (gsc[:, 1:2], A["gate_bias"].partition_broadcast(P)),
                             (gsc[:, 2:3], A["bu2"].partition_broadcast(P)),
                             (b3[:, :], A["b3"]), (b8[:, :], A["b3row"][0:E].partition_broadcast(P)),
                             (lim[:, :], A["lim"]), (limT[:, :], A["limT"]),
                             (cw[:, :], A["conv_w"].partition_broadcast(NB)),
                             (lc_i[:, :], A["len3"].rearrange("(n a) -> n a", a=1))):
                pool.dma_start(dst, src).then_inc(s["l_sml"], 16)
            for q in range(4):
                src = A["lang"][q]
                pool.dma_start(lan_i[q * S:(q + 1) * S, :], src.partition_broadcast(S)).then_inc(s["l_sml"], 16)
            pool.wait_ge(s["d_mask"], 1)
            for c in range(DC):
                pool.wait_ge(s["l_u"], 16 * DC)
                v = uc[:, c, :].rearrange("p (h b) -> p h b", b=NB)
                nc.gpsimd.tensor_tensor(v, v, mrev[:, c:c + 1, :].to_broadcast([P, S, NB]), ALU.mult
                                        ).then_inc(s["g_u"], 1)
            count = [0]

            def link(ins):
                count[0] += 1
                ins.then_inc(s["g_step"], 1)
                pool.wait_ge(s["g_step"], count[0])

            def levels(k):
                u = k // 3
                h, w = unit_shape(u)
                w0_ = split_cols(k)
                if w0_ == w:
                    return
                ac = acc_of(u)[0:h, w0_:w]
                normed(pool, u)
                if k % 3 == 0 and banks_before(u):
                    pool.wait_ge(s["p_qt"], banks_before(u))
                elif k % 3 and not shared(k - 1):
                    pool.wait_ge(s["m_used"], LV * k)
                for i in range(LV * (k % 3), LV * (k % 3 + 1)):
                    dst = lstep[0:h, 0:w - w0_] if i else ac
                    link(nc.gpsimd.tensor_scalar(dst, raw[0:h, u % 2, w0_:w], float(BOUNDS[i]), float(STEPS[i]),
                                                 ALU.is_gt, ALU.mult))
                    if i:
                        last = nc.gpsimd.tensor_tensor(ac, ac, dst, ALU.add)
                    else:
                        last = nc.gpsimd.tensor_scalar(ac, ac, float(NF4[0]), None, ALU.add)
                    last.then_inc(s["g_used"], 1)
                    pool.wait_ge(s["g_used"], g_levels(15 * u + i))
                if k % 3 == 1 and u + 1 < NU:
                    v = u + 1
                    h, w = unit_shape(v)
                    pool.wait_ge(s["d_rmx"], v + 1)
                    r = raw[0:h, v % 2, 0:w].rearrange("p (n k) -> p n k", k=BLK)
                    nc.gpsimd.tensor_tensor(r, r, rmax[0:h, 0:w // BLK].unsqueeze(2).to_broadcast([h, w // BLK, BLK]),
                                            ALU.mult).then_inc(s["g_nrm"], 1)
                    pool.wait_ge(s["g_nrm"], sum(pool_norm(i) for i in range(v + 1)))
                if k % 3 == 2 and pool_scale(u):
                    pool.wait_ge(s["m_used"], 15 * (u + 1))
                    acb = acc_of(u)[0:h, 0:w].rearrange("p (n k) -> p n k", k=BLK)
                    nc.gpsimd.tensor_tensor(acb, acb, amax[0:h, u % 2, 0:w // BLK].unsqueeze(2).to_broadcast(
                        [h, w // BLK, BLK]), ALU.mult).then_inc(s["g_dq"], 1)

            for k in range(K_FFN0[-1]):
                levels(k)
            pool.wait_ge(s["d_ord"], 1)
            pool.wait_ge(s["d_x1"], TB * DC)
            with pool.Fori(DP, NB) as t:
                b = pool.value_load(order[0:1, bass.ds(t, 1)], min_val=0, max_val=NB - 1)
                pool.tensor_copy(Y[:, :, bass.ds(t * S, S)], X[:, :, bass.ds(b * S, S)]).then_inc(s["g_xs"], 1)
            nc.gpsimd.memset(Yp[:, DC * TOK:], 0.0).then_inc(s["g_xs"], GB)
            for k in range(K_FFN0[-1], PARTS):
                levels(k)
            for tb in range(TB):
                pool.wait_ge(s["a_fo"], tb + 1)
                n_ = TW // S if tb < TB - 1 else TW // S // 2
                with pool.Fori(0, n_, 4) as t:
                    bs = [pool.value_load(order[0:1, bass.ds(t + (tb * (TW // S) + i), 1)], min_val=0, max_val=NB - 1)
                          for i in range(4)]
                    for i, b in enumerate(bs):
                        pool.tensor_tensor(X[:, :, bass.ds(b * S, S)], X[:, :, bass.ds(b * S, S)],
                                           Up[:, :, bass.ds(t * S + (tb * TW + i * S), S)], ALU.add
                                           ).then_inc(s["g_x2"], 1)
            for tb in range(TB):
                pool.wait_ge(s["a_c2"], tb + 1)
                pool.wait_ge(s["p_c2"], tb + 1)
                nc.gpsimd.tensor_tensor(X[:, :, tok(tb)], X[:, :, tok(tb)], Y[:, :, tok(tb)], ALU.add
                                        ).then_inc(s["g_xc"], 1)
            pool.wait_ge(s["d_mx"], 1)
            nc.gpsimd.partition_all_reduce(gm4, mx4, P, bass.bass_isa.ReduceOp.absmax).then_inc(s["g_mx"], 1)

        NSML = 16 * 20

        @block.scalar
        def _(act):
            act.wait_ge(s["d_ang"], 1)
            nc.scalar.activation(dec, dec, ACT.Exp).then_inc(s["a_ang"], 1)
            act.wait_ge(s["d_ang"], 2)
            nc.scalar.activation(ang, ang, ACT.Sin).then_inc(s["a_ang"], 1)

            def levels(k):
                u = k // 3
                h, w = unit_shape(u)
                normed(act, u)
                for i in range(LV * (k % 3), LV * (k % 3 + 1)):
                    m = 15 * u + i
                    if m >= 2:
                        act.wait_ge(s["m_used"], m - 1)
                    nc.scalar.activation(above[0:h, m % 2, 0:split_cols(k)], raw[0:h, u % 2, 0:split_cols(k)], ACT.Relu,
                                         scale=STEEP, bias=cst[0:h, C_BND + i:C_BND + i + 1]).then_inc(s["m_ready"], 1)

            def evac_quant(u):
                for m, pairs in enumerate(quant_dests(u)):
                    act.wait_ge(s["p_qt"], QB[u] + m + 1)
                    for dst, src in pairs:
                        last = nc.scalar.activation(dst, src, ACT.Copy)
                    last.then_inc(s["a_qt"], 1)

            def step(k):
                levels(k)
                if k % 3 == 0 and k:
                    evac_quant(k // 3 - 1)

            for k in range(K_FFN0[-1]):
                step(k)
            evac_quant(K_FFN0[-1] // 3 - 1)
            act.wait_ge(s["d_ord"], 1)
            act.sem_inc(s["ad_out"], 2)
            for a in range(ADAPT):
                for k in parts_of(K_AD, a, K_FFN0[-1]):
                    levels(k)
                lo = act.value_load(order[0:1, NB + a:NB + a + 1], min_val=0, max_val=NGR)
                hi = act.value_load(order[0:1, NB + a + 1:NB + a + 2], min_val=0, max_val=NGR)
                with act.If(lo < hi), act.Fori(lo, hi) as g:
                    t = act.value_load(order[0:1, bass.ds(g + (NB + ADAPT + 1), 1)], min_val=0, max_val=NB - 1)
                    act.wait_ge(s["p_ad"], g + 2)
                    act.activation(Up[:, :, bass.ds(t * S, GB * S)],
                                   gslot[:, bass.ds(g % 2, 1), :, :].rearrange("p a c n -> p (a c) n"),
                                   ACT.Copy).then_inc(s["ad_out"], 1)
                for u in turns_ad(a):
                    evac_quant(u)
            evac_quant(W3_FIRST)
            def layer1_out(tb):
                act.wait_ge(s["p_down"], (tb + 1) * NH)
                nc.scalar.activation(Up[:, :, tok(tb)], ps[:, 4:8, :], ACT.Copy).then_inc(s["a_fo"], 1)

            for n in range(TB * NH):
                h = HCH[n % NH]
                if n < NH:
                    for k in parts_of(K_UP, n, K_AD[-1]):
                        levels(k)
                if n >= 2 * NH and n % NH == 0:
                    layer1_out(n // NH - 2)
                act.wait_ge(s["p_gu"], n + 1)
                if n >= 2:
                    act.wait_ge(s["d_h"], n - 1)
                nc.scalar.activation(sg[n % 2][0:h, :], ps[0:h, n % 2, :], ACT.Silu).then_inc(s["a_silu"], 1)
                if n in TURN_UP:
                    evac_quant(TURN_UP[n][0])
            layer1_out(TB - 2)
            layer1_out(TB - 1)
            act.wait_ge(s["p_prep"], 1)
            nc.scalar.activation(v1, ps[0:VB, 1, 0:NSLOT], ACT.Copy).then_inc(s["a_v1"], 1)
            nc.scalar.activation(rk[0:RDIM, :], ps[0:RDIM, 0, 0:NSLOT], ACT.Copy,
                                 scale=float(RDIM ** -0.5)).then_inc(s["a_rk"], 1)
            act.wait_ge(s["p_v2"], 1)
            act.wait_ge(s["d_x2"], NB // 8)
            act.wait_ge(s["g_x2"], NB - NB // 8)
            nc.scalar.activation(v2, ps[:, 3, :], ACT.Copy).then_inc(s["a_v2"], 1)

            def gates(tb):
                act.wait_ge(s["p_lgt"], tb + 1)
                if tb:
                    act.wait_ge(s["p_lg"], tb)
                nc.scalar.activation(lgT, ps[0:E, 1, :], ACT.Copy).then_inc(s["a_lgt"], 1)
                act.wait_ge(s["p_ha"], tb + 1)
                if tb:
                    act.wait_ge(s["d_hg"], tb)
                nc.scalar.activation(ha, ps[:, 0, :], ACT.Copy).then_inc(s["a_ha"], 1)
                act.wait_ge(s["d_gl"], tb + 1)
                nc.scalar.activation(ge, ge, ACT.Exp).then_inc(s["a_ge"], 1)

            gates(0)
            act.wait_ge(s["p_w16"], 1)
            nc.scalar.activation(w16[:, :, E:2 * E], ps[:, 3, 0:DC * E].rearrange("p (c e) -> p c e", c=DC),
                                 ACT.Copy).then_inc(s["a_w16"], 1)
            for tb in range(TB):
                act.wait_ge(s["p_c2"], tb + 1)
                nc.scalar.activation(Y[:, :, tok(tb)], ps[:, 4:8, :], ACT.Copy).then_inc(s["a_c2"], 1)
                if tb + 1 < TB:
                    gates(tb + 1)
                act.wait_ge(s["p_q"], tb + 1)
                if tb:
                    act.wait_ge(s["p_sc"], tb)
                nc.scalar.activation(qT[0:BOT, :], ps[0:BOT, 0, :], ACT.Copy).then_inc(s["a_q"], 1)
                act.wait_ge(s["p_rq"], tb + 1)
                nc.scalar.activation(rqT[0:RDIM, :], ps[0:RDIM, 1, :], ACT.Copy).then_inc(s["a_rq"], 1)
                act.wait_ge(s["p_gup"], tb + 1)
                nc.scalar.activation(gu, ps[:, 4, :], ACT.Gelu_apprx_tanh, bias=bu1[:, 0:1]).then_inc(s["a_gu"], 1)
                act.wait_ge(s["p_lr"], tb + 1)
                nc.scalar.activation(lrn[:, tb * NT:(tb + 1) * NT], ps[:, 5, 0:NT], ACT.Copy).then_inc(s["a_lr"], 1)
                if tb == TB - 1:
                    act.wait_ge(s["d_st"], TT + 1)
                    nc.scalar.activation(lv[:, :], var[:, :, 1], ACT.Ln, bias=1.0, accum_out=lvs[:, 0:1]).then_inc(s["a_lv"], 1)
                    act.wait_ge(s["a_lr"], TB)
                    nc.scalar.activation(gq[:, 0, :], lrn[:, :], ACT.Sigmoid, bias=gsc[:, 2:3]).then_inc(s["a_sg"], 1)
                act.wait_ge(s["d_am"], tb + 1)
                for t in range(NT):
                    k = tb * NT + t
                    nc.scalar.activation(PR[:, k, :], am[:, t, :], ACT.Exp, bias=nmx[:, t:t + 1],
                                         accum_out=den[:, k:k + 1]).then_inc(s["a_pr"], 1)
            act.wait_ge(s["d_un"], 1)
            nc.scalar.activation(gq[:, 2, :], gq[:, 1, :], ACT.Sigmoid, scale=gsc[:, 0:1], bias=gsc[:, 1:2]
                                 ).then_inc(s["a_gt"], 1)

            def gate3(tb):
                act.wait_ge(s["d_ys"], tb + 1)
                nc.scalar.activation(ysm[:, 2, 0:S], ysm[:, 1, 0:S], ACT.Sigmoid).then_inc(s["a_yg"], 1)

            for tb in range(TB):
                act.wait_ge(s["p_pt"], tb + 1)
                nc.scalar.activation(PT[:, tok(tb)], ps[:, tb % 2, :], ACT.Copy).then_inc(s["a_pt"], 1)
                if tb >= 2:
                    gate3(tb - 2)
            gate3(TB - 2)
            gate3(TB - 1)
            for tb in range(TB):
                act.wait_ge(s["p_z"], tb + 1)
                nc.scalar.activation(zt[:, tok(tb)], ps[0:RANK + 2 * E, 2, :], ACT.Copy).then_inc(s["a_z"], 1)
            act.wait_ge(s["d_lg3"], 1)
            nc.scalar.activation(pr3, lg3, ACT.Exp).then_inc(s["a_e3"], 1)
            act.wait_ge(s["d_th"], 1)
            nc.scalar.activation(mk3, mk3, ACT.Sigmoid, scale=2.0).then_inc(s["a_mk"], 1)
            for k in range(2):
                act.wait_ge(s["p_wt"], k + 1)
                nc.scalar.activation(wT[:, k * 512:(k + 1) * 512], ps[0:E, 2 + k, :], ACT.Copy).then_inc(s["a_wt"], 1)

        @block.tensor
        def _(pe):
            def mm(o, l, r, start, stop, **kw):
                return nc.tensor.matmul(o, l, r, start=start, stop=stop, **kw)

            pe.wait_ge(s["l_cst"], 16)
            pe.wait_ge(s["d_ones"], 1)
            pe.wait_ge(s["d_oneh"], 1)
            mm(ps[0:1, 5, 0:NB], cst[0:NB, C_PCOL:C_PCOL + 1], oneh[:, 0:NB], True, True)
            mm(ps[0:1, 5, NB:NB + ADAPT + 1], ones[0:NB, 0:1], oneh[:, NB:], True, True).then_inc(s["p_ord"], 1)
            pe.wait_ge(s["d_pp"], 1)
            for h in range(S):
                last = mm(ps[0:LA, 6 + h // 16, (h % 16) * LC:(h % 16 + 1) * LC], pc[:, h, :], turn[:, h, 0:LC],
                          True, True)
            last.then_inc(s["p_k"], 1)

            def turn_unit(u):
                kind, c = UNITS[u]
                if pool_scale(u):
                    pe.wait_ge(s["g_dq"], sum(pool_scale(i) for i in range(u + 1)))
                else:
                    pe.wait_ge(s["d_dq"], sum(not pool_scale(i) for i in range(u + 1)))
                n = QB[u]
                acc = acc_of(u)
                groups = []
                if kind == 1:
                    h = HCH[c]
                    for m in range(2):
                        groups.append([(ps[:, 6 + (n + m) % 2, k * P:k * P + h],
                                        acc[0:h, m * D + k * P:m * D + (k + 1) * P], h) for k in range(DC)])
                else:
                    o = (c % 2) * (HALF - HID)
                    for m, c0 in enumerate(range(0, NH, 4)):
                        groups.append([(ps[0:HCH[i], 6 + (n + m) % 2, (i - c0) * P:(i - c0 + 1) * P],
                                        acc[:, o + i * P:o + i * P + HCH[i]], P) for i in range(c0, min(c0 + 4, NH))])
                for m, group in enumerate(groups):
                    if n + m >= 2:
                        pe.wait_ge(s["a_qt"], n + m - 1)
                    else:
                        pe.wait_ge(s["d_k"], 1)
                    for dst, src, h in group:
                        last = nc.tensor.transpose(dst, src, ident[0:h, 0:h])
                    last.then_inc(s["p_qt"], 1)

            pe.wait_ge(s["g_u"], DC)
            for g in range(HG):
                pe.wait_ge(s[f"l_strip{g % 2}"], 16 * (g // 2 + 1))
                if g >= 4:
                    pe.wait_ge(s["d_conv"], g - 3)
                for k in range(GH):
                    h = g * GH + k
                    for lb in range(DC):
                        o = lb * GH * NB + k * NB
                        for jb in range(lb + 1):
                            last = mm(ps[:, g % 4, o:o + NB], T[:, g % 2, k, (lb - jb) * P:(lb - jb + 1) * P],
                                      uc[:, jb, h * NB:(h + 1) * NB], jb == 0, jb == lb)
                last.then_inc(s["p_conv"], 1)
                for u in turns_conv(g):
                    turn_unit(u)
            pe.wait_ge(s["d_conv"], HG)
            pe.wait_ge(s["d_w0"], 1)
            pe.wait_ge(s["d_ord"], 1)
            for n in range(TB * DC):
                tb, oc = n // DC, n % DC
                if n >= len(BANKS0):
                    pe.wait_ge(s["d_x1"], n - len(BANKS0) + 1)
                for c in range(DC):
                    last = mm(ps[:, BANKS0[n % len(BANKS0)], :], w0[:, c, oc * P:(oc + 1) * P], Y[:, c, tok(tb)], c == 0, c == DC - 1)
                last.then_inc(s["p_ffn0"], 1)
                if oc == DC - 1:
                    for u in turns_ffn0(tb):
                        turn_unit(u)
            pe.wait_ge(s["ad_out"], 2)
            pe.sem_inc(s["p_ad"], 1)
            pe.wait_ge(s["d_xs"], DP)
            for a in range(ADAPT):
                pe.wait_ge(s[f"l_wa{a % 2}"], 16 * (a // 2 + 1))
                lo = pe.value_load(order[0:1, NB + a:NB + a + 1], min_val=0, max_val=NGR)
                hi = pe.value_load(order[0:1, NB + a + 1:NB + a + 2], min_val=0, max_val=NGR)
                with pe.If(lo < hi), pe.Fori(lo, hi) as g:
                    t = pe.value_load(order[0:1, bass.ds(g + (NB + ADAPT + 1), 1)], min_val=0, max_val=NB - 1)
                    pe.wait_ge(s["ad_out"], g + 1)
                    pe.wait_ge(s["g_xs"], t + GB - DP)
                    for oc in range(DC):
                        for c in range(DC):
                            last = mm(gslot[:, bass.ds(g % 2, 1), oc, :].rearrange("p a n -> p (a n)"),
                                      WS[a % 2][:, c, oc * P:(oc + 1) * P],
                                      Yp[:, bass.ds(t * S + c * TOK, GB * S)], c == 0, c == DC - 1)
                    last.then_inc(s["p_ad"], 1)
                for u in turns_ad(a):
                    turn_unit(u)
            pe.wait_ge(s["ad_out"], hi + 2)

            def up(n):
                tb, c, h = n // NH, n % NH, HCH[n % NH]
                if n < NH:
                    pe.wait_ge(s["a_qt"], QB[n + 1])
                if n >= 2:
                    pe.wait_ge(s["d_h"], n - 1)
                for w, bk in ((W1T, n % 2), (W2T, 2 + n % 2)):
                    for k in range(DC):
                        last = mm(ps[0:h, bk, :], w[:, k, c * P:c * P + h], Up[:, k, tok(tb)], k == 0, k == DC - 1)
                last.then_inc(s["p_gu"], 1)

            def down(n):
                tb, c, h = n // NH, n % NH, HCH[n % NH]
                pe.wait_ge(s["d_h"], n + 1)
                if c == 0 and tb:
                    pe.wait_ge(s["a_fo"], tb)
                for oc in range(DC):
                    last = mm(ps[:, 4 + oc, :], W3T[0:h, c, oc * P:(oc + 1) * P], hs[0:h, c, :], c == 0, c == NH - 1)
                last.then_inc(s["p_down"], 1)

            turn_unit(W3_FIRST)
            for n in range(NH):
                up(n)
                for u in TURN_UP.get(n, []):
                    turn_unit(u)
            pe.wait_ge(s["a_qt"], QB[NU])
            for n in range(TB * NH):
                down(n)
                if n + NH < TB * NH:
                    up(n + NH)
            pe.wait_ge(s["l_sml"], NSML)
            pe.wait_ge(s["l_prep"], 32)
            pe.wait_ge(s["l_late"], 16 * 6)
            pe.wait_ge(s["a_silu"], TB * NH)
            pe.wait_ge(s["d_h"], TB * NH)
            mm(ps[0:RDIM, 0, 0:NSLOT], rq48[:, :], akT[0:BOT, :], True, True)
            for c in range(DC):
                last = mm(ps[0:VB, 1, 0:NSLOT], wvd[:, c, :], avT[:, c, :], c == 0, c == DC - 1)
            last.then_inc(s["p_prep"], 1)
            pe.wait_ge(s["a_v1"], 1)
            mm(ps[:, 3, :], v1, wvu, True, True).then_inc(s["p_v2"], 1)
            pe.wait_ge(s["a_rk"], 1)
            pe.wait_ge(s["a_fo"], TB)
            pe.wait_ge(s["d_x2"], NB // 8)
            pe.wait_ge(s["g_x2"], NB - NB // 8)

            def gates(tb):
                if tb >= 2:
                    pe.wait_ge(s["a_rq"], tb - 1)
                    pe.wait_ge(s["a_q"], tb - 1)
                for c in range(DC):
                    last = mm(ps[0:E, 1, :], l2r[:, c, :], X[:, c, tok(tb)], c == 0, c == DC - 1)
                last.then_inc(s["p_lgt"], 1)
                for c in range(DC):
                    last = mm(ps[:, 0, :], l2a[:, c, :], X[:, c, tok(tb)], c == 0, c == DC - 1)
                last.then_inc(s["p_ha"], 1)
                pe.wait_ge(s["a_lgt"], tb + 1)
                for t in range(NT):
                    last = nc.tensor.transpose(ps[:, 2, t * E:(t + 1) * E], lgT[:, t * P:(t + 1) * P], ident[0:E, 0:E])
                last.then_inc(s["p_lg"], 1)

            gates(0)
            for tb in range(TB):
                for oc in range(DC):
                    if tb:
                        if oc == 0:
                            pe.wait_ge(s["a_gu"], tb)
                        if oc == 1:
                            pe.wait_ge(s["a_lr"], tb)
                        if oc == 2:
                            pe.wait_ge(s["d_am"], tb)
                    for c in range(DC):
                        mm(ps[:, 4 + oc, :], l2w[:, c, oc * P:(oc + 1) * P], X[:, c, tok(tb)], c == 0, False)
                if tb == 0:
                    pe.wait_ge(s["l_l3"], 32)
                    pe.wait_ge(s["a_v2"], 1)
                    for c in range(DC):
                        last = mm(ps[:, 3, c * E:(c + 1) * E], aT[:, c * P:(c + 1) * P], limT[:, :], True, True)
                    last.then_inc(s["p_w16"], 1)
                pe.wait_ge(s["d_gate"], tb + 1)
                if tb:
                    pe.wait_ge(s["d_st"], NT * tb)
                for t in range(NT):
                    last = nc.tensor.transpose(ps[:, 2, t * P:(t + 1) * P],
                                               gt[:, t, :], ident)
                last.then_inc(s["p_gx"], 1)
                pe.wait_ge(s["d_hg"], tb + 1)
                for oc in range(DC):
                    last = mm(ps[:, 4 + oc, :], l2b[:, oc * P:(oc + 1) * P], hgx, False, True)
                last.then_inc(s["p_c2"], 1)
                if tb + 1 < TB:
                    gates(tb + 1)
                pe.wait_ge(s["a_c2"], tb + 1)
                if tb + 1 < TB:
                    pe.wait_ge(s["a_ha"], tb + 2)
                for c in range(DC):
                    last = mm(ps[0:BOT, 0, :], l2q[:, c, :], Y[:, c, tok(tb)], c == 0, c == DC - 1)
                last.then_inc(s["p_q"], 1)
                for c in range(DC):
                    last = mm(ps[:, 4, :], l2u[:, c, :], Y[:, c, tok(tb)], c == 0, c == DC - 1)
                last.then_inc(s["p_gup"], 1)
                pe.wait_ge(s["a_q"], tb + 1)
                if tb + 1 < TB:
                    pe.wait_ge(s["d_gl"], tb + 2)
                mm(ps[0:RDIM, 1, :], rq48[:, :], qT[0:BOT, :], True, True).then_inc(s["p_rq"], 1)
                for t in range(NT):
                    if tb or t >= 2:
                        pe.wait_ge(s["d_st"], NT * tb + t - 1)
                    else:
                        pe.wait_ge(s["a_w16"], 1)
                    for c in range(DC):
                        last = nc.tensor.transpose(ps[:, 3 - t % 2, c * P:(c + 1) * P], Y[:, c, tile(tb, t)], ident)
                    last.then_inc(s["p_tr"], 1)
                pe.wait_ge(s["a_rq"], tb + 1)
                pe.wait_ge(s["d_ak"], 1)
                for t in range(NT):
                    mm(ps[:, 6, t * NSLOT:(t + 1) * NSLOT], rqT[:, t * P:(t + 1) * P], rk[:, :], True, True)
                    last = mm(ps[:, 7, t * NSLOT:(t + 1) * NSLOT], qT[:, t * P:(t + 1) * P], akT[:, :], True, True)
                last.then_inc(s["p_sc"], 1)
                pe.wait_ge(s["a_gu"], tb + 1)
                for t in range(NT):
                    last = mm(ps[:, 5, t:t + 1], gu[:, t * P:(t + 1) * P], wu2[:, :], True, True)
                last.then_inc(s["p_lr"], 1)
            pe.wait_ge(s["a_lv"], 1)
            mm(ps[:, 0, 0:1], ones[:, :], lvs[:, 0:1], True, True).then_inc(s["p_lv"], 1)

            def masked_sums(tb):
                pe.wait_ge(s["d_x3"], tb + 1)
                if tb >= 2:
                    pe.wait_ge(s["d_ys"], tb - 1)
                for c in range(DC):
                    last = mm(ps[0:NB, 2 + tb % 2, :], mnat[:, c, :], X[:, c, tok(tb)], c == 0, c == DC - 1)
                last.then_inc(s["p_y"], 1)

            for tb in range(TB):
                pe.wait_ge(s["d_pn"], tb + 1)
                if tb >= 2:
                    pe.wait_ge(s["a_pt"], tb - 1)
                for t in range(NT):
                    last = nc.tensor.transpose(ps[:, tb % 2, t * P:(t + 1) * P], PR[:, tb * NT + t, :], ident)
                last.then_inc(s["p_pt"], 1)
                pe.wait_ge(s["a_pt"], tb + 1)
                if tb:
                    pe.wait_ge(s["d_x3"], tb)
                for oc in range(DC):
                    last = mm(ps[:, 4 + oc, :], v2[:, oc * P:(oc + 1) * P], PT[:, tok(tb)], True, True)
                last.then_inc(s["p_aux"], 1)
                if tb:
                    masked_sums(tb - 1)
            masked_sums(TB - 1)
            pe.wait_ge(s["l_l3w"], 32)
            pe.wait_ge(s["d_w16"], 1)

            def spread_gate(tb):
                pe.wait_ge(s["d_gex"], tb + 1)
                if tb >= 2:
                    pe.wait_ge(s["d_c3"], tb - 1)
                mm(ps[:, tb % 2, :], ones[0:NB, :], gex[tb], True, True).then_inc(s["p_gb"], 1)

            spread_gate(0)
            for tb in range(TB):
                if tb + 1 < TB:
                    spread_gate(tb + 1)
                pe.wait_ge(s["d_c3"], tb + 1)
                if tb:
                    pe.wait_ge(s["a_z"], tb)
                for c in range(DC):
                    last = mm(ps[0:RANK + 2 * E, 2, :], w48[:, c, :], Y[:, c, tok(tb)], c == 0, c == DC - 1)
                last.then_inc(s["p_z"], 1)
                for oc in range(DC):
                    if tb:
                        pe.wait_ge(s["d_b"], (tb - 1) * DC + oc + 1)
                    for c in range(DC):
                        last = mm(ps[:, 4 + oc, :], l3w[:, c, oc * P:(oc + 1) * P], Y[:, c, tok(tb)],
                                  c == 0, c == DC - 1)
                    last.then_inc(s["p_b"], 1)
                    if oc == 0:
                        pe.wait_ge(s["a_z"], tb + 1)
                        if tb:
                            pe.wait_ge(s["d_sl"], tb)
                        for k in range(2):
                            a0 = tb * TW + k * 2 * P + 1
                            last = nc.tensor.transpose(ps[:, 3, k * ZW:(k + 1) * ZW], zt[:, a0:a0 + 2 * P - 1:2],
                                                       ident[0:ZW, 0:ZW])
                        last.then_inc(s["p_sl"], 1)
            pe.wait_ge(s["d_w3"], 1)
            for k in range(2):
                for t in range(4):
                    last = nc.tensor.transpose(ps[0:E, 2 + k, t * P:(t + 1) * P], tm3[:, 4 * k + t, :], ident)
                last.then_inc(s["p_wt"], 1)
            pe.wait_ge(s["a_wt"], 2)
            pe.wait_ge(s["d_b"], TB * DC)
            for tb in range(TB):
                if tb >= 2:
                    pe.wait_ge(s["d_zp"], tb - 1)
                mm(ps[0:RANK, tb % 2, :], lim[:, :],
                   wT[:, tb * 256:(tb + 1) * 256].unsqueeze(2).to_broadcast([E, 256, 2]), True, True
                   ).then_inc(s["p_pm"], 1)
                for oc in range(DC):
                    if tb:
                        pe.wait_ge(s["d_o"], (tb - 1) * DC + oc + 1)
                    if oc == 0:
                        pe.wait_ge(s["d_zp"], tb + 1)
                    mm(ps[:, 4 + oc, :], bm[:, oc * P:(oc + 1) * P], zp[tb % 2], True, True).then_inc(s["p_o"], 1)

        @block.vector
        def _(dve):
            V = nc.vector
            count = [0]

            def link(ins):
                count[0] += 1
                ins.then_inc(s["v_step"], 1)
                dve.wait_ge(s["v_step"], count[0])

            def tt(o, a, b, op):
                link(V.tensor_tensor(o, a, b, op))

            def ts(o, a, x, y, op0, op1):
                link(V.tensor_scalar(o, a, x, y, op0, op1))

            def stt(o, a, x, b, op0, op1):
                link(V.scalar_tensor_tensor(out=o, in0=a, scalar=x, in1=b, op0=op0, op1=op1))

            V.memset(ones[:, :], 1.0).then_inc(s["d_ones"], 1)
            dve.wait_ge(s["d_ones"], 1)
            dve.wait_ge(s["l_cst"], 16)
            dve.wait_ge(s["l_len"], 32)
            link(V.tensor_copy(lenf[:, :, :], leni[:, :, :]))
            for c in range(DC):
                link(V.tensor_scalar(mnat[:, c, :], lenf[:, 0, :], cst[:, C_L + c:C_L + c + 1], None, ALU.is_gt))
            for c in range(DC):
                last = V.tensor_scalar(mrev[:, c, :], lenf[:, 0, :], cst[:, C_LREV + c:C_LREV + c + 1], None, ALU.is_gt)
            last.then_inc(s["d_mask"], 1)
            dve.wait_ge(s["l_ids"], 32)
            link(V.tensor_copy(idc[:, :], idc_i[:, :]))
            link(V.tensor_copy(keyr[:, :], idr_i[:, :]))
            ts(idc[:, :], idc[:, :], 0.0, float(ADAPT - 1), ALU.max, ALU.min)
            ts(keyr[:, :], keyr[:, :], 0.0, float(ADAPT - 1), ALU.max, ALU.min)
            stt(keyc[:, :], idc[:, :], float(NB), cst[0:NB, C_PCOL:C_PCOL + 1], ALU.mult, ALU.add)
            stt(keyr[:, :], keyr[:, :], float(NB), cst[0:NB, C_IOTA:C_IOTA + NB], ALU.mult, ALU.add)
            link(V.tensor_scalar(below[:, :], keyr[:, :], keyc[:, 0:1], None, ALU.is_lt))
            link(V.reduce_sum(rank[:, :], below[:, :], AX.X))
            link(V.tensor_scalar(oneh[:, 0:NB], cst[0:NB, C_IOTA:C_IOTA + NB], rank[:, 0:1], None, ALU.is_equal))
            V.tensor_scalar(oneh[:, NB:], cst[0:NB, C_IOTA:C_IOTA + ADAPT + 1], idc[:, 0:1], None, ALU.is_gt
                            ).then_inc(s["d_oneh"], 1)

            dve.wait_ge(s["l_s4"], 160)
            sl_ = [sm[:, i, :] for i in range(32)]
            ldt, lar, aim, cre, cim = sl_[0:5]

            def expm1(x, y, one, w):
                k, r, p, sc_ = w
                ts(k, x, LOG2E, ROUND, ALU.mult, ALU.add)
                ts(k, k, ROUND, -126.0, ALU.subtract, ALU.max)
                stt(r, k, -LN2_HI, x, ALU.mult, ALU.add)
                stt(r, k, -LN2_LO, r, ALU.mult, ALU.add)
                ts(p, r, 1.0 / 40320, None, ALU.mult, ALU.bypass)
                for c in (1.0 / 5040, 1.0 / 720, 1.0 / 120, 1.0 / 24, 1.0 / 6, 0.5, 1.0):
                    stt(p, p, c, r, ALU.add, ALU.mult)
                ts(sc_.bitcast(i32), k, 127.0, float(2 ** 23), ALU.add, ALU.mult)
                tt(p, p, sc_, ALU.mult)
                if one:
                    ts(sc_, sc_, -1.0, None, ALU.add, ALU.bypass)
                tt(y, p, sc_, ALU.add)

            two = sm[:, 0:2, :]
            expm1(two, sm[:, 6:8, :], False, [sm[:, 8 + 2 * i:10 + 2 * i, :] for i in range(4)])
            dt_, are = sl_[6], sl_[7]
            ts(are, are, -1.0, None, ALU.mult, ALU.bypass)
            a_, b_ = sl_[16], sl_[17]
            tt(a_, are, dt_, ALU.mult)
            tt(b_, aim, dt_, ALU.mult)
            mul = cst[:, C_MUL:C_MUL + CMULT].unsqueeze(1).to_broadcast([P, S, CMULT])
            ph = cst[:, C_PH:C_PH + CMULT].unsqueeze(1).to_broadcast([P, S, CMULT])
            V.tensor_tensor(dec, a_.unsqueeze(2).to_broadcast([P, S, CMULT]), mul, ALU.mult).then_inc(s["d_ang"], 1)
            tt(ang, b_.unsqueeze(2).to_broadcast([P, S, CMULT]), mul, ALU.mult)
            link(V.tensor_tensor(turn, ang, ph, ALU.add))
            ts(turn, turn, float(1 / TWO_PI), ROUND, ALU.mult, ALU.add)
            ts(turn, turn, ROUND, None, ALU.subtract, ALU.bypass)
            for c in (PI_A, PI_B, PI_C):
                stt(ang, turn, -c, ang, ALU.mult, ALU.add)
            tt(ang, ang, ph, ALU.add)
            V.tensor_scalar(ang, ang, float(np.float32(-3.1415925)), float(np.float32(3.1415925)), ALU.max, ALU.min
                            ).then_inc(s["d_ang"], 1)
            expm1(a_, sl_[18], True, [sl_[19], sl_[20], sl_[21], sl_[22]])
            em1 = sl_[18]
            dve.wait_ge(s["l_w0"], 32)
            link(V.tensor_copy(h16a, w0u))
            link(V.tensor_scalar(h16b, h16a, 0x7F, 7, ALU.bitwise_and, ALU.logical_shift_left))
            link(V.tensor_scalar(h16a, h16a, 0x80, 8, ALU.bitwise_and, ALU.logical_shift_left))
            link(V.tensor_tensor(h16a, h16a, h16b, ALU.bitwise_or))
            V.tensor_scalar(w0, h16a.bitcast(f16), 256.0, None, ALU.mult).then_inc(s["d_w0"], 1)
            dve.wait_ge(s["a_ang"], 2)
            o0 = LC + 2 * LA
            cb, sb_, hb = ang[:, :, o0], ang[:, :, o0 + 1], ang[:, :, o0 + 2]
            t1, t2, zr, zi, dn, rr, ri, yr, yi, cr, ci = sl_[19:30]
            tt(t1, em1, cb, ALU.mult)
            stt(t2, hb, -2.0, hb, ALU.mult, ALU.mult)
            tt(zr, t1, t2, ALU.add)
            stt(zi, em1, 1.0, sb_, ALU.add, ALU.mult)
            tt(t1, are, are, ALU.mult)
            tt(t2, aim, aim, ALU.mult)
            tt(dn, t1, t2, ALU.add)
            link(V.reciprocal(dn, dn))
            tt(rr, are, dn, ALU.mult)
            stt(ri, aim, -1.0, dn, ALU.mult, ALU.mult)

            def cmul(xr, xi, ar, ai, br, bi):
                tt(t1, ar, br, ALU.mult)
                tt(t2, ai, bi, ALU.mult)
                tt(xr, t1, t2, ALU.subtract)
                tt(t1, ar, bi, ALU.mult)
                tt(t2, ai, br, ALU.mult)
                tt(xi, t1, t2, ALU.add)

            cmul(yr, yi, cre, cim, zr, zi)
            cmul(cr, ci, yr, yi, rr, ri)
            al, be = sl_[30], sl_[31]
            lo, hi = slice(0, MODES), slice(MODES, P)
            ts(al[lo], cr[lo], 2.0, None, ALU.mult, ALU.bypass)
            ts(al[hi], ci[hi], -2.0, None, ALU.mult, ALU.bypass)
            ts(be[lo], ci[lo], -2.0, None, ALU.mult, ALU.bypass)
            ts(be[hi], cr[hi], -2.0, None, ALU.mult, ALU.bypass)
            tt(turn, ang, dec, ALU.mult)
            tt(pc, turn[:, :, LC:LC + LA], al.unsqueeze(2).to_broadcast([P, S, LA]), ALU.mult)
            tt(pq, turn[:, :, LC + LA:LC + 2 * LA], be.unsqueeze(2).to_broadcast([P, S, LA]), ALU.mult)
            V.tensor_tensor(pc, pc, pq, ALU.add).then_inc(s["d_pp"], 1)
            link(V.memset(zpad, 0.0))
            dve.wait_ge(s["p_ord"], 1)
            link(V.tensor_copy(order[:, 0:NB], ps[0:1, 5, 0:NB]))
            n_, m_, w_, e_ = (cnt[:, i, :] for i in range(4))
            link(V.tensor_copy(gord[:, 0:ADAPT + 1], ps[0:1, 5, NB:NB + ADAPT + 1]))
            tt(n_, gord[:, 1:ADAPT + 1], gord[:, 0:ADAPT], ALU.subtract)
            link(V.tensor_scalar(m_, n_, 0.0, None, ALU.is_gt))
            for k in range(GB, NB, GB):
                stt(m_, n_, float(k), m_, ALU.is_gt, ALU.add)
            link(V.memset(gord[:, 0:1], 0.0))
            link(V.tensor_copy(gord[:, 1:ADAPT + 1], m_))
            step = 1
            while step < ADAPT:
                link(V.tensor_copy(w_, gord[:, 1:ADAPT + 1]))
                tt(gord[:, 1 + step:ADAPT + 1], w_[:, step:], w_[:, 0:ADAPT - step], ALU.add)
                step *= 2
            giota = cst[0:1, C_IOTA:C_IOTA + NGR]
            tt(gmat[:, :, :], giota.unsqueeze(2).to_broadcast([1, NGR, ADAPT]),
               gord[:, 1:ADAPT + 1].unsqueeze(1).to_broadcast([1, NGR, ADAPT]), ALU.is_ge)
            stt(e_, m_, -float(GB), n_, ALU.mult, ALU.add)
            tt(gmat[:, :, :], gmat[:, :, :], cnt[:, 3:4, :].to_broadcast([1, NGR, ADAPT]), ALU.mult)
            link(V.tensor_reduce(gord[:, ADAPT + 1:], gmat[:, :, :], AX.X, ALU.add))
            stt(gord[:, ADAPT + 1:], giota, float(GB), gord[:, ADAPT + 1:], ALU.mult, ALU.add)
            V.tensor_copy(order[:, NB:], gord[:, :]).then_inc(s["d_ord"], 1)
            dve.wait_ge(s["p_k"], 1)
            link(V.tensor_copy(ksb, ps[0:LA, 6:8, :].rearrange("p a (h c) -> p (a h) c", c=LC)))
            V.tensor_tensor(ksb[0:1, :, 0], ksb[0:1, :, 0], sm[0:1, 5, :], ALU.add).then_inc(s["d_k"], 1)

            def start_unit(u):
                h, w = unit_shape(u)
                nb = w // BLK
                dve.wait_ge(s[f"l_raw{u % 2}"], 32 * (u // 2 + 1))
                r = raw[0:h, u % 2, 0:w].rearrange("p (n k) -> p n k", k=BLK)
                am_ = amax[0:h, u % 2, 0:nb]
                if u >= 2 and pool_scale(u - 2):
                    dve.wait_ge(s["g_dq"], sum(pool_scale(i) for i in range(u - 1)))
                if u >= 1 and pool_norm(u - 1):
                    normed(dve, u - 1)
                link(V.tensor_reduce(am_, r, AX.X, ALU.max, apply_absolute_value=True))
                link(V.tensor_scalar(rmax[0:h, 0:nb], am_, 0.0, None, ALU.is_equal))
                tt(rmax[0:h, 0:nb], rmax[0:h, 0:nb], am_, ALU.add)
                V.reciprocal(rmax[0:h, 0:nb], rmax[0:h, 0:nb]).then_inc(s["d_rmx"], 1)
                dve.wait_ge(s["d_rmx"], u + 1)
                if pool_norm(u):
                    return
                V.tensor_tensor(r, r, rmax[0:h, 0:nb].unsqueeze(2).to_broadcast([h, nb, BLK]), ALU.mult
                                ).then_inc(s["d_nrm"], 1)
                normed(dve, u)

            def levels(k):
                u = k // 3
                h, w = unit_shape(u)
                ac = acc_of(u)[0:h, 0:split_cols(k)]
                if k % 3 and k and shared(k - 1) and not shared(k):
                    dve.wait_ge(s["g_used"], g_levels(LV * k - 1))
                if k % 3 == 0 and banks_before(u):
                    dve.wait_ge(s["p_qt"], banks_before(u))
                if k % 3 == 1 and u + 1 < NU:
                    start_unit(u + 1)
                for i in range(LV * (k % 3), LV * (k % 3 + 1)):
                    m = 15 * u + i
                    dve.wait_ge(s["m_ready"], m + 1)
                    src = above[0:h, m % 2, 0:split_cols(k)]
                    if i == 0:
                        V.tensor_scalar(ac, src, float(STEPS[0]), float(NF4[0]), ALU.min, ALU.add
                                        ).then_inc(s["m_used"], 1)
                    else:
                        V.scalar_tensor_tensor(out=ac, in0=src, scalar=float(STEPS[i]), in1=ac,
                                               op0=ALU.min, op1=ALU.add).then_inc(s["m_used"], 1)
                    dve.wait_ge(s["m_used"], m + 1)
                if k % 3 == 2 and not pool_scale(u):
                    nb = w // BLK
                    if g_levels(LV * k + LV - 1):
                        dve.wait_ge(s["g_used"], g_levels(LV * k + LV - 1))
                    acb = acc_of(u)[0:h, 0:w].rearrange("p (n k) -> p n k", k=BLK)
                    V.tensor_tensor(acb, acb, amax[0:h, u % 2, 0:nb].unsqueeze(2).to_broadcast([h, nb, BLK]), ALU.mult
                                    ).then_inc(s["d_dq"], 1)
                    dve.wait_ge(s["d_dq"], sum(not pool_scale(i) for i in range(u + 1)))

            def conv_out(g):
                dve.wait_ge(s["p_conv"], g + 1)
                V.tensor_tensor(Y.rearrange("p c (b s) -> p c s b", s=S)[:, :, g * GH:(g + 1) * GH, :],
                                ps[:, g % 4, :].rearrange("p (c k b) -> p c k b", c=DC, k=GH),
                                mnat[:, :, :].unsqueeze(2).to_broadcast([P, DC, GH, NB]), ALU.mult
                                ).then_inc(s["d_conv"], 1)

            start_unit(0)
            for g in range(HG):
                for k in parts_of(K_CONV, g):
                    levels(k)
                conv_out(g)
            dve.wait_ge(s["l_x"], 32)
            for n in range(TB * DC):
                tb, oc = n // DC, n % DC
                if oc == 0:
                    for k in parts_of(K_FFN0, tb, K_CONV[-1]):
                        levels(k)
                dve.wait_ge(s["p_ffn0"], n + 1)
                if tb:
                    dve.wait_ge(s["l_xt"], 16)
                V.scalar_tensor_tensor(out=X[:, oc, tok(tb)], in0=ps[:, BANKS0[n % len(BANKS0)], :], scalar=wsc[:, 0:1],
                                       in1=X[:, oc, tok(tb)], op0=ALU.mult, op1=ALU.add).then_inc(s["d_x1"], 1)
            dve.wait_ge(s["d_x1"], TB * DC)
            with dve.Fori(0, DP) as t:
                b = dve.value_load(order[0:1, bass.ds(t, 1)], min_val=0, max_val=NB - 1)
                dve.tensor_copy(Y[:, :, bass.ds(t * S, S)], X[:, :, bass.ds(b * S, S)]).then_inc(s["d_xs"], 1)
            dve.wait_ge(s["d_conv"], HG)
            for c in range(DC):
                link(V.tensor_scalar(mnat[:, c, :], lenf[:, 1, :], cst[:, C_L + c:C_L + c + 1], None, ALU.is_gt))
            for a in range(ADAPT):
                for k in parts_of(K_AD, a, K_FFN0[-1]):
                    levels(k)
            dve.wait_ge(s["l_sml"], NSML)
            link(V.tensor_copy(lan[:, :], lan_i[:, :]))
            tt(lbias[:, :, :], cst[:, C_IOTA:C_IOTA + E].unsqueeze(1).to_broadcast([P, TT, E]),
               lan[:, :].unsqueeze(2).to_broadcast([P, TT, E]), ALU.is_equal)
            ts(lbias[:, :, :], lbias[:, :, :], 5.0, None, ALU.mult, ALU.bypass)
            link(V.tensor_copy(ilen[:, 0:1], lc_i[:, :]))
            link(V.reciprocal(ilen[:, 1:2], ilen[:, 0:1]))
            def hidden(n):
                h = HCH[n % NH]
                dve.wait_ge(s["a_silu"], n + 1)
                if n >= NH:
                    dve.wait_ge(s["p_down"], n - NH + 1)
                V.tensor_tensor(hs[0:h, n % NH, :], sg[n % 2][0:h, :], ps[0:h, 2 + n % 2, :], ALU.mult
                                ).then_inc(s["d_h"], 1)

            for n in range(NH):
                for k in parts_of(K_UP, n, K_AD[-1]):
                    levels(k)
                hidden(n)
            for n in range(TB * NH):
                if n + NH < TB * NH:
                    hidden(n + NH)
            dve.wait_ge(s["a_fo"], TB)
            with dve.Fori(NB - NB // 8, NB, 4) as t:
                bs = [dve.value_load(order[0:1, bass.ds(t + i, 1)], min_val=0, max_val=NB - 1) for i in range(4)]
                for i, b in enumerate(bs):
                    dve.tensor_tensor(X[:, :, bass.ds(b * S, S)], X[:, :, bass.ds(b * S, S)],
                                      Up[:, :, bass.ds(t * S + i * S, S)], ALU.add).then_inc(s["d_x2"], 1)
            dve.wait_ge(s["g_x2"], NB - NB // 8)
            dve.wait_ge(s["d_x2"], NB // 8)
            for i in range(SENT):
                link(V.memset(repl[:, :, 2 + i:3 + i], -1e30 * (i + 1)))
                link(V.memset(vals[:, :, E + i:E + i + 1], -1e30 * (i + 1)))
            link(V.memset(rqT[:, :], 1.0))
            link(V.memset(qT[BOT:BOT + 1, :], 1.0))
            dve.wait_ge(s["p_prep"], 1)
            V.tensor_scalar(akT[0:BOT, :], akT[0:BOT, :], float(BOT ** -0.5), None, ALU.mult).then_inc(s["d_ak"], 1)

            def gates(tb):
                dve.wait_ge(s["p_lg"], tb + 1)
                tt(vals[:, :, 0:E], ps[:, 2, 0:NT * E].rearrange("p (t e) -> p t e", e=E),
                   lbias[:, tb * NT:(tb + 1) * NT, :], ALU.add)
                for t in range(NT):
                    link(V.max(top[:, t, :], vals[:, t, 0:E]))
                link(V.tensor_copy(repl[:, :, 0:2], top[:, :, 0:2]))
                V.tensor_tensor(ge, vals[:, :, 0:E], top[:, :, 0:1].to_broadcast([P, NT, E]), ALU.subtract
                                ).then_inc(s["d_gl"], 1)
                for t in range(NT):
                    link(V.match_replace(vrep[:, t, 0:E + SENT], repl[:, t, :], vals[:, t, 0:E + SENT], -3e38))
                ts(gs, vrep[:, :, 0:E], -2e38, None, ALU.is_lt, ALU.bypass)
                dve.wait_ge(s["a_ge"], tb + 1)
                tt(gs, gs, ge, ALU.mult)
                link(V.tensor_reduce(z4[:, 0, :], gs, AX.X, ALU.add))
                link(V.reciprocal(z4[:, 1, :], z4[:, 0, :]))
                ts(z4[:, 2, :], z4[:, 1, :], 2.0, None, ALU.mult, ALU.bypass)
                tt(gs, gs, z4[:, 2, :].unsqueeze(2).to_broadcast([P, NT, E]), ALU.mult)
                V.tensor_copy(gt.rearrange("p t (e r) -> p t e r", e=E), gs.unsqueeze(3).to_broadcast([P, NT, E, R])
                              ).then_inc(s["d_gate"], 1)

            gates(0)
            dve.wait_ge(s["l_l3w"], 32)
            V.tensor_copy(w16[:, :, 0:E], l3w[:, :, 0:E]).then_inc(s["d_w16"], 1)
            for tb in range(TB):
                dve.wait_ge(s["a_ha"], tb + 1)
                dve.wait_ge(s["p_gx"], tb + 1)
                if tb:
                    dve.wait_ge(s["p_c2"], tb)
                V.tensor_tensor(hgx, ha, ps[:, 2, :], ALU.mult).then_inc(s["d_hg"], 1)
                if tb + 1 < TB:
                    gates(tb + 1)
                for t in range(NT):
                    dve.wait_ge(s["p_tr"], tb * NT + t + 1)
                    V.bn_stats(bst[:, t, 0:6], ps[:, 3 - t % 2, :]).then_inc(s["d_st"], 1)
                dve.wait_ge(s["d_st"], tb * NT + NT)
                for t in range(NT):
                    link(V.bn_aggr(var[:, tb * NT + t, :], bst[:, t, 0:6]))
                if tb == TB - 1:
                    V.tensor_copy(lvs[:, 1:2], ones[:, 0:1]).then_inc(s["d_st"], 1)
                dve.wait_ge(s["p_sc"], tb + 1)
                if tb:
                    dve.wait_ge(s["a_pr"], NT * tb)
                for t in range(NT):
                    sl8 = ps[:, 6, t * NSLOT:(t + 1) * NSLOT]
                    link(V.max(top8[:, t, :], sl8))
                    link(V.match_replace(sc[:, t, :], top8[:, t, :], sl8, -3e38))
                ts(am, sc, -2e38, -1e30, ALU.is_gt, ALU.mult)
                tt(am, am, ps[:, 7, :].rearrange("p (t k) -> p t k", t=NT), ALU.add)
                V.tensor_reduce(nmx, am, AX.X, ALU.max, negate=True).then_inc(s["d_am"], 1)
                dve.wait_ge(s["d_am"], tb + 1)
            dve.wait_ge(s["d_st"], TT + 1)
            dve.wait_ge(s["p_lv"], 1)
            dve.wait_ge(s["a_sg"], 1)
            ts(lvs[:, 1:2], ps[:, 0, 0:1], 1.0 / TOK, 1e-6, ALU.mult, ALU.add)
            link(V.reciprocal(lvs[:, 1:2], lvs[:, 1:2]))
            ts(gq[:, 1, :], lv[:, :], lvs[:, 1:2], None, ALU.mult, ALU.bypass)
            ts(gq[:, 1, :], gq[:, 1, :], 0.5, None, ALU.mult, ALU.bypass)
            stt(gq[:, 1, :], gq[:, 0, :], 2.5, gq[:, 1, :], ALU.mult, ALU.add)
            ts(gq[:, 1, :], gq[:, 1, :], 0.0, 5.0, ALU.max, ALU.min)
            ts(gq[:, 1, :], gq[:, 1, :], 0.5, 1.0 / 1.5, ALU.subtract, ALU.mult)
            V.tensor_scalar(gq[:, 1, :], gq[:, 1, :], 0.0, 1.0, ALU.max, ALU.min).then_inc(s["d_un"], 1)
            dve.wait_ge(s["a_pr"], TT)
            link(V.reciprocal(gq[:, 3, :], den[:, :]))
            dve.wait_ge(s["a_gt"], 1)
            stt(gq[:, 4, :], gq[:, 2, :], 0.05, gq[:, 2, :], ALU.is_ge, ALU.mult)
            tt(gq[:, 4, :], gq[:, 4, :], gq[:, 3, :], ALU.mult)
            for tb in range(TB):
                tl = slice(tb * NT, (tb + 1) * NT)
                V.tensor_tensor(PR[:, tl, :], PR[:, tl, :], gq[:, 4, tl].unsqueeze(2).to_broadcast([P, NT, NSLOT]),
                                ALU.mult).then_inc(s["d_pn"], 1)
            dve.wait_ge(s["l_diag"], 16)
            link(V.memset(ysm[:, :, :], 0.0))

            def gate3(tb):
                dve.wait_ge(s["p_y"], tb + 1)
                dg = diag[:, tok(tb)]
                tt(yd, ps[0:NB, 2 + tb % 2, :], dg, ALU.mult)
                link(V.tensor_reduce(ysm[:, 0, 2:2 + S], yd.rearrange("p (b s) -> p s b", s=S), AX.X, ALU.add))
                link(V.tensor_scalar(ysm[:, 0, 2:2 + S], ysm[:, 0, 2:2 + S], ilen[:, 1:2], None, ALU.mult))
                link(V.tensor_scalar(ysm[:, 1, 0:S], ysm[:, 0, 0:S], cw[:, 0:1], None, ALU.mult))
                for k in range(1, 4):
                    stt(ysm[:, 1, 0:S], ysm[:, 0, k:k + S], cw[:, k:k + 1], ysm[:, 1, 0:S], ALU.mult, ALU.add)
                V.scalar_tensor_tensor(out=ysm[:, 1, 0:S], in0=ysm[:, 0, 4:4 + S], scalar=cw[:, 4:5], in1=ysm[:, 1, 0:S],
                                       op0=ALU.mult, op1=ALU.add).then_inc(s["d_ys"], 1)
                dve.wait_ge(s["a_yg"], tb + 1)
                V.tensor_tensor(gex[tb].rearrange("p (b s) -> p b s", s=S), dg.rearrange("p (b s) -> p b s", s=S),
                                ysm[:, 2:3, 0:S].to_broadcast([NB, TW // S, S]), ALU.mult).then_inc(s["d_gex"], 1)

            for tb in range(TB):
                dve.wait_ge(s["p_aux"], tb + 1)
                dve.wait_ge(s["g_xc"], tb + 1)
                V.tensor_tensor(X[:, :, tok(tb)], X[:, :, tok(tb)], ps[:, 4:8, :], ALU.add).then_inc(s["d_x3"], 1)
                if tb >= 2:
                    gate3(tb - 2)
            gate3(TB - 2)
            gate3(TB - 1)

            def gated(tb):
                dve.wait_ge(s["p_gb"], tb + 1)
                V.tensor_tensor(Y[:, :, tok(tb)], X[:, :, tok(tb)], ps[:, tb % 2, :].unsqueeze(1).to_broadcast([P, DC, TW]),
                                ALU.mult).then_inc(s["d_c3"], 1)

            gated(0)
            for tb in range(TB):
                if tb + 1 < TB:
                    gated(tb + 1)
                for oc in range(DC):
                    n = tb * DC + oc
                    dve.wait_ge(s["p_b"], n + 1)
                    V.scalar_tensor_tensor(out=X[:, oc, tok(tb)], in0=ps[:, 4 + oc, :], scalar=b3[:, oc:oc + 1],
                                           in1=X[:, oc, tok(tb)], op0=ALU.add, op1=ALU.add).then_inc(s["d_b"], 1)
                dve.wait_ge(s["p_sl"], tb + 1)
                src = ps[:, 3, 0:2 * ZW].rearrange("p (t k) -> p t k", t=2)
                link(V.tensor_copy(sl[:, 2 * tb:2 * tb + 2, E:2 * E], src[:, :, RANK + E:]))
                V.tensor_tensor(sl[:, 2 * tb:2 * tb + 2, 0:E], src[:, :, RANK:RANK + E],
                                b8[:, :].unsqueeze(1).to_broadcast([P, 2, E]), ALU.add).then_inc(s["d_sl"], 1)
            dve.wait_ge(s["d_sl"], TB)
            for k in range(2):
                v = sl[:, :, k * E:(k + 1) * E]
                link(V.tensor_reduce(mx4[:, k:k + 1], v, AX.XY, ALU.max))
                link(V.tensor_reduce(mx4[:, 2 + k:3 + k], v, AX.XY, ALU.min))
            V.tensor_copy(gm2, mx4).then_inc(s["d_mx"], 1)
            dve.wait_ge(s["g_mx"], 1)
            tt(gm2[:, 0:2], gm4[:, 0:2], gm4[:, 2:4], ALU.max)
            ts(gm2[:, 0:2], gm2[:, 0:2], 1e-6, None, ALU.max, ALU.bypass)
            link(V.reciprocal(gm2[:, 0:2], gm2[:, 0:2]))
            ts(gm2[:, 0:2], gm2[:, 0:2], 0.5, None, ALU.mult, ALU.bypass)
            link(V.tensor_scalar(lg3, sl[:, :, 0:E], gm2[:, 0:1], None, ALU.mult))
            stt(lg3, sl[:, :, E:2 * E], gm2[:, 1:2], lg3, ALU.mult, ALU.add)
            link(V.tensor_reduce(ss3[:, 0, :], lg3, AX.X, ALU.max))
            V.tensor_tensor(lg3, lg3, ss3[:, 0, :].unsqueeze(2).to_broadcast([P, 8, E]), ALU.subtract
                            ).then_inc(s["d_lg3"], 1)
            dve.wait_ge(s["a_e3"], 1)
            link(V.tensor_reduce(ss3[:, 1, :], pr3, AX.X, ALU.add))
            link(V.reciprocal(ss3[:, 2, :], ss3[:, 1, :]))
            tt(pr3, pr3, ss3[:, 2, :].unsqueeze(2).to_broadcast([P, 8, E]), ALU.mult)
            for t in range(8):
                link(V.max(tp3[:, t, :], pr3[:, t, :]))
            V.tensor_tensor(mk3, pr3, tp3[:, :, 1:2].to_broadcast([P, 8, E]), ALU.subtract).then_inc(s["d_th"], 1)
            dve.wait_ge(s["a_mk"], 1)
            tt(tm3, pr3, mk3, ALU.mult)
            link(V.tensor_reduce(ss3[:, 3, :], tm3, AX.X, ALU.add))
            ts(ss3[:, 3, :], ss3[:, 3, :], 1e-9, None, ALU.add, ALU.bypass)
            link(V.reciprocal(ss3[:, 4, :], ss3[:, 3, :]))
            V.tensor_tensor(tm3, tm3, ss3[:, 4, :].unsqueeze(2).to_broadcast([P, 8, E]), ALU.mult).then_inc(s["d_w3"], 1)
            dve.wait_ge(s["d_b"], TB * DC)

            def ranks(tb):
                dve.wait_ge(s["p_pm"], tb + 1)
                if tb >= 2:
                    dve.wait_ge(s["p_o"], (tb - 1) * DC)
                V.scalar_tensor_tensor(out=zp[tb % 2], in0=ps[0:RANK, tb % 2, :], scalar=0.5, in1=zt[0:RANK, tok(tb)],
                                       op0=ALU.mult, op1=ALU.mult).then_inc(s["d_zp"], 1)

            for tb in range(TB):
                ranks(tb)
                for oc in range(DC):
                    n = tb * DC + oc
                    dve.wait_ge(s["p_o"], n + 1)
                    V.tensor_tensor(X[:, oc, tok(tb)], ps[:, 4 + oc, :], X[:, oc, tok(tb)], ALU.add).then_inc(s["d_o"], 1)



def kernel(**inputs):
    import numpy as _np
    import concourse.bacc as _bacc
    from concourse import mybir as _mybir
    from concourse.bass_utils import run_bass_kernel_spmd as _run

    g = {k: _np.asarray(v) for k, v in inputs.items()}
    x = g["x"]
    const, diag = constants()
    lay = {
        "const": const, "diag": diag,
        "xconv": x.transpose(2, 1, 0).reshape(DC, P, S * NB)[:, ::-1],
        "xT": x.reshape(TOK, D).T,
        "log_A_real": g["L0_cond_log_A_real"].T, "A_imag": g["L0_cond_A_imag"].T,
        "C_re": g["L0_cond_C"][..., 0].T, "C_im": g["L0_cond_C"][..., 1].T,
        "log_dt": g["L0_cond_log_dt"], "Dskip": g["L0_cond_D"],
        "len0": g["itok_B_8_3872"], "len3": g["itok_B_9_3973"], "ids": g["itok_B_1_14"], "lang": g["itok_B_0_7"].reshape(TT, 4).T,
        "w0": g["L0_ffn_weight_fp8"].T, "w0scale": g["L0_ffn_weight_scale"],
        "wa": g["L1_cond_weight"].transpose(0, 2, 1),
        "w1": g["L1_ffn_w1"], "w2": g["L1_ffn_w2"], "w3": g["L1_ffn_w3"].reshape(D // 2, 2 * HID),
        "l2w": g["L2_cond_W"].T, "wr": g["L2_cond_Wr"].T, "l2a": g["L2_cond_A"].reshape(E * R, D).T,
        "l2b": g["L2_cond_B"].transpose(0, 2, 1).reshape(E * R, D),
        "wq": g["L2_ffn_Wq"].T, "wrq": g["L2_ffn_Wr"].T, "akT": g["L2_ffn_aux_keys"].T,
        "avT": g["L2_ffn_aux_values"].T, "wvd": g["L2_ffn_Wvd"].T, "wvu": g["L2_ffn_Wvu"].T,
        "wu1": g["L2_ffn_Wu1"].T, "bu1": g["L2_ffn_bu1"], "wu2": g["L2_ffn_Wu2"].T, "bu2": g["L2_ffn_bu2"],
        "gate_w1": g["L2_ffn_gate_w1"].reshape(1), "gate_bias": g["L2_ffn_gate_bias"].reshape(1),
        "log_rel": g["L2_ffn_log_rel"],
        "conv_w": g["L3_cond_conv_w"].reshape(5),
        "l3w": g["L3_ffn_W"].T, "b3": g["L3_ffn_b"].reshape(DC, P).T, "b3row": g["L3_ffn_b"],
        "l3a": g["L3_ffn_A"], "l3aT": g["L3_ffn_A"].T, "bmat": g["L3_ffn_Bmat"],
        "lim": g["L3_ffn_LiMEs"], "limT": g["L3_ffn_LiMEs"].T,
    }
    nc = _bacc.Bacc("TRN2", target_bir_lowering=False, num_devices=1)
    arrays, A = {}, {}
    for name, a in lay.items():
        a = _np.ascontiguousarray(a)
        arrays[f"in_{name}"] = a
        A[name] = nc.dram_tensor(f"in_{name}", a.shape, _mybir.dt.from_np(a.dtype), kind="ExternalInput").ap()
    out = nc.dram_tensor("out_T", (D, TOK), f32, kind="ExternalOutput").ap()
    build(nc, A, out)
    r = _run(nc, [arrays], core_ids=[0])
    return _np.ascontiguousarray(r.results[0]["out_T"].T).reshape(NB, S, D)
```
